# Optimizing a Trainium2 kernel written in Bass

```python
import numpy as np
import jax
import jax.numpy as jnp

def _softmax(x, axis=-1):
    return jax.nn.softmax(x, axis=axis)

def _gelu(x):
    return jax.nn.gelu(x, approximate=True)

def _silu(x):
    return jax.nn.silu(x)

def _sigmoid(x):
    return jax.nn.sigmoid(x)

def _layernorm(x, axis=-1, eps=1e-05):
    m = jnp.mean(x, axis=axis, keepdims=True)
    v = jnp.var(x, axis=axis, keepdims=True)
    return (x - m) / jnp.sqrt(v + eps)

def _scatter_add(tgt, idx, src, axis=0):
    return tgt.at[idx].add(src)

def _segment_sum(src, seg, n):
    return jax.ops.segment_sum(src, seg, n)
kernel_name = 'mk_audio_tower_d1_tok_audfeat512_r4_f575de'

def setup_inputs(seed: int=0):
    np.random.seed(seed)
    _w = jnp.asarray

    def _rec_inputs():
        import jax
        import jax.numpy as jnp
        _rk = jax.random.key(seed)
        x = -0.000124254 + 0.999853 * jax.random.normal(jax.random.fold_in(_rk, 1), (64, 256, 128), jnp.float32)
        return x
    x = _rec_inputs()

    def _L0_tok_setup():
        import jax, jax.numpy as jnp
        import numpy as np
        CONTEXT = 5
        DILATION = 1
        IN_DIM = 128
        OUT_DIM = 128
        EPS = 1e-05

        def _tdnn(x, W, b, gamma, beta):
            K = W.reshape(OUT_DIM, CONTEXT, IN_DIM).transpose(1, 2, 0)
            y = jax.lax.conv_general_dilated(x, K, window_strides=(1,), padding='VALID', rhs_dilation=(DILATION,), dimension_numbers=('NWC', 'WIO', 'NWC')) + b
            mean = jnp.mean(y, axis=(0, 1))
            var = jnp.mean(jnp.square(y - mean), axis=(0, 1))
            y = (y - mean) * (gamma * jax.lax.rsqrt(var + EPS)) + beta
            return jax.nn.relu(y)
        key = jax.random.key(seed)
        k1, k2, k3, k4, k5 = jax.random.split(key, 5)
        x = jax.random.normal(k1, (64, 250, IN_DIM), dtype=jnp.float32)
        fan_in = IN_DIM * CONTEXT
        bound = 1.0 / np.sqrt(fan_in)
        W = jax.random.uniform(k2, (OUT_DIM, fan_in), minval=-bound, maxval=bound, dtype=jnp.float32)
        b = jax.random.uniform(k3, (OUT_DIM,), minval=-bound, maxval=bound, dtype=jnp.float32)
        gamma = jnp.ones((OUT_DIM,), dtype=jnp.float32)
        beta = jnp.zeros((OUT_DIM,), dtype=jnp.float32)
        return {'x': x, 'W': W, 'b': b, 'gamma': gamma, 'beta': beta}
    _L0_tok_all = _L0_tok_setup()
    _L0_tok_in = {k: v for k, v in _L0_tok_all.items() if k in ('W', 'b', 'gamma', 'beta')}
    del _L0_tok_all

    def _L0_attn_setup():
        import jax, jax.numpy as jnp
        import numpy as np
        H_HEADS = 8
        HIDDEN = 128
        D_K = HIDDEN // H_HEADS

        def rel_shift(x):
            B, H, T, P = x.shape
            x = jnp.pad(x, ((0, 0), (0, 0), (0, 0), (1, 0)))
            x = x.reshape(B, H, P + 1, T)[:, :, 1:, :]
            return x.reshape(B, H, T, P)
        key = jax.random.key(seed)
        ks = jax.random.split(key, 16)
        B, T = (4, 256)
        P = 2 * T - 1
        s = 0.02
        inp = {'x': jax.random.normal(ks[0], (B, T, HIDDEN), dtype=jnp.float32), 'pos_emb': jax.random.normal(ks[1], (1, P, HIDDEN), dtype=jnp.float32), 'Wq': jax.random.normal(ks[2], (HIDDEN, HIDDEN), dtype=jnp.float32) * s, 'bq': jnp.zeros((HIDDEN,), dtype=jnp.float32), 'Wk': jax.random.normal(ks[3], (HIDDEN, HIDDEN), dtype=jnp.float32) * s, 'bk': jnp.zeros((HIDDEN,), dtype=jnp.float32), 'Wv': jax.random.normal(ks[4], (HIDDEN, HIDDEN), dtype=jnp.float32) * s, 'bv': jnp.zeros((HIDDEN,), dtype=jnp.float32), 'Wp': jax.random.normal(ks[5], (HIDDEN, HIDDEN), dtype=jnp.float32) * s, 'bp': jnp.zeros((HIDDEN,), dtype=jnp.float32), 'Wo': jax.random.normal(ks[6], (HIDDEN, HIDDEN), dtype=jnp.float32) * s, 'bo': jnp.zeros((HIDDEN,), dtype=jnp.float32), 'pos_bias_u': jax.random.normal(ks[7], (H_HEADS, D_K), dtype=jnp.float32) * s, 'pos_bias_v': jax.random.normal(ks[8], (H_HEADS, D_K), dtype=jnp.float32) * s}
        return inp
    _L0_attn_all = _L0_attn_setup()
    _L0_attn_in = {k: v for k, v in _L0_attn_all.items() if k in ('pos_emb', 'Wq', 'bq', 'Wk', 'bk', 'Wv', 'bv', 'Wp', 'bp', 'Wo', 'bo', 'pos_bias_u', 'pos_bias_v')}
    del _L0_attn_all

    def _L0_ffn_setup():
        import jax, jax.numpy as jnp
        import numpy as np
        MARK_AX, OP_ADD, OP_SUB = (0, 1, 2)
        ALU_LO, ALU_HI = (16, 32)
        AX_CARRY_LO, AX_CARRY_HI = (48, 64)
        OPCODE_BASE = 80
        OUTPUT_LO, OUTPUT_HI, CARRY = (128, 144, 160)
        NIB_A, NIB_B, OP_START = (0, 1, 10)
        RESULT, CARRY_OUT = (100, 101)
        GE_POS, GE_DIM = (8, 160)
        OPC_ADD, OPC_SUB = (25, 26)
        B, S, D = (8, 1024, 128)

        def _decode_nibble(x, base):
            return jnp.argmax(x[..., base:base + 16] > 0.5, axis=-1).astype(x.dtype)

        def _pipeline(h, W, b):
            for i in range(3):
                h = jnp.einsum('bspd,od->bspo', h, W[i]) + b[i]
                if i < 2:
                    h = jax.nn.relu(h)
            return h
        key = jax.random.key(seed)
        kx, k1, k2, k3, k4 = jax.random.split(key, 5)
        x_bd = jax.random.uniform(kx, (B, S, D), dtype=jnp.float32)
        Wa = jax.random.normal(k1, (3, GE_DIM, GE_DIM), dtype=jnp.float32) * 0.05
        ba = jax.random.normal(k2, (3, GE_DIM), dtype=jnp.float32) * 0.05
        Ws = jax.random.normal(k3, (3, GE_DIM, GE_DIM), dtype=jnp.float32) * 0.05
        bs = jax.random.normal(k4, (3, GE_DIM), dtype=jnp.float32) * 0.05
        return {'x_bd': x_bd, 'Wa': Wa, 'ba': ba, 'Ws': Ws, 'bs': bs}
    _L0_ffn_all = _L0_ffn_setup()
    _L0_ffn_in = {k: v for k, v in _L0_ffn_all.items() if k in ('Wa', 'ba', 'Ws', 'bs')}
    del _L0_ffn_all
    return {'x': x, 'L0_tok_W': _L0_tok_in['W'], 'L0_tok_b': _L0_tok_in['b'], 'L0_tok_gamma': _L0_tok_in['gamma'], 'L0_tok_beta': _L0_tok_in['beta'], 'L0_attn_pos_emb': _L0_attn_in['pos_emb'], 'L0_attn_Wq': _L0_attn_in['Wq'], 'L0_attn_bq': _L0_attn_in['bq'], 'L0_attn_Wk': _L0_attn_in['Wk'], 'L0_attn_bk': _L0_attn_in['bk'], 'L0_attn_Wv': _L0_attn_in['Wv'], 'L0_attn_bv': _L0_attn_in['bv'], 'L0_attn_Wp': _L0_attn_in['Wp'], 'L0_attn_bp': _L0_attn_in['bp'], 'L0_attn_Wo': _L0_attn_in['Wo'], 'L0_attn_bo': _L0_attn_in['bo'], 'L0_attn_pos_bias_u': _L0_attn_in['pos_bias_u'], 'L0_attn_pos_bias_v': _L0_attn_in['pos_bias_v'], 'L0_ffn_Wa': _L0_ffn_in['Wa'], 'L0_ffn_ba': _L0_ffn_in['ba'], 'L0_ffn_Ws': _L0_ffn_in['Ws'], 'L0_ffn_bs': _L0_ffn_in['bs']}

def reference(x, L0_tok_W, L0_tok_b, L0_tok_gamma, L0_tok_beta, L0_attn_pos_emb, L0_attn_Wq, L0_attn_bq, L0_attn_Wk, L0_attn_bk, L0_attn_Wv, L0_attn_bv, L0_attn_Wp, L0_attn_bp, L0_attn_Wo, L0_attn_bo, L0_attn_pos_bias_u, L0_attn_pos_bias_v, L0_ffn_Wa, L0_ffn_ba, L0_ffn_Ws, L0_ffn_bs):
    import jax
    import jax.numpy as jnp

    def _L0_tok_ref(x, W, b, gamma, beta):
        import jax, jax.numpy as jnp
        import numpy as np
        CONTEXT = 5
        DILATION = 1
        IN_DIM = 128
        OUT_DIM = 128
        EPS = 1e-05

        def _tdnn(x, W, b, gamma, beta):
            K = W.reshape(OUT_DIM, CONTEXT, IN_DIM).transpose(1, 2, 0)
            y = jax.lax.conv_general_dilated(x, K, window_strides=(1,), padding='VALID', rhs_dilation=(DILATION,), dimension_numbers=('NWC', 'WIO', 'NWC')) + b
            mean = jnp.mean(y, axis=(0, 1))
            var = jnp.mean(jnp.square(y - mean), axis=(0, 1))
            y = (y - mean) * (gamma * jax.lax.rsqrt(var + EPS)) + beta
            return jax.nn.relu(y)
        return _tdnn(x, W, b, gamma, beta)

    def _L0_attn_ref(x, pos_emb, Wq, bq, Wk, bk, Wv, bv, Wp, bp, Wo, bo, pos_bias_u, pos_bias_v):
        import jax, jax.numpy as jnp
        import numpy as np
        H_HEADS = 8
        HIDDEN = 128
        D_K = HIDDEN // H_HEADS

        def rel_shift(x):
            B, H, T, P = x.shape
            x = jnp.pad(x, ((0, 0), (0, 0), (0, 0), (1, 0)))
            x = x.reshape(B, H, P + 1, T)[:, :, 1:, :]
            return x.reshape(B, H, T, P)
        B, T, _ = x.shape
        Hh, d = (H_HEADS, D_K)
        scale = 1.0 / jnp.sqrt(jnp.asarray(d, dtype=x.dtype))
        q = (x @ Wq + bq).reshape(B, T, Hh, d)
        k = (x @ Wk + bk).reshape(B, T, Hh, d).transpose(0, 2, 1, 3)
        v = (x @ Wv + bv).reshape(B, T, Hh, d).transpose(0, 2, 1, 3)
        P = pos_emb.shape[1]
        p = (pos_emb @ Wp + bp).reshape(pos_emb.shape[0], P, Hh, d).transpose(0, 2, 1, 3)
        q_u = (q + pos_bias_u).transpose(0, 2, 1, 3)
        q_v = (q + pos_bias_v).transpose(0, 2, 1, 3)
        matrix_bd = jnp.matmul(q_v, p.transpose(0, 1, 3, 2))
        matrix_bd = rel_shift(matrix_bd)[:, :, :, :T] * scale
        scores = jnp.matmul(q_u, k.transpose(0, 1, 3, 2)) * scale + matrix_bd
        attn = jax.nn.softmax(scores.astype(jnp.float32), axis=-1).astype(x.dtype)
        out = jnp.matmul(attn, v)
        out = out.transpose(0, 2, 1, 3).reshape(B, T, Hh * d)
        return out @ Wo + bo

    def _L0_ffn_ref(x_bd, Wa, ba, Ws, bs):
        import jax, jax.numpy as jnp
        import numpy as np
        MARK_AX, OP_ADD, OP_SUB = (0, 1, 2)
        ALU_LO, ALU_HI = (16, 32)
        AX_CARRY_LO, AX_CARRY_HI = (48, 64)
        OPCODE_BASE = 80
        OUTPUT_LO, OUTPUT_HI, CARRY = (128, 144, 160)
        NIB_A, NIB_B, OP_START = (0, 1, 10)
        RESULT, CARRY_OUT = (100, 101)
        GE_POS, GE_DIM = (8, 160)
        OPC_ADD, OPC_SUB = (25, 26)
        B, S, D = (8, 1024, 128)

        def _decode_nibble(x, base):
            return jnp.argmax(x[..., base:base + 16] > 0.5, axis=-1).astype(x.dtype)

        def _pipeline(h, W, b):
            for i in range(3):
                h = jnp.einsum('bspd,od->bspo', h, W[i]) + b[i]
                if i < 2:
                    h = jax.nn.relu(h)
            return h
        x = x_bd
        Bsz, seq, _ = x.shape
        x_ge = jnp.zeros((Bsz, seq, GE_POS, GE_DIM), dtype=x.dtype)
        x_ge = x_ge.at[..., 0, NIB_A].set(_decode_nibble(x, ALU_LO))
        x_ge = x_ge.at[..., 1, NIB_A].set(_decode_nibble(x, ALU_HI))
        x_ge = x_ge.at[..., 0, NIB_B].set(_decode_nibble(x, AX_CARRY_LO))
        x_ge = x_ge.at[..., 1, NIB_B].set(_decode_nibble(x, AX_CARRY_HI))
        x_ge = x_ge.at[..., :, OP_START + OPC_ADD].set(x[..., OPCODE_BASE + OPC_ADD][..., None])
        x_ge = x_ge.at[..., :, OP_START + OPC_SUB].set(x[..., OPCODE_BASE + OPC_SUB][..., None])
        mark = x[..., MARK_AX] > 0.5
        m_add = mark & (x[..., OP_ADD] > 0.5)
        m_sub = mark & ~(x[..., OP_ADD] > 0.5) & (x[..., OP_SUB] > 0.5)
        active = (m_add | m_sub).astype(x.dtype)
        y_add = _pipeline(x_ge, Wa, ba)
        y_sub = _pipeline(x_ge, Ws, bs)
        y = jnp.where(m_add[..., None, None], y_add, jnp.where(m_sub[..., None, None], y_sub, x_ge))
        res_lo = jnp.clip(jnp.round(y[..., 0, RESULT]), 0, 15).astype(jnp.int32)
        res_hi = jnp.clip(jnp.round(y[..., 1, RESULT]), 0, 15).astype(jnp.int32)
        oh_lo = jax.nn.one_hot(res_lo, 16, dtype=x.dtype) * active[..., None]
        oh_hi = jax.nn.one_hot(res_hi, 16, dtype=x.dtype) * active[..., None]
        carry = (jnp.round(y[..., 1, CARRY_OUT]) > 0.5).astype(x.dtype) * active
        out = x
        out = out.at[..., OUTPUT_LO:OUTPUT_LO + 16].add(2.0 * oh_lo)
        out = out.at[..., OUTPUT_HI:OUTPUT_HI + 16].add(2.0 * oh_hi)
        out = out.at[..., CARRY].add(carry)
        return out
    h = _L0_tok_ref(x, L0_tok_W, L0_tok_b, L0_tok_gamma, L0_tok_beta)
    h = h + _L0_attn_ref(_layernorm(h, axis=-1), L0_attn_pos_emb, L0_attn_Wq, L0_attn_bq, L0_attn_Wk, L0_attn_bk, L0_attn_Wv, L0_attn_bv, L0_attn_Wp, L0_attn_bp, L0_attn_Wo, L0_attn_bo, L0_attn_pos_bias_u, L0_attn_pos_bias_v)
    h = h + _L0_ffn_ref(_layernorm(h, axis=-1), L0_ffn_Wa, L0_ffn_ba, L0_ffn_Ws, L0_ffn_bs)
    return h

_drawn_inputs = setup_inputs


def setup_inputs(seed=0):
    import zlib

    import numpy as np

    out = dict(_drawn_inputs(seed))
    spreads = {'L0_tok_gamma': (1.0, 0.2),
     'L0_tok_beta': (0.0, 0.1),
     'L0_attn_bq': (0.0, 0.8),
     'L0_attn_bk': (0.0, 2.0),
     'L0_attn_bv': (0.0, 0.1),
     'L0_attn_bp': (0.0, 2.0),
     'L0_attn_bo': (0.0, 0.1)}
    factors = {'L0_tok_b': 64.0,
     'L0_attn_pos_emb': 8.0,
     'L0_attn_Wq': 8.0,
     'L0_attn_Wk': 8.0,
     'L0_attn_Wv': 4.528,
     'L0_attn_Wp': 8.0,
     'L0_attn_pos_bias_u': 25.029,
     'L0_attn_pos_bias_v': 8.0}
    for name, (base, spread) in spreads.items():
        noise = np.random.default_rng([zlib.crc32(name.encode()), seed]).standard_normal(out[name].shape)
        drawn = base * np.exp(spread * noise) if base else spread * noise
        out[name] = jnp.asarray(drawn.astype(out[name].dtype))
    for name, factor in factors.items():
        out[name] = (out[name] * factor).astype(out[name].dtype)
    return out
```

```python
import concourse.bass as bass
from concourse import mybir
from concourse.alu_op_type import AluOpType as ALU
from contextlib import ExitStack

F32 = mybir.dt.float32
BF16 = mybir.dt.bfloat16
ACT = mybir.ActivationFunctionType
AX_X = mybir.AxisListType.X

PARTS = 128
QUERY_PART = (0, 0, 1, 1, 0, 2)
KEY_PART = (0, 1, 0, 1, 2, 0)
SLOTS = len(QUERY_PART)
EPS = 1e-5


def wait(engine, semaphore, value):
    if not (isinstance(value, int) and value <= 0):
        engine.wait_ge(semaphore, value)


def dram(ap, offset, pattern):
    return bass.AP(tensor=ap.tensor, offset=offset, ap=pattern)


class Shapes:
    def __init__(self, x, conv_w, pos_emb, pos_bias_u):
        self.B, self.S, self.D = x.shape
        self.CONTEXT = conv_w.shape[1] // self.D
        self.T = self.S - self.CONTEXT + 1
        self.P = pos_emb.shape[1]
        self.H, self.DK = pos_bias_u.shape
        self.TT = self.T // 2
        self.QT = self.T // 4
        self.J0 = PARTS
        self.J1 = self.T - PARTS
        self.PAIRS = self.B // 2
        self.ROW = self.B * self.T
        self.VW = self.DK + 1
        self.PW = 512
        assert self.D == PARTS and self.H * self.DK == self.D and self.T == 252 and self.B == 64


def build(nc, x, tok_w, tok_b, tok_gamma, tok_beta, pos_emb, wq, bq, wk, bk, wv, bv, wp, bp, wo, bo, bias_u, bias_v,
          out):
    s = Shapes(x, tok_w, pos_emb, bias_u)
    scratch = {
        "q": nc.dram_tensor("scratch_q", [SLOTS * PARTS, s.ROW], BF16, kind="Internal").ap(),
        "k": nc.dram_tensor("scratch_k", [SLOTS * PARTS, s.ROW], BF16, kind="Internal").ap(),
        "p": nc.dram_tensor("scratch_p", [SLOTS * PARTS, s.PW], BF16, kind="Internal").ap(),
        "c": nc.dram_tensor("scratch_c", [3, s.H * s.PW], BF16, kind="Internal").ap(),
        "v": nc.dram_tensor("scratch_v", [s.H * PARTS, s.B * 2 * s.VW], F32, kind="Internal").ap(),
        "h": nc.dram_tensor("scratch_h", [2 * s.TT, s.B * s.D], F32, kind="Internal").ap(),
        "o": nc.dram_tensor("scratch_o", [2 * s.TT, s.H * s.B * s.DK], F32, kind="Internal").ap(),
    }
    with ExitStack() as ctx:
        ident = ctx.enter_context(nc.sbuf_tensor("ident", [PARTS, PARTS], F32))
        ones = ctx.enter_context(nc.sbuf_tensor("ones", [PARTS, PARTS], F32))
        eps = ctx.enter_context(nc.sbuf_tensor("eps", [PARTS, 1], F32))
        zeros = ctx.enter_context(nc.sbuf_tensor("zeros", [PARTS, 1], F32))
        with ExitStack() as early:
            y = early.enter_context(nc.sbuf_tensor("y", [PARTS, s.ROW], F32))
            norm = early.enter_context(nc.sbuf_tensor("norm", [PARTS, 8], F32))
            conv_block(nc, s, x, tok_w, tok_b, tok_gamma, tok_beta, ident, ones, eps, zeros, y, norm)
            project_block(nc, s, pos_emb, wq, bq, wk, bk, wv, bv, wp, bp, bias_u, bias_v, ident, ones, eps, zeros, y, norm,
                          scratch)
        attend_block(nc, s, ident, scratch)
        finish_block(nc, s, wo, bo, ident, ones, eps, zeros, scratch, out)


def opener(nc, ctx):
    def sb(name, shape, dt=F32):
        return ctx.enter_context(nc.sbuf_tensor(name, shape, dt))

    def ps(name, shape=(PARTS, 512), dt=F32):
        return ctx.enter_context(nc.psum_tensor(name, list(shape), dt))

    def sem(name):
        return ctx.enter_context(nc.semaphore(name))

    return sb, ps, sem


def conv_block(nc, s, x, tok_w, tok_b, tok_gamma, tok_beta, ident, ones, eps, zeros, y, norm):
    U = 4
    STEPS = s.PAIRS // U
    NT = 2 * s.T
    with ExitStack() as ctx:
        sb, ps, sem = opener(nc, ctx)
        w_in = sb("w_in", [PARTS, s.CONTEXT * s.D])
        w_t = sb("w_t", [PARTS, s.CONTEXT, PARTS])
        vec = sb("vec", [PARTS, 4])
        x_in = sb("x_in", [PARTS, U, 4 * s.D])
        x_t = sb("x_t", [PARTS, 2, 2 * s.S])
        stats = sb("stats", [PARTS, s.PAIRS, 6])
        mv = sb("mv", [PARTS, 5])
        x_tp = [ps(f"x_tp{i}") for i in range(2)]
        y_p = [ps(f"y_p{i}") for i in range(2)]
        w_p = [ps(f"w_p{i}") for i in range(2)]
        const_set = sem("const_set")
        ident_ready = sem("ident_ready")
        w_loaded = sem("w_loaded")
        vec_loaded = sem("vec_loaded")
        x_loaded = [sem(f"x_loaded{u}") for u in range(U)]
        w_transposed = sem("w_transposed")
        w_copied = sem("w_copied")
        x_transposed = sem("x_transposed")
        x_copied = sem("x_copied")
        y_ready = sem("y_ready")
        y_copied = sem("y_copied")
        stats_done = sem("stats_done")
        moments_ready = sem("moments_ready")
        std_ready = sem("std_ready")
        norm_step = sem("norm_step")
        block = ctx.enter_context(nc.Block())

        @block.sync
        def _(sp):
            sp.dma_start(w_in[:, :], tok_w).then_inc(w_loaded, 16)
            for i, v in enumerate((tok_b, tok_gamma, tok_beta)):
                sp.dma_start(vec[:, i:i + 1], v.rearrange("(p a) -> p a", a=1)).then_inc(vec_loaded, 16)

            def step(k):
                for u in range(U):
                    n = U * k + u
                    wait(sp, x_transposed, n - U + 1)
                    sp.dma_start(x_in[:, u, :].rearrange("p (a c) -> p a c", a=4),
                                 dram(x, 2 * s.S * s.D * n, [[s.D, PARTS], [PARTS * s.D, 4], [1, s.D]]))\
                      .then_inc(x_loaded[u], 16)

            step(0)
            with sp.Fori(1, STEPS) as k:
                step(k)

        @block.gpsimd
        def _(pool):
            nc.gpsimd.memset(ident[:, :], 0.0).then_inc(const_set, 1)
            nc.gpsimd.memset(ones[:, :], 1.0).then_inc(const_set, 1)
            nc.gpsimd.memset(eps[:, :], EPS).then_inc(const_set, 1)
            nc.gpsimd.memset(zeros[:, :], 0.0).then_inc(const_set, 1)
            pool.wait_ge(const_set, 4)
            nc.gpsimd.affine_select(out=ident[:, :], in_=ident[:, :], compare_op=ALU.not_equal, fill=1.0, base=0,
                                    pattern=[[-1, PARTS]], channel_multiplier=1).then_inc(ident_ready, 1)

        @block.tensor
        def _(pe):
            pe.wait_ge(ident_ready, 1)
            pe.wait_ge(w_loaded, 16)
            for tap in range(s.CONTEXT):
                last = nc.tensor.matmul(w_p[tap // 4][:, PARTS * (tap % 4):PARTS * (tap % 4 + 1)],
                                        w_in[:, PARTS * tap:PARTS * (tap + 1)], ident[:, :], start=True, stop=True,
                                        is_transpose=True)
                if tap == 3 or tap == s.CONTEXT - 1:
                    last.then_inc(w_transposed, 1)

            def transpose_x(u, k):
                n = U * k + u
                pe.wait_ge(x_loaded[u], 16 * (k + 1))
                wait(pe, x_copied, n - 1)
                for a in range(4):
                    last = nc.tensor.matmul(x_tp[u % 2][:, PARTS * a:PARTS * (a + 1)],
                                            x_in[:, u, PARTS * a:PARTS * (a + 1)], ident[:, :], start=True,
                                            stop=True, is_transpose=True)
                last.then_inc(x_transposed, 1)

            def convolve(u, n):
                wait(pe, x_copied, n + 1)
                wait(pe, y_copied, n - 1)
                src = x_t[:, u % 2, :].rearrange("p (b c) -> p b c", b=2)
                for tap in range(s.CONTEXT):
                    last = nc.tensor.matmul(y_p[u % 2][:, 0:NT], w_t[:, tap, :], src[:, :, tap:tap + s.T],
                                            start=(tap == 0), stop=(tap == s.CONTEXT - 1))
                last.then_inc(y_ready, 1)

            def step(k):
                for u in range(U):
                    transpose_x(u, k)
                    if not (isinstance(k, int) and k == 0 and u == 0):
                        convolve((u - 1) % U, U * k + u - 1)

            pe.wait_ge(w_copied, 2)
            step(0)
            with pe.Fori(1, STEPS) as k:
                step(k)
            convolve(U - 1, s.PAIRS - 1)

        @block.scalar
        def _(act):
            act.wait_ge(w_transposed, 2)
            nc.scalar.activation(w_t[:, 0:4, :].rearrange("p a c -> p (a c)"), w_p[0][:, :], ACT.Copy)\
              .then_inc(w_copied, 1)
            nc.scalar.activation(w_t[:, 4, :], w_p[1][:, 0:PARTS], ACT.Copy).then_inc(w_copied, 1)
            act.wait_ge(vec_loaded, 48)

            def copy_x(u, n):
                act.wait_ge(x_transposed, n + 1)
                wait(act, y_ready, n - 1)
                nc.scalar.activation(x_t[:, u % 2, :], x_tp[u % 2][:, :], ACT.Copy).then_inc(x_copied, 1)

            def copy_y(u, n):
                act.wait_ge(y_ready, n + 1)
                nc.scalar.activation(y[:, bass.ds(NT * n, NT)], y_p[u % 2][:, 0:NT], ACT.Identity,
                                     bias=vec[:, 0:1]).then_inc(y_copied, 1)

            def step(k):
                for u in range(U):
                    copy_x(u, U * k + u)
                    if not (isinstance(k, int) and k == 0 and u == 0):
                        copy_y((u - 1) % U, U * k + u - 1)

            step(0)
            with act.Fori(1, STEPS) as k:
                step(k)
            copy_y(U - 1, s.PAIRS - 1)
            act.wait_ge(moments_ready, 1)
            act.wait_ge(const_set, 4)
            nc.scalar.activation(mv[:, 2:3], mv[:, 1:2], ACT.Sqrt, bias=eps[:, 0:1]).then_inc(std_ready, 1)

        @block.vector
        def _(dve):
            with dve.Fori(0, s.PAIRS) as n:
                dve.wait_ge(y_copied, n + 1)
                nc.vector.bn_stats(stats[:, bass.ds(n, 1), :].rearrange("p a b -> p (a b)"),
                                   y[:, bass.ds(NT * n, NT)]).then_inc(stats_done, 1)
            dve.wait_ge(stats_done, s.PAIRS)
            nc.vector.bn_aggr(mv[:, 0:2], stats[:, :, :].rearrange("p a b -> p (a b)")).then_inc(moments_ready, 1)
            dve.wait_ge(std_ready, 1)
            nc.vector.reciprocal(mv[:, 4:5], mv[:, 2:3]).then_inc(norm_step, 1)
            dve.wait_ge(norm_step, 1)
            dve.wait_ge(vec_loaded, 48)
            nc.vector.tensor_tensor(norm[:, 0:1], mv[:, 4:5], vec[:, 1:2], ALU.mult).then_inc(norm_step, 1)
            dve.wait_ge(norm_step, 2)
            nc.vector.tensor_tensor(mv[:, 3:4], mv[:, 0:1], norm[:, 0:1], ALU.mult).then_inc(norm_step, 1)
            dve.wait_ge(norm_step, 3)
            nc.vector.tensor_tensor(norm[:, 1:2], vec[:, 2:3], mv[:, 3:4], ALU.subtract)


def project_block(nc, s, pos_emb, wq, bq, wk, bk, wv, bv, wp, bp, bias_u, bias_v, ident, ones, eps, zeros, y, norm, scratch):
    U = 4
    STEPS = s.PAIRS // U
    NT = 2 * s.T
    GB = 4
    SCALE = float(s.DK) ** -0.5
    with ExitStack() as ctx:
        sb, ps, sem = opener(nc, ctx)
        w_qkvp = sb("w_qkvp", [PARTS, 4, s.D])
        vec = sb("vec2", [PARTS, 8])
        bv_row = sb("bv_row", [1, 4, s.D])
        pos_in = sb("pos_in", [PARTS, 4, s.D])
        pos_t = sb("pos_t", [PARTS, s.PW])
        pos_f = sb("pos_f", [PARTS, s.PW])
        pos_r = sb("pos_r", [PARTS, s.PW])
        pos_parts = sb("pos_parts", [PARTS, 3, s.PW], BF16)
        head_mask = sb("head_mask", [PARTS, s.H])
        vu_block = sb("vu_block", [PARTS, s.H])
        c_f = sb("c_f", [s.H, s.PW])
        c_parts = sb("c_parts", [s.H, 3, s.PW], BF16)
        h_t = sb("h_t", [PARTS, 2, NT])
        h_sb = sb("h_sb", [s.TT, U, 4, s.D])
        xn = sb("xn", [s.TT, 2, 4, s.D])
        xn_t = sb("xn_t", [PARTS, 2, NT])
        stats = sb("stats2", [s.TT, U, 4, 6])
        mv = sb("mv2", [s.TT, U, 4, 2])
        std = sb("std", [s.TT, U, 4])
        rstd = sb("rstd", [s.TT, U, 4])
        q_f = sb("q_f", [PARTS, 2, NT])
        k_f = sb("k_f", [PARTS, 2, NT])
        q_parts = sb("q_parts", [PARTS, 2, 3, 2, GB * s.TT], BF16)
        k_parts = sb("k_parts", [PARTS, 2, 3, GB * s.T], BF16)
        v_sb = sb("v_sb", [PARTS, 2, s.H, GB, 2, s.VW])
        h_p = [ps(f"h_p{i}") for i in range(2)]
        xn_p = [ps(f"xn_p{i}") for i in range(2)]
        q_p, k_p = ps("q_p"), ps("k_p")
        v_p = [ps(f"v_p{i}") for i in range(2)]
        w_loaded = sem("w_loaded2")
        pos_loaded = sem("pos_loaded")
        setup = sem("setup")
        pool_set = sem("pool_set")
        pos_transposed = sem("pos_transposed")
        pos_copied = sem("pos_copied")
        pos_projected = sem("pos_projected")
        pos_biased = sem("pos_biased")
        vu_ready = sem("vu_ready")
        c_ready = sem("c_ready")
        pos_cut = sem("pos_cut")
        tables_stored = sem("tables_stored")
        h_ready = sem("h_ready")
        h_turned = sem("h_turned")
        h_copied = sem("h_copied")
        h_stored = [sem(f"h_stored{u}") for u in range(U)]
        stats_done = sem("stats_done2")
        moments_ready = sem("moments_ready2")
        std_ready = sem("std_ready2")
        rstd_ready = sem("rstd_ready")
        xn_ready = sem("xn_ready")
        xn_turned = sem("xn_turned")
        xn_copied = sem("xn_copied")
        qk_projected = sem("qk_projected")
        v_projected = sem("v_projected")
        q_biased = sem("q_biased")
        k_biased = sem("k_biased")
        v_copied = sem("v_copied")
        q_step = sem("q_step")
        k_step = sem("k_step")
        qkv_stored = [sem(f"qkv_stored{i}") for i in range(2)]
        STORES = 2 * SLOTS + 1
        block = ctx.enter_context(nc.Block())

        @block.sync
        def _(sp):
            for i, w in enumerate((wq, wk, wv, wp)):
                sp.dma_start(w_qkvp[:, i, :], w).then_inc(w_loaded, 16)
            for i, v in enumerate((bq, bk, bp)):
                sp.dma_start(vec[:, i:i + 1], v.rearrange("(p a) -> p a", a=1)).then_inc(w_loaded, 16)
            for i, v in enumerate((bias_u, bias_v)):
                sp.dma_start(vec[:, 3 + i:4 + i], dram(v, 0, [[1, PARTS], [1, 1]])).then_inc(w_loaded, 16)
            sp.dma_start(bv_row[0:1, :, :], dram(bv, 0, [[s.D, 1], [0, 4], [1, s.D]])).then_inc(w_loaded, 16)
            for a in range(4):
                rows = min(PARTS, s.P - PARTS * a)
                sp.dma_start(pos_in[0:rows, a, :], pos_emb[0, PARTS * a:PARTS * a + rows, :]).then_inc(pos_loaded, 16)
            sp.wait_ge(pos_cut, 2)
            for slot in range(SLOTS):
                sp.dma_start(dram(scratch["p"], s.PW * slot, [[s.PW * SLOTS, PARTS], [1, s.PW]]),
                             pos_parts[:, KEY_PART[slot], :]).then_inc(tables_stored, 16)
            for part in range(3):
                sp.dma_start(dram(scratch["c"], s.H * s.PW * part, [[s.PW, s.H], [1, s.PW]]),
                             c_parts[:, part, :]).then_inc(tables_stored, 16)

            def store_h(u, k):
                n = U * k + u
                sp.wait_ge(h_copied, n + 1)
                sp.dma_start(dram(scratch["h"], 2 * s.D * n,
                                  [[s.B * s.D, s.TT], [s.TT * s.B * s.D, 2], [1, 2 * s.D]]),
                             h_sb[:, u, :, :].rearrange("p (a b) c -> p a (b c)", a=2)).then_inc(h_stored[u], 16)

            def store_group(i, k):
                n = U * k + 2 * i + 1
                b0 = GB * (2 * k + i)
                sp.wait_ge(q_step, 4 * (n + 1))
                for slot in range(SLOTS):
                    sp.dma_start(dram(scratch["q"], b0 * s.TT + s.ROW * slot,
                                      [[s.ROW * SLOTS, PARTS], [s.B * s.TT, 2], [1, GB * s.TT]]),
                                 q_parts[:, i, QUERY_PART[slot], :, :]).then_inc(qkv_stored[i], 16)
                sp.wait_ge(k_step, 4 * (n + 1))
                for slot in range(SLOTS):
                    sp.dma_start(dram(scratch["k"], b0 * s.T + s.ROW * slot,
                                      [[s.ROW * SLOTS, PARTS], [1, GB * s.T]]),
                                 k_parts[:, i, KEY_PART[slot], :]).then_inc(qkv_stored[i], 16)
                sp.wait_ge(v_copied, 2 * (n + 1))
                sp.dma_start(dram(scratch["v"], b0 * 2 * s.VW,
                                  [[s.B * 2 * s.VW, PARTS], [PARTS * s.B * 2 * s.VW, s.H], [1, GB * 2 * s.VW]]),
                             v_sb[:, i, :, :, :, :].rearrange("p h b j c -> p h (b j c)")).then_inc(qkv_stored[i], 16)

            with sp.Fori(0, STEPS) as k:
                for u in range(U):
                    store_h(u, k)
                    if u % 2:
                        store_group(u // 2, k)
            sp.wait_ge(tables_stored, 16 * (SLOTS + 3))
            for u in range(U):
                sp.wait_ge(h_stored[u], 16 * STEPS)
            for i in range(2):
                sp.wait_ge(qkv_stored[i], 16 * STORES * STEPS)

        @block.gpsimd
        def _(pool):
            nc.gpsimd.memset(head_mask[:, :], 1.0).then_inc(pool_set, 1)
            pool.wait_ge(pool_set, 1)
            nc.gpsimd.affine_select(out=head_mask[:, :], in_=head_mask[:, :], compare_op=ALU.is_ge, fill=0.0, base=0,
                                    pattern=[[-s.DK, s.H]], channel_multiplier=1).then_inc(pool_set, 1)
            pool.wait_ge(pool_set, 2)
            nc.gpsimd.affine_select(out=head_mask[:, :], in_=head_mask[:, :], compare_op=ALU.is_ge, fill=0.0,
                                    base=s.DK - 1, pattern=[[s.DK, s.H]], channel_multiplier=-1)\
              .then_inc(pool_set, 1)
            nc.gpsimd.memset(v_sb[:, :, :, :, :, :], 0.0).then_inc(pool_set, 1)
            pool.wait_ge(pool_set, 4)
            nc.gpsimd.memset(v_sb[:, :, :, :, :, s.DK:s.VW], 1.0).then_inc(pool_set, 1)
            pool.wait_ge(pool_set, 5)

            def cut_keys(u, k):
                n = U * k + u
                pool.wait_ge(k_biased, n + 1)
                if u % 2 == 0:
                    wait(pool, qkv_stored[u // 2], 16 * STORES * k)
                left, zero = k_f[:, u % 2, :], zeros[:, :].to_broadcast([PARTS, NT])
                part = [k_parts[:, u // 2, j, NT * (u % 2):NT * (u % 2 + 1)] for j in range(3)]
                nc.gpsimd.tensor_tensor(part[0], left, zero, ALU.add).then_inc(k_step, 1)
                pool.wait_ge(k_step, 4 * n + 1)
                nc.gpsimd.tensor_tensor(left, left, part[0], ALU.subtract).then_inc(k_step, 1)
                pool.wait_ge(k_step, 4 * n + 2)
                nc.gpsimd.tensor_tensor(part[1], left, zero, ALU.add).then_inc(k_step, 1)
                pool.wait_ge(k_step, 4 * n + 3)
                nc.gpsimd.tensor_tensor(part[2], left, part[1], ALU.subtract).then_inc(k_step, 1)

            for u in range(U):
                cut_keys(u, 0)
            with pool.Fori(1, STEPS) as k:
                for u in range(U):
                    cut_keys(u, k)

        @block.tensor
        def _(pe):
            pe.wait_ge(pos_loaded, 64)
            for a in range(4):
                rows = min(PARTS, s.P - PARTS * a)
                last = nc.tensor.matmul(h_p[0][:, PARTS * a:PARTS * a + rows], pos_in[0:rows, a, :],
                                        ident[0:rows, 0:rows], start=True, stop=True, is_transpose=True)
            last.then_inc(pos_transposed, 1)
            pe.wait_ge(w_loaded, 160)
            pe.wait_ge(pos_copied, 1)
            nc.tensor.matmul(q_p[:, 0:s.P], w_qkvp[:, 3, :], pos_t[:, 0:s.P], start=True, stop=True)\
              .then_inc(pos_projected, 1)
            pe.wait_ge(pos_biased, 1)
            pe.wait_ge(vu_ready, 1)
            nc.tensor.matmul(k_p[0:s.H, 0:s.P], vu_block[:, :], pos_f[:, 0:s.P], start=True, stop=True)\
              .then_inc(c_ready, 1)
            pe.wait_ge(pos_cut, 2)

            def turn_h(u, n):
                pe.wait_ge(h_ready, n + 1)
                wait(pe, h_copied, n - 1)
                src = h_t[:, u % 2, :].rearrange("p (b a t) -> p a b t", b=2, a=2)
                for a in range(2):
                    for b in range(2):
                        c = PARTS * (2 * a + b)
                        last = nc.tensor.matmul(h_p[u % 2][0:s.TT, c:c + PARTS], src[:, a, b, :], ident[:, :],
                                                start=True, stop=True, is_transpose=True)
                last.then_inc(h_turned, 1)

            def turn_xn(u, n):
                pe.wait_ge(xn_ready, n + 1)
                wait(pe, xn_copied, n - 1)
                for a in range(2):
                    for b in range(2):
                        c = s.T * b + s.TT * a
                        last = nc.tensor.matmul(xn_p[u % 2][:, c:c + s.TT], xn[:, u % 2, 2 * a + b, :],
                                                ident[0:s.TT, 0:s.TT], start=True, stop=True, is_transpose=True)
                last.then_inc(xn_turned, 1)

            def project(u, n):
                pe.wait_ge(xn_copied, n + 1)
                wait(pe, q_biased, n)
                wait(pe, k_biased, n)
                nc.tensor.matmul(q_p[:, 0:NT], w_qkvp[:, 0, :], xn_t[:, u % 2, :], start=True, stop=True)
                nc.tensor.matmul(k_p[:, 0:NT], w_qkvp[:, 1, :], xn_t[:, u % 2, :], start=True, stop=True)\
                  .then_inc(qk_projected, 1)
                wait(pe, v_copied, 2 * (n - 1))
                bank = v_p[u % 2]
                nc.tensor.matmul(bank[:, :], ones[0:1, :], bv_row[0:1, :, :].rearrange("p a c -> p (a c)"),
                                 start=True, stop=False, skip_group_check=True)
                for b in range(2):
                    for j, keys in enumerate((s.J0, s.J1)):
                        c = PARTS * (2 * b + j)
                        lhs = xn_t[:, u % 2, s.T * b + PARTS * j:s.T * b + PARTS * j + keys]
                        last = nc.tensor.matmul(bank[0:keys, c:c + PARTS], lhs, w_qkvp[:, 2, :], start=False,
                                                stop=True, skip_group_check=True)
                last.then_inc(v_projected, 1)

            def step(k):
                for u in range(U):
                    n = U * k + u
                    turn_h(u, n)
                    if not (isinstance(k, int) and n < 2):
                        turn_xn((u - 2) % U, n - 2)
                    if not (isinstance(k, int) and n < 3):
                        project((u - 3) % U, n - 3)

            step(0)
            with pe.Fori(1, STEPS) as k:
                step(k)
            turn_xn(U - 2, s.PAIRS - 2)
            project(U - 3, s.PAIRS - 3)
            turn_xn(U - 1, s.PAIRS - 1)
            project(U - 2, s.PAIRS - 2)
            project(U - 1, s.PAIRS - 1)

        @block.scalar
        def _(act):
            act.wait_ge(pos_transposed, 1)
            nc.scalar.activation(pos_t[:, 0:s.P], h_p[0][:, 0:s.P], ACT.Copy).then_inc(pos_copied, 1)
            act.wait_ge(pos_projected, 1)
            act.wait_ge(setup, 3)
            nc.scalar.activation(pos_f[:, 0:s.P], q_p[:, 0:s.P], ACT.Identity, bias=vec[:, 2:3])\
              .then_inc(pos_biased, 1)

            def make_h(u, n):
                wait(act, h_turned, n - 1)
                nc.scalar.activation(h_t[:, u % 2, :], y[:, bass.ds(NT * n, NT)], ACT.Relu, bias=norm[:, 1:2],
                                     scale=norm[:, 0:1]).then_inc(h_ready, 1)

            def copy_h(u, k):
                n = U * k + u
                act.wait_ge(h_turned, n + 1)
                wait(act, h_stored[u], 16 * k)
                wait(act, xn_ready, n - U + 1)
                nc.scalar.activation(h_sb[:, u, :, :].rearrange("p a c -> p (a c)"), h_p[u % 2][0:s.TT, :], ACT.Copy)\
                  .then_inc(h_copied, 1)

            def deviation(u, n):
                act.wait_ge(moments_ready, n + 1)
                nc.scalar.activation(std[:, u, :], mv[:, u, :, 1], ACT.Sqrt, bias=eps[0:s.TT, 0:1])\
                  .then_inc(std_ready, 1)

            def copy_xn(u, n):
                act.wait_ge(xn_turned, n + 1)
                wait(act, v_projected, n - 1)
                nc.scalar.activation(xn_t[:, u % 2, :], xn_p[u % 2][:, 0:NT], ACT.Copy).then_inc(xn_copied, 1)

            def copy_qkv(u, k):
                n = U * k + u
                act.wait_ge(qk_projected, n + 1)
                wait(act, q_step, 4 * (n - 1))
                nc.scalar.activation(q_f[:, u % 2, :], q_p[:, 0:NT], ACT.Identity, bias=vec[:, 5:6], scale=SCALE)\
                  .then_inc(q_biased, 1)
                wait(act, k_step, 4 * (n - 1))
                nc.scalar.activation(k_f[:, u % 2, :], k_p[:, 0:NT], ACT.Identity, bias=vec[:, 1:2])\
                  .then_inc(k_biased, 1)
                act.wait_ge(v_projected, n + 1)
                if u % 2 == 0:
                    wait(act, qkv_stored[u // 2], 16 * STORES * k)
                    if isinstance(k, int) and k == 0:
                        act.wait_ge(pool_set, 5)
                src = v_p[u % 2][:, :].rearrange("p (b j h d) -> p j h b d", b=2, j=2, h=s.H)
                dst = v_sb[:, u // 2, :, 2 * (u % 2):2 * (u % 2) + 2, :, 0:s.DK]
                for j, keys in enumerate((s.J0, s.J1)):
                    nc.scalar.activation(dst[0:keys, :, :, j, :], src[0:keys, j, :, :, :], ACT.Copy)\
                      .then_inc(v_copied, 1)

            def step(k, last=False):
                for u in range(U):
                    n = U * k + u
                    if not (last and u == U - 1):
                        make_h((u + 1) % U, n + 1)
                    copy_h(u, k)
                    if not (isinstance(k, int) and n < 1):
                        deviation((u - 1) % U, n - 1)
                    if not (isinstance(k, int) and n < 2):
                        copy_xn((u - 2) % U, n - 2)
                    if not (isinstance(k, int) and n < 3):
                        copy_qkv((u - 3) % U, k if u >= 3 else k - 1)

            act.wait_ge(setup, 3)
            act.wait_ge(pos_cut, 2)
            make_h(0, 0)
            step(0)
            with act.Fori(1, STEPS - 1) as k:
                step(k)
            step(STEPS - 1, last=True)
            deviation(U - 1, s.PAIRS - 1)
            copy_xn(U - 2, s.PAIRS - 2)
            copy_qkv(U - 3, STEPS - 1)
            copy_xn(U - 1, s.PAIRS - 1)
            copy_qkv(U - 2, STEPS - 1)
            copy_qkv(U - 1, STEPS - 1)

        @block.vector
        def _(dve):
            dve.wait_ge(w_loaded, 160)
            nc.vector.tensor_scalar(vec[:, 5:6], vec[:, 0:1], vec[:, 3:4], SCALE, ALU.add, ALU.mult).then_inc(setup, 1)
            nc.vector.tensor_scalar(vec[:, 6:7], vec[:, 4:5], vec[:, 3:4], SCALE, ALU.subtract, ALU.mult)\
              .then_inc(setup, 1)
            nc.vector.memset(pos_f[:, s.P:s.PW], 0.0).then_inc(setup, 1)
            dve.wait_ge(setup, 3)
            dve.wait_ge(pool_set, 3)
            nc.vector.tensor_scalar(vu_block[:, :], head_mask[:, :], vec[:, 6:7], None, ALU.mult).then_inc(vu_ready, 1)
            nc.vector.memset(c_f[:, s.P:s.PW], 0.0).then_inc(setup, 1)
            dve.wait_ge(c_ready, 1)
            nc.vector.tensor_copy(c_f[:, 0:s.P], k_p[0:s.H, 0:s.P]).then_inc(setup, 1)
            dve.wait_ge(setup, 5)
            done = 5
            for full, left, part in ((c_f, c_f, c_parts), (pos_f, pos_r, pos_parts)):
                nc.vector.tensor_copy(part[:, 0, :], full[:, :]).then_inc(setup, 1)
                dve.wait_ge(setup, done + 1)
                nc.vector.tensor_tensor(left[:, :], full[:, :], part[:, 0, :], ALU.subtract).then_inc(setup, 1)
                dve.wait_ge(setup, done + 2)
                nc.vector.tensor_copy(part[:, 1, :], left[:, :]).then_inc(setup, 1)
                dve.wait_ge(setup, done + 3)
                nc.vector.tensor_tensor(part[:, 2, :], left[:, :], part[:, 1, :], ALU.subtract).then_inc(pos_cut, 1)
                done += 3

            def stats_of(u, n):
                dve.wait_ge(h_copied, n + 1)
                for a in range(4):
                    last = nc.vector.bn_stats(stats[:, u, a, :], h_sb[:, u, a, :])
                last.then_inc(stats_done, 1)

            def invert(u, n):
                dve.wait_ge(std_ready, n + 1)
                nc.vector.reciprocal(rstd[:, u, :], std[:, u, :]).then_inc(rstd_ready, 1)

            def moments(u):
                for a in range(4):
                    last = nc.vector.bn_aggr(mv[:, u, a, :], stats[:, u, a, :])
                last.then_inc(moments_ready, 1)

            def normalise(u, n):
                dve.wait_ge(rstd_ready, n + 1)
                wait(dve, xn_turned, n - 1)
                for a in range(4):
                    last = nc.vector.tensor_scalar(xn[:, u % 2, a, :], h_sb[:, u, a, :], mv[:, u, a, 0:1],
                                                   rstd[:, u, a:a + 1], ALU.subtract, ALU.mult)
                last.then_inc(xn_ready, 1)

            def cut_queries(u, k):
                n = U * k + u
                dve.wait_ge(q_biased, n + 1)
                if u % 2 == 0:
                    wait(dve, qkv_stored[u // 2], 16 * STORES * k)
                left = q_f[:, u % 2, :].rearrange("p (b a t) -> p b a t", b=2, a=2)
                part = [q_parts[:, u // 2, j, :, :].rearrange("p a (b t) -> p b a t", b=GB)
                        [:, 2 * (u % 2):2 * (u % 2) + 2, :, :] for j in range(3)]
                nc.vector.tensor_copy(part[0], left).then_inc(q_step, 1)
                dve.wait_ge(q_step, 4 * n + 1)
                nc.vector.tensor_tensor(left, left, part[0], ALU.subtract).then_inc(q_step, 1)
                dve.wait_ge(q_step, 4 * n + 2)
                nc.vector.tensor_copy(part[1], left).then_inc(q_step, 1)
                dve.wait_ge(q_step, 4 * n + 3)
                nc.vector.tensor_tensor(part[2], left, part[1], ALU.subtract).then_inc(q_step, 1)

            def step(k):
                for u in range(U):
                    n = U * k + u
                    stats_of(u, n)
                    dve.wait_ge(stats_done, n + 1)
                    if isinstance(k, int) and n < 1:
                        moments(u)
                    else:
                        invert((u - 1) % U, n - 1)
                        moments(u)
                        normalise((u - 1) % U, n - 1)
                    if not (isinstance(k, int) and n < 4):
                        cut_queries(u, k - 1)

            step(0)
            with dve.Fori(1, STEPS) as k:
                step(k)
            invert(U - 1, s.PAIRS - 1)
            normalise(U - 1, s.PAIRS - 1)
            for u in range(U):
                cut_queries(u, STEPS - 1)


def attend_block(nc, s, ident, scratch):
    UNITS = 2 * s.H
    ITERS = 4
    G = UNITS * ITERS
    IB = s.B // ITERS
    NP = IB // 2
    HALF = IB // 2
    CT = 7
    CHUNKS = s.QT // CT
    CN = CT * s.B
    UROW = s.B * s.T
    STACK = SLOTS * s.DK
    CROWS = STACK + 3
    EW = 256
    BESIDE = ((0, 1), (2,), (3, 4), (5,), (6, 7), (8,), (), ())
    assert CHUNKS == 9 and NP == len(BESIDE)
    with ExitStack() as ctx:
        sb, ps, sem = opener(nc, ctx)
        pos = sb("pos", [CROWS, s.H, s.PW], BF16)
        q_all = sb("q_all", [CROWS, 2 * s.B * s.TT], BF16)
        bd_t = sb("bd_t", [PARTS, 2 * UROW])
        bd_in = sb("bd_in", [PARTS, 2, HALF, 2, s.TT])
        q_in = sb("q_in", [STACK, 2, HALF, s.TT], BF16)
        k_in = sb("k_in", [STACK, 2, HALF, s.T], BF16)
        v_in = sb("v_in", [PARTS, 2, HALF, 2, s.VW])
        neg_max = sb("neg_max", [s.TT, 4, 2])
        e_sb = sb("e_sb", [s.TT, 2, 2, EW])
        e_t = sb("e_t", [PARTS, 2, 2 * s.T])
        recip = sb("recip", [s.TT, IB])
        o_sb = sb("o_sb", [s.TT, IB, s.DK])
        bd_p = [ps(f"bd_p{i}") for i in range(3)]
        s_p = [ps(f"s_p{i}") for i in range(2)]
        e_p = [ps(f"e_p{i}") for i in range(2)]
        o_p = ps("o_p")
        const_set = sem("const_set3")
        tables_loaded = sem("tables_loaded")
        q_all_loaded = sem("q_all_loaded")
        bd_ready = sem("bd_ready")
        bd_copied = sem("bd_copied")
        in_loaded = [sem(f"in_loaded{i}") for i in range(2)]
        v_loaded = [sem(f"v_loaded{i}") for i in range(2)]
        s_ready = sem("s_ready")
        max_ready = sem("max_ready")
        exp_done = sem("exp_done")
        e_turned = sem("e_turned")
        e_copied = sem("e_copied")
        o_ready = sem("o_ready")
        recip_done = sem("recip_done")
        o_copied = sem("o_copied")
        o_stored = sem("o_stored")
        block = ctx.enter_context(nc.Block())

        @block.sync
        def _(sp):
            sp.dma_start(pos[0:STACK, :, :], dram(scratch["p"], 0, [[s.PW, STACK], [STACK * s.PW, s.H], [1, s.PW]]))\
              .then_inc(tables_loaded, 16)
            sp.dma_start(pos[STACK:CROWS, :, :].rearrange("p h c -> p (h c)"), scratch["c"])\
              .then_inc(tables_loaded, 16)

            PART = s.B // ITERS * s.TT

            def load_queries(unit, part, before):
                wait(sp, q_all_loaded, 16 * before)
                sp.dma_start(q_all[0:STACK, bass.ds((unit % 2) * s.B * s.TT + part * PART, PART)],
                             dram(scratch["q"],
                                  (unit // 2) * STACK * s.ROW + (unit % 2) * s.B * s.TT + part * PART,
                                  [[s.ROW, STACK], [1, PART]])).then_inc(q_all_loaded, 16)

            def load_next_queries(i):
                wait(sp, bd_ready, CHUNKS * ITERS * (i // ITERS))
                load_queries(i // ITERS + 1, i % ITERS, i + ITERS)

            def load_half(g, half):
                unit, head = g // ITERS, g // (2 * ITERS)
                b0 = (g % ITERS) * IB + half * HALF
                wait(sp, s_ready, NP * (g - 1) + NP // 2 * (half + 1))
                sp.wait_ge(bd_copied, CHUNKS * ITERS * (unit + 1))
                sp.dma_start(bd_in[:, half, :, :, :].rearrange("p b j t -> p (b j t)"),
                             bd_t[:, bass.ds((unit % 2) * UROW + b0 * s.T, HALF * s.T)]).then_inc(in_loaded[half], 16)
                sp.dma_start(q_in[:, half, :, :].rearrange("p b t -> p (b t)"),
                             dram(scratch["q"], head * STACK * s.ROW + (unit % 2) * s.B * s.TT + b0 * s.TT,
                                  [[s.ROW, STACK], [1, HALF * s.TT]]))\
                  .then_inc(in_loaded[half], 16)
                sp.dma_start(k_in[:, half, :, :].rearrange("p b t -> p (b t)"),
                             dram(scratch["k"], head * STACK * s.ROW + b0 * s.T, [[s.ROW, STACK], [1, HALF * s.T]]))\
                  .then_inc(in_loaded[half], 16)

            def load_values(g, half):
                head = g // (2 * ITERS)
                b0 = (g % ITERS) * IB + half * HALF
                wait(sp, o_ready, NP * (g - 1) + NP // 2 * (half + 1))
                sp.dma_start(v_in[:, half, :, :, :].rearrange("p b j c -> p (b j c)"),
                             dram(scratch["v"], head * PARTS * s.B * 2 * s.VW + b0 * 2 * s.VW,
                                  [[s.B * 2 * s.VW, PARTS], [1, HALF * 2 * s.VW]])).then_inc(v_loaded[half], 16)

            def store_o(g):
                unit = g // ITERS
                sp.wait_ge(o_copied, g + 1)
                sp.dma_start(dram(scratch["o"],
                                  (unit % 2) * s.TT * s.H * s.B * s.DK + (unit // 2) * s.B * s.DK
                                  + (g % ITERS) * IB * s.DK,
                                  [[s.H * s.B * s.DK, s.TT], [1, IB * s.DK]]),
                             o_sb[:, :, :].rearrange("p b c -> p (b c)")).then_inc(o_stored, 16)

            for i in range(ITERS):
                load_queries(0, i, i)
            for i in range(ITERS):
                load_next_queries(i)
            load_half(0, 0)
            load_values(0, 0)
            load_half(0, 1)
            load_values(0, 1)

            def step(g, queries, first=False):
                if queries:
                    load_next_queries(g + ITERS)
                if not first:
                    store_o(g - 1)
                load_half(g + 1, 0)
                load_values(g + 1, 0)
                load_half(g + 1, 1)
                load_values(g + 1, 1)

            LAST = G - 2 * ITERS
            step(0, True, first=True)
            with sp.Fori(1, LAST) as g:
                step(g, True)
            with sp.Fori(LAST, G - 1) as g:
                step(g, False)
            store_o(G - 2)
            store_o(G - 1)
            sp.wait_ge(o_stored, 16 * G)

        @block.gpsimd
        def _(pool):
            nc.gpsimd.memset(q_all[STACK:CROWS, :], 1.0).then_inc(const_set, 1)
            pool.wait_ge(const_set, 1)
            nc.gpsimd.memset(e_sb[:, :, :, s.T:EW], 0.0).then_inc(const_set, 1)

        @block.tensor
        def _(pe):
            pe.wait_ge(const_set, 2)
            pe.wait_ge(tables_loaded, 32)
            pos_flat = pos[:, :, :].rearrange("p h c -> p (h c)")

            def position_chunk(i, c):
                head, quarter, tile = i // 8, (i // 2) % 4, i % 2
                if c == 0:
                    pe.wait_ge(q_all_loaded, 16 * ITERS * (i // ITERS + 1))
                wait(pe, bd_copied, CHUNKS * i + c - 2)
                window = pe.snap(head * s.PW + PARTS * tile + s.T - 1 - s.QT * quarter - CT * c - (CT - 1))
                column = pe.snap(((i // ITERS) % 2) * s.B * s.TT + ((i // 2) % 2) * s.QT + CT * c)
                for t in range(CT):
                    last = nc.tensor.matmul(
                        bd_p[c % 3][:, s.B * t:s.B * (t + 1)],
                        pos_flat[:, bass.ds(window + (CT - 1 - t), PARTS)],
                        bass.AP(tensor=q_all[:, :].tensor, offset=column + t,
                                ap=[[2 * s.B * s.TT, CROWS], [s.TT, s.B]]),
                        start=True, stop=True)
                last.then_inc(bd_ready, 1)

            def scores(g, p):
                half = p // (NP // 2)
                if p % (NP // 2) == 0:
                    pe.wait_ge(in_loaded[half], 48 * (g + 1))
                wait(pe, exp_done, 2 * (NP * g + p - 1))
                for i in range(2):
                    b = (2 * p + i) % HALF
                    bank, c = s_p[p % 2], s.T * i
                    nc.tensor.matmul(bank[0:s.TT, c:c + s.J0], bd_in[:, half, b, 0, :], ident[:, :], start=(i == 0),
                                     stop=False, is_transpose=True, skip_group_check=True)
                    nc.tensor.matmul(bank[0:s.TT, c + s.J0:c + s.T], bd_in[0:s.J1, half, b, 1, :],
                                     ident[0:s.J1, 0:s.J1], start=False, stop=False, is_transpose=True,
                                     skip_group_check=True)
                    last = nc.tensor.matmul(bank[0:s.TT, c:c + s.T], q_in[:, half, b, :], k_in[:, half, b, :],
                                            start=False, stop=True, skip_group_check=True)
                last.then_inc(s_ready, 1)

            def turn_weights(n, p):
                pe.wait_ge(exp_done, 2 * (n + 1))
                wait(pe, e_copied, n - 1)
                for i in range(2):
                    for j in range(2):
                        c = s.T * i + s.TT * j
                        last = nc.tensor.matmul(e_p[p % 2][:, c:c + s.TT], e_sb[:, p % 2, i, PARTS * j:PARTS * (j + 1)],
                                                ident[0:s.TT, 0:s.TT], start=True, stop=True, is_transpose=True)
                last.then_inc(e_turned, 1)

            def values(n, g, p):
                half = p // (NP // 2)
                if p % (NP // 2) == 0:
                    pe.wait_ge(v_loaded[half], 16 * (g + 1))
                if p == 0:
                    wait(pe, o_copied, g)
                pe.wait_ge(e_copied, n + 1)
                for i in range(2):
                    b = 2 * p + i
                    for j in range(2):
                        c = s.T * i + s.TT * j
                        last = nc.tensor.matmul(o_p[0:s.TT, s.VW * b:s.VW * (b + 1)], e_t[:, p % 2, c:c + s.TT],
                                                v_in[:, half, b % HALF, j, :], start=(j == 0), stop=(j == 1))
                last.then_inc(o_ready, 1)

            def step(g, positions, first=False):
                for p in range(NP):
                    scores(g, p)
                    if positions:
                        for c in BESIDE[p]:
                            position_chunk(g + ITERS, c)
                    if not (first and p < 1):
                        turn_weights(NP * g + p - 1, (p - 1) % NP)
                    if not (first and p < 2):
                        values(NP * g + p - 2, g if p >= 2 else g - 1, (p - 2) % NP)

            for c in range(CHUNKS):
                position_chunk(0, c)
            with pe.Fori(1, ITERS) as i:
                for c in range(CHUNKS):
                    position_chunk(i, c)
            step(0, True, first=True)
            with pe.Fori(1, G - ITERS) as g:
                step(g, True)
            with pe.Fori(G - ITERS, G) as g:
                step(g, False)
            turn_weights(NP * G - 1, NP - 1)
            values(NP * G - 2, G - 1, NP - 2)
            values(NP * G - 1, G - 1, NP - 1)

        @block.scalar
        def _(act):
            def copy_chunk(i, c, g=0):
                unit, part, tile = i // 4, (i // 2) % 2, i % 2
                if c == 0:
                    for half in range(2):
                        wait(act, in_loaded[half], 48 * ITERS * (g // ITERS))
                act.wait_ge(bd_ready, CHUNKS * i + c + 1)
                first = act.snap((unit % 2) * UROW + tile * s.TT + part * s.QT + CT * c)
                dst = bass.AP(tensor=bd_t[:, :].tensor, offset=first,
                              ap=[[2 * UROW, PARTS], [1, CT], [s.T, s.B]])
                nc.scalar.activation(dst, bd_p[c % 3][:, 0:CN].rearrange("p (t b) -> p t b", t=CT), ACT.Copy)\
                  .then_inc(bd_copied, 1)

            def exps(n, p):
                act.wait_ge(max_ready, n + 1)
                wait(act, e_turned, n - 1)
                for i in range(2):
                    nc.scalar.activation(e_sb[:, p % 2, i, 0:s.T], s_p[p % 2][0:s.TT, s.T * i:s.T * (i + 1)], ACT.Exp,
                                         bias=neg_max[:, p % 4, i:i + 1]).then_inc(exp_done, 1)

            def step(g, positions):
                for p in range(NP):
                    exps(NP * g + p, p)
                    if positions:
                        for c in BESIDE[p]:
                            copy_chunk(g + ITERS, c, g)

            for i in range(ITERS):
                for c in range(CHUNKS):
                    copy_chunk(i, c)
            step(0, True)
            with act.Fori(1, G - ITERS) as g:
                step(g, True)
            with act.Fori(G - ITERS, G) as g:
                step(g, False)

        @block.vector
        def _(dve):
            def maxima(n, p):
                dve.wait_ge(s_ready, n + 1)
                nc.vector.tensor_reduce(neg_max[:, p % 4, :],
                                        s_p[p % 2][0:s.TT, 0:2 * s.T].rearrange("p (b t) -> p b t", b=2), AX_X,
                                        ALU.max, negate=True).then_inc(max_ready, 1)

            def copy_weights(n, p):
                dve.wait_ge(e_turned, n + 1)
                wait(dve, o_ready, n - 1)
                nc.vector.tensor_copy(e_t[:, p % 2, :], e_p[p % 2][:, 0:2 * s.T]).then_inc(e_copied, 1)

            def normalise(g):
                dve.wait_ge(o_ready, NP * (g + 1))
                o = o_p[0:s.TT, 0:IB * s.VW].rearrange("p (b c) -> p b c", b=IB)
                nc.vector.reciprocal(recip[:, :], o[:, :, s.DK]).then_inc(recip_done, 1)
                dve.wait_ge(recip_done, g + 1)
                wait(dve, o_stored, 16 * g)
                nc.vector.tensor_tensor(o_sb[:, :, :], o[:, :, 0:s.DK],
                                        recip[:, :].unsqueeze(2).to_broadcast([s.TT, IB, s.DK]), ALU.mult)\
                  .then_inc(o_copied, 1)

            def step(g, first=False):
                for p in range(NP):
                    maxima(NP * g + p, p)
                    if not (first and p < 1):
                        copy_weights(NP * g + p - 1, (p - 1) % NP)
                    if p == 1 and not first:
                        normalise(g - 1)

            step(0, first=True)
            with dve.Fori(1, G) as g:
                step(g)
            copy_weights(NP * G - 1, NP - 1)
            normalise(G - 1)


def finish_block(nc, s, wo, bo, ident, ones, eps, zeros, scratch, out):
    U = 4
    GB = 4
    N = 2 * s.B // GB
    STEPS = N // U
    PER = s.B // GB
    NT = GB * s.TT
    with ExitStack() as ctx:
        sb, ps, sem = opener(nc, ctx)
        wo_sb = sb("wo_sb", [PARTS, s.D])
        bo_row = sb("bo_row", [1, GB, s.D])
        o_in = sb("o_in", [s.TT, U, s.H, GB, s.DK])
        h_in = sb("h_in", [s.TT, U, GB, s.D])
        o_rows = sb("o_rows", [s.TT, 2, GB, s.D])
        o_t = sb("o_t", [PARTS, 2, NT])
        r_sb = sb("r_sb", [s.TT, U, GB, s.D])
        z_sb = sb("z_sb", [s.TT, 2, GB, s.D])
        out_sb = sb("out_sb", [s.TT, U, GB, s.D])
        stats = sb("stats4", [s.TT, U, GB, 6])
        mv = sb("mv4", [s.TT, U, GB, 2])
        std = sb("std4", [s.TT, U, GB])
        shift = sb("shift4", [s.TT, U, GB])
        scale = sb("scale4", [s.TT, U, GB])
        t_p = [ps(f"t_p{i}") for i in range(2)]
        a_p = [ps(f"a_p{i}") for i in range(2)]
        w_loaded = sem("w_loaded4")
        group_loaded = [sem(f"group_loaded{u}") for u in range(U)]
        o_gathered = sem("o_gathered")
        o_turned = sem("o_turned")
        o_turned_copied = sem("o_turned_copied")
        attention_ready = sem("attention_ready")
        r_ready = sem("r_ready")
        stats_done = sem("stats_done4")
        moments_ready = sem("moments_ready4")
        std_ready = sem("std_ready4")
        scale_ready = sem("scale_ready")
        coefficients_ready = sem("coefficients_ready")
        z_ready = sem("z_ready")
        out_ready = sem("out_ready")
        out_stored = [sem(f"out_stored{u}") for u in range(U)]
        block = ctx.enter_context(nc.Block())

        @block.sync
        def _(sp):
            sp.dma_start(wo_sb[:, :], wo).then_inc(w_loaded, 16)
            sp.dma_start(bo_row[0:1, :, :], dram(bo, 0, [[s.D, 1], [0, GB], [1, s.D]])).then_inc(w_loaded, 16)

            def load(k, u):
                n = U * k + u
                tile, b0 = n // PER, GB * (n % PER)
                wait(sp, o_gathered, n - U + 1)
                sp.dma_start(o_in[:, u, :, :, :].rearrange("p h b c -> p h (b c)"),
                             dram(scratch["o"], tile * s.TT * s.H * s.B * s.DK + b0 * s.DK,
                                  [[s.H * s.B * s.DK, s.TT], [s.B * s.DK, s.H], [1, GB * s.DK]]))\
                  .then_inc(group_loaded[u], 16)
                wait(sp, r_ready, n - U + 1)
                sp.dma_start(h_in[:, u, :, :].rearrange("p b c -> p (b c)"),
                             dram(scratch["h"], tile * s.TT * s.B * s.D + b0 * s.D,
                                  [[s.B * s.D, s.TT], [1, GB * s.D]])).then_inc(group_loaded[u], 16)

            for u in range(U):
                load(0, u)
            with sp.Fori(1, STEPS) as k:
                for u in range(U):
                    load(k, u)

        @block.gpsimd
        def _(pool):
            def gather_heads(k, u):
                n = U * k + u
                pool.wait_ge(group_loaded[u], 32 * (k + 1))
                wait(pool, o_turned, n - 1)
                nc.gpsimd.tensor_tensor(o_rows[:, u % 2, :, :].rearrange("p b (h c) -> p h b c", h=s.H),
                                        o_in[:, u, :, :, :],
                                        zeros[0:s.TT, :].unsqueeze(2).unsqueeze(3)
                                        .to_broadcast([s.TT, s.H, GB, s.DK]), ALU.add).then_inc(o_gathered, 1)

            def add_and_store(k, u):
                n = U * k + u
                tile, b0 = n // PER, GB * (n % PER)
                pool.wait_ge(z_ready, n + 1)
                wait(pool, out_stored[u], 16 * k)
                nc.gpsimd.tensor_tensor(out_sb[:, u, :, :], r_sb[:, u, :, :], z_sb[:, u % 2, :, :], ALU.add)\
                  .then_inc(out_ready, 1)
                pool.wait_ge(out_ready, n + 1)
                pool.dma_start(dram(out, b0 * s.T * s.D + tile * s.TT * s.D,
                                    [[s.D, s.TT], [s.T * s.D, GB], [1, s.D]]), out_sb[:, u, :, :])\
                    .then_inc(out_stored[u], 16)

            def step(k):
                for u in range(U):
                    gather_heads(k, u)
                    if not (isinstance(k, int) and u < 2):
                        add_and_store(k if u >= 2 else k - 1, (u - 2) % U)

            step(0)
            with pool.Fori(1, STEPS) as k:
                step(k)
            add_and_store(STEPS - 1, U - 2)
            add_and_store(STEPS - 1, U - 1)
            for u in range(U):
                pool.wait_ge(out_stored[u], 16 * STEPS)

        @block.tensor
        def _(pe):
            pe.wait_ge(w_loaded, 32)

            def turn(k, u):
                n = U * k + u
                pe.wait_ge(o_gathered, n + 1)
                wait(pe, o_turned_copied, n - 1)
                for b in range(GB):
                    last = nc.tensor.matmul(t_p[u % 2][:, s.TT * b:s.TT * (b + 1)], o_rows[:, u % 2, b, :],
                                            ident[0:s.TT, 0:s.TT], start=True, stop=True, is_transpose=True)
                last.then_inc(o_turned, 1)

            def project(n, u):
                pe.wait_ge(o_turned_copied, n + 1)
                wait(pe, r_ready, n - 1)
                bank = a_p[u % 2]
                nc.tensor.matmul(bank[0:s.TT, :], ones[0:1, 0:s.TT], bo_row[0:1, :, :].rearrange("p a c -> p (a c)"),
                                 start=True, stop=False, skip_group_check=True)
                for b in range(GB):
                    last = nc.tensor.matmul(bank[0:s.TT, s.D * b:s.D * (b + 1)], o_t[:, u % 2, s.TT * b:s.TT * (b + 1)],
                                            wo_sb[:, :], start=False, stop=True, skip_group_check=True)
                last.then_inc(attention_ready, 1)

            def step(k):
                for u in range(U):
                    turn(k, u)
                    if not (isinstance(k, int) and u == 0):
                        project(U * k + u - 1, (u - 1) % U)

            step(0)
            with pe.Fori(1, STEPS) as k:
                step(k)
            project(N - 1, U - 1)

        @block.scalar
        def _(act):
            def copy_turned(n, u):
                act.wait_ge(o_turned, n + 1)
                wait(act, attention_ready, n - 1)
                nc.scalar.activation(o_t[:, u % 2, :], t_p[u % 2][:, 0:NT], ACT.Copy).then_inc(o_turned_copied, 1)

            def deviation(n, u):
                act.wait_ge(moments_ready, n + 1)
                nc.scalar.activation(std[:, u, :], mv[:, u, :, 1], ACT.Sqrt, bias=eps[0:s.TT, 0:1])\
                  .then_inc(std_ready, 1)

            def normed(n, u):
                act.wait_ge(coefficients_ready, n + 1)
                wait(act, out_ready, n - 1)
                for b in range(GB):
                    last = nc.scalar.activation(z_sb[:, u % 2, b, :], r_sb[:, u, b, :], ACT.Identity,
                                                bias=shift[:, u, b:b + 1], scale=scale[:, u, b:b + 1])
                last.then_inc(z_ready, 1)

            def step(k):
                for u in range(U):
                    n = U * k + u
                    copy_turned(n, u)
                    if not (isinstance(k, int) and u < 1):
                        deviation(n - 1, (u - 1) % U)
                    if not (isinstance(k, int) and u < 2):
                        normed(n - 2, (u - 2) % U)

            step(0)
            with act.Fori(1, STEPS) as k:
                step(k)
            deviation(N - 1, U - 1)
            normed(N - 2, U - 2)
            normed(N - 1, U - 1)

        @block.vector
        def _(dve):
            def residual(k, u):
                n = U * k + u
                dve.wait_ge(attention_ready, n + 1)
                dve.wait_ge(group_loaded[u], 32 * (k + 1))
                wait(dve, out_ready, n - U + 1)
                nc.vector.tensor_tensor(r_sb[:, u, :, :].rearrange("p b c -> p (b c)"), a_p[u % 2][0:s.TT, :],
                                        h_in[:, u, :, :].rearrange("p b c -> p (b c)"), ALU.add).then_inc(r_ready, 1)
                dve.wait_ge(r_ready, n + 1)
                for b in range(GB):
                    last = nc.vector.bn_stats(stats[:, u, b, :], r_sb[:, u, b, :])
                last.then_inc(stats_done, 1)

            def moments(u):
                for b in range(GB):
                    last = nc.vector.bn_aggr(mv[:, u, b, :], stats[:, u, b, :])
                last.then_inc(moments_ready, 1)

            def invert(n, u):
                dve.wait_ge(std_ready, n + 1)
                nc.vector.reciprocal(scale[:, u, :], std[:, u, :]).then_inc(scale_ready, 1)

            def shift_of(n, u):
                dve.wait_ge(scale_ready, n + 1)
                nc.vector.scalar_tensor_tensor(shift[:, u, :], mv[:, u, :, 0], -1.0, scale[:, u, :], ALU.mult,
                                               ALU.mult).then_inc(coefficients_ready, 1)

            def step(k):
                for u in range(U):
                    n = U * k + u
                    residual(k, u)
                    dve.wait_ge(stats_done, n + 1)
                    if isinstance(k, int) and u < 1:
                        moments(u)
                    else:
                        invert(n - 1, (u - 1) % U)
                        moments(u)
                        shift_of(n - 1, (u - 1) % U)

            step(0)
            with dve.Fori(1, STEPS) as k:
                step(k)
            invert(N - 1, U - 1)
            shift_of(N - 1, U - 1)


_INS = ["x", "L0_tok_W", "L0_tok_b", "L0_tok_gamma", "L0_tok_beta", "L0_attn_pos_emb", "L0_attn_Wq", "L0_attn_bq",
        "L0_attn_Wk", "L0_attn_bk", "L0_attn_Wv", "L0_attn_bv", "L0_attn_Wp", "L0_attn_bp", "L0_attn_Wo",
        "L0_attn_bo", "L0_attn_pos_bias_u", "L0_attn_pos_bias_v"]


def kernel(**inputs):
    import numpy as _np
    import concourse.bacc as _bacc
    from concourse import mybir as _mybir
    from concourse.bass_utils import run_bass_kernel_spmd as _run

    nc = _bacc.Bacc("TRN2", target_bir_lowering=False, num_devices=1)
    arrays, args = {}, []
    for name in _INS:
        a = _np.ascontiguousarray(inputs[name])
        arrays[f"in_{name}"] = a
        args.append(nc.dram_tensor(f"in_{name}", a.shape, _mybir.dt.from_np(a.dtype), kind="ExternalInput").ap())
    batches, steps, channels = inputs["x"].shape
    frames = steps - inputs["L0_tok_W"].shape[1] // channels + 1
    out = nc.dram_tensor("out_0", (batches, frames, channels), _mybir.dt.float32, kind="ExternalOutput").ap()
    build(nc, *args, out)
    r = _run(nc, [arrays], core_ids=[0])
    return r.results[0]["out_0"]
```

```python
import concourse.bass as bass
from concourse import mybir
from concourse.alu_op_type import AluOpType as ALU
from contextlib import ExitStack

F32 = mybir.dt.float32
BF16 = mybir.dt.bfloat16
ACT = mybir.ActivationFunctionType
AX_X = mybir.AxisListType.X

PARTS = 128
QUERY_PART = (0, 0, 1, 1, 0, 2)
KEY_PART = (0, 1, 0, 1, 2, 0)
SLOTS = len(QUERY_PART)
EPS = 1e-5


def wait(engine, semaphore, value):
    if not (isinstance(value, int) and value <= 0):
        engine.wait_ge(semaphore, value)


def dram(ap, offset, pattern):
    return bass.AP(tensor=ap.tensor, offset=offset, ap=pattern)


class Shapes:
    def __init__(self, x, conv_w, pos_emb, pos_bias_u):
        self.B, self.S, self.D = x.shape
        self.CONTEXT = conv_w.shape[1] // self.D
        self.T = self.S - self.CONTEXT + 1
        self.P = pos_emb.shape[1]
        self.H, self.DK = pos_bias_u.shape
        self.TT = self.T // 2
        self.QT = self.T // 4
        self.J0 = PARTS
        self.J1 = self.T - PARTS
        self.PAIRS = self.B // 2
        self.ROW = self.B * self.T
        self.VW = self.DK + 1
        self.PW = 512
        assert self.D == PARTS and self.H * self.DK == self.D and self.T == 252 and self.B == 64


def build(nc, x, tok_w, tok_b, tok_gamma, tok_beta, pos_emb, wq, bq, wk, bk, wv, bv, wp, bp, wo, bo, bias_u, bias_v,
          out):
    s = Shapes(x, tok_w, pos_emb, bias_u)
    scratch = {
        "q": nc.dram_tensor("scratch_q", [SLOTS * PARTS, s.ROW], BF16, kind="Internal").ap(),
        "k": nc.dram_tensor("scratch_k", [SLOTS * PARTS, s.ROW], BF16, kind="Internal").ap(),
        "p": nc.dram_tensor("scratch_p", [SLOTS * PARTS, s.PW], BF16, kind="Internal").ap(),
        "c": nc.dram_tensor("scratch_c", [3, s.H * s.PW], BF16, kind="Internal").ap(),
        "v": nc.dram_tensor("scratch_v", [s.H * PARTS, s.B * 2 * s.VW], F32, kind="Internal").ap(),
        "h": nc.dram_tensor("scratch_h", [2 * s.TT, s.B * s.D], F32, kind="Internal").ap(),
        "o": nc.dram_tensor("scratch_o", [s.H * 2 * s.B // 16 * PARTS, 4 * s.TT], F32, kind="Internal").ap(),
    }
    with ExitStack() as ctx:
        ident = ctx.enter_context(nc.sbuf_tensor("ident", [PARTS, PARTS], F32))
        ones = ctx.enter_context(nc.sbuf_tensor("ones", [PARTS, PARTS], F32))
        eps = ctx.enter_context(nc.sbuf_tensor("eps", [PARTS, 1], F32))
        zeros = ctx.enter_context(nc.sbuf_tensor("zeros", [PARTS, 1], F32))
        with ExitStack() as early:
            y = early.enter_context(nc.sbuf_tensor("y", [PARTS, s.ROW], F32))
            norm = early.enter_context(nc.sbuf_tensor("norm", [PARTS, 8], F32))
            conv_block(nc, s, x, tok_w, tok_b, tok_gamma, tok_beta, ident, ones, eps, zeros, y, norm)
            project_block(nc, s, pos_emb, wq, bq, wk, bk, wv, bv, wp, bp, bias_u, bias_v, ident, ones, eps, zeros, y, norm,
                          scratch)
        attend_block(nc, s, ident, scratch)
        finish_block(nc, s, wo, bo, ident, ones, eps, zeros, scratch, out)


def opener(nc, ctx):
    def sb(name, shape, dt=F32):
        return ctx.enter_context(nc.sbuf_tensor(name, shape, dt))

    def ps(name, shape=(PARTS, 512), dt=F32):
        return ctx.enter_context(nc.psum_tensor(name, list(shape), dt))

    def sem(name):
        return ctx.enter_context(nc.semaphore(name))

    return sb, ps, sem


def conv_block(nc, s, x, tok_w, tok_b, tok_gamma, tok_beta, ident, ones, eps, zeros, y, norm):
    U = 4
    STEPS = s.PAIRS // U
    NT = 2 * s.T
    with ExitStack() as ctx:
        sb, ps, sem = opener(nc, ctx)
        w_in = sb("w_in", [PARTS, s.CONTEXT * s.D])
        w_t = sb("w_t", [PARTS, s.CONTEXT, PARTS])
        vec = sb("vec", [PARTS, 4])
        x_in = sb("x_in", [PARTS, U, 4 * s.D])
        x_t = sb("x_t", [PARTS, 2, 2 * s.S])
        stats = sb("stats", [PARTS, s.PAIRS, 6])
        mv = sb("mv", [PARTS, 5])
        x_tp = [ps(f"x_tp{i}") for i in range(2)]
        y_p = [ps(f"y_p{i}") for i in range(2)]
        w_p = [ps(f"w_p{i}") for i in range(2)]
        const_set = sem("const_set")
        ident_ready = sem("ident_ready")
        w_loaded = sem("w_loaded")
        vec_loaded = sem("vec_loaded")
        x_loaded = [sem(f"x_loaded{u}") for u in range(U)]
        w_transposed = sem("w_transposed")
        w_copied = sem("w_copied")
        x_transposed = sem("x_transposed")
        x_copied = sem("x_copied")
        y_ready = sem("y_ready")
        y_copied = sem("y_copied")
        stats_done = sem("stats_done")
        moments_ready = sem("moments_ready")
        std_ready = sem("std_ready")
        norm_step = sem("norm_step")
        block = ctx.enter_context(nc.Block())

        @block.sync
        def _(sp):
            sp.dma_start(w_in[:, :], tok_w).then_inc(w_loaded, 16)
            for i, v in enumerate((tok_b, tok_gamma, tok_beta)):
                sp.dma_start(vec[:, i:i + 1], v.rearrange("(p a) -> p a", a=1)).then_inc(vec_loaded, 16)

            def step(k):
                for u in range(U):
                    n = U * k + u
                    wait(sp, x_transposed, n - U + 1)
                    sp.dma_start(x_in[:, u, :].rearrange("p (a c) -> p a c", a=4),
                                 dram(x, 2 * s.S * s.D * n, [[s.D, PARTS], [PARTS * s.D, 4], [1, s.D]]))\
                      .then_inc(x_loaded[u], 16)

            step(0)
            with sp.Fori(1, STEPS) as k:
                step(k)

        @block.gpsimd
        def _(pool):
            nc.gpsimd.memset(ident[:, :], 0.0).then_inc(const_set, 1)
            nc.gpsimd.memset(ones[:, :], 1.0).then_inc(const_set, 1)
            nc.gpsimd.memset(eps[:, :], EPS).then_inc(const_set, 1)
            nc.gpsimd.memset(zeros[:, :], 0.0).then_inc(const_set, 1)
            pool.wait_ge(const_set, 4)
            nc.gpsimd.affine_select(out=ident[:, :], in_=ident[:, :], compare_op=ALU.not_equal, fill=1.0, base=0,
                                    pattern=[[-1, PARTS]], channel_multiplier=1).then_inc(ident_ready, 1)

        @block.tensor
        def _(pe):
            pe.wait_ge(ident_ready, 1)
            pe.wait_ge(w_loaded, 16)
            for tap in range(s.CONTEXT):
                last = nc.tensor.matmul(w_p[tap // 4][:, PARTS * (tap % 4):PARTS * (tap % 4 + 1)],
                                        w_in[:, PARTS * tap:PARTS * (tap + 1)], ident[:, :], start=True, stop=True,
                                        is_transpose=True)
                if tap == 3 or tap == s.CONTEXT - 1:
                    last.then_inc(w_transposed, 1)

            def transpose_x(u, k):
                n = U * k + u
                pe.wait_ge(x_loaded[u], 16 * (k + 1))
                wait(pe, x_copied, n - 1)
                for a in range(4):
                    last = nc.tensor.matmul(x_tp[u % 2][:, PARTS * a:PARTS * (a + 1)],
                                            x_in[:, u, PARTS * a:PARTS * (a + 1)], ident[:, :], start=True,
                                            stop=True, is_transpose=True)
                last.then_inc(x_transposed, 1)

            def convolve(u, n):
                wait(pe, x_copied, n + 1)
                wait(pe, y_copied, n - 1)
                src = x_t[:, u % 2, :].rearrange("p (b c) -> p b c", b=2)
                for tap in range(s.CONTEXT):
                    last = nc.tensor.matmul(y_p[u % 2][:, 0:NT], w_t[:, tap, :], src[:, :, tap:tap + s.T],
                                            start=(tap == 0), stop=(tap == s.CONTEXT - 1))
                last.then_inc(y_ready, 1)

            def step(k):
                for u in range(U):
                    transpose_x(u, k)
                    if not (isinstance(k, int) and k == 0 and u == 0):
                        convolve((u - 1) % U, U * k + u - 1)

            pe.wait_ge(w_copied, 2)
            step(0)
            with pe.Fori(1, STEPS) as k:
                step(k)
            convolve(U - 1, s.PAIRS - 1)

        @block.scalar
        def _(act):
            act.wait_ge(w_transposed, 2)
            nc.scalar.activation(w_t[:, 0:4, :].rearrange("p a c -> p (a c)"), w_p[0][:, :], ACT.Copy)\
              .then_inc(w_copied, 1)
            nc.scalar.activation(w_t[:, 4, :], w_p[1][:, 0:PARTS], ACT.Copy).then_inc(w_copied, 1)
            act.wait_ge(vec_loaded, 48)

            def copy_x(u, n):
                act.wait_ge(x_transposed, n + 1)
                wait(act, y_ready, n - 1)
                nc.scalar.activation(x_t[:, u % 2, :], x_tp[u % 2][:, :], ACT.Copy).then_inc(x_copied, 1)

            def copy_y(u, n):
                act.wait_ge(y_ready, n + 1)
                nc.scalar.activation(y[:, bass.ds(NT * n, NT)], y_p[u % 2][:, 0:NT], ACT.Identity,
                                     bias=vec[:, 0:1]).then_inc(y_copied, 1)

            def step(k):
                for u in range(U):
                    copy_x(u, U * k + u)
                    if not (isinstance(k, int) and k == 0 and u == 0):
                        copy_y((u - 1) % U, U * k + u - 1)

            step(0)
            with act.Fori(1, STEPS) as k:
                step(k)
            copy_y(U - 1, s.PAIRS - 1)
            act.wait_ge(moments_ready, 1)
            act.wait_ge(const_set, 4)
            nc.scalar.activation(mv[:, 2:3], mv[:, 1:2], ACT.Sqrt, bias=eps[:, 0:1]).then_inc(std_ready, 1)

        @block.vector
        def _(dve):
            with dve.Fori(0, s.PAIRS) as n:
                dve.wait_ge(y_copied, n + 1)
                nc.vector.bn_stats(stats[:, bass.ds(n, 1), :].rearrange("p a b -> p (a b)"),
                                   y[:, bass.ds(NT * n, NT)]).then_inc(stats_done, 1)
            dve.wait_ge(stats_done, s.PAIRS)
            nc.vector.bn_aggr(mv[:, 0:2], stats[:, :, :].rearrange("p a b -> p (a b)")).then_inc(moments_ready, 1)
            dve.wait_ge(std_ready, 1)
            nc.vector.reciprocal(mv[:, 4:5], mv[:, 2:3]).then_inc(norm_step, 1)
            dve.wait_ge(norm_step, 1)
            dve.wait_ge(vec_loaded, 48)
            nc.vector.tensor_tensor(norm[:, 0:1], mv[:, 4:5], vec[:, 1:2], ALU.mult).then_inc(norm_step, 1)
            dve.wait_ge(norm_step, 2)
            nc.vector.tensor_tensor(mv[:, 3:4], mv[:, 0:1], norm[:, 0:1], ALU.mult).then_inc(norm_step, 1)
            dve.wait_ge(norm_step, 3)
            nc.vector.tensor_tensor(norm[:, 1:2], vec[:, 2:3], mv[:, 3:4], ALU.subtract)


def project_block(nc, s, pos_emb, wq, bq, wk, bk, wv, bv, wp, bp, bias_u, bias_v, ident, ones, eps, zeros, y, norm, scratch):
    U = 4
    STEPS = s.PAIRS // U
    NT = 2 * s.T
    GB = 4
    SCALE = float(s.DK) ** -0.5
    with ExitStack() as ctx:
        sb, ps, sem = opener(nc, ctx)
        w_qkvp = sb("w_qkvp", [PARTS, 4, s.D])
        vec = sb("vec2", [PARTS, 8])
        bv_row = sb("bv_row", [1, 4 * s.D])
        bv_parts = sb("bv_parts", [1, 3, 4 * s.D], BF16)
        bv_stack = sb("bv_stack", [3, 4 * s.D], BF16)
        ones_bf = sb("ones_bf", [3, PARTS], BF16)
        pos_in = sb("pos_in", [PARTS, 4, s.D])
        pos_t = sb("pos_t", [PARTS, s.PW])
        pos_f = sb("pos_f", [PARTS, s.PW])
        pos_r = sb("pos_r", [PARTS, s.PW])
        pos_parts = sb("pos_parts", [PARTS, 3, s.PW], BF16)
        head_mask = sb("head_mask", [PARTS, s.H])
        vu_block = sb("vu_block", [PARTS, s.H])
        c_f = sb("c_f", [s.H, s.PW])
        c_parts = sb("c_parts", [s.H, 3, s.PW], BF16)
        h_t = sb("h_t", [PARTS, 2, NT])
        h_sb = sb("h_sb", [s.TT, U, 4, s.D])
        xn = sb("xn", [s.TT, 2, 4, s.D])
        xn_t = sb("xn_t", [PARTS, 2, NT])
        stats = sb("stats2", [s.TT, U, 4, 6])
        mv = sb("mv2", [s.TT, U, 4, 2])
        std = sb("std", [s.TT, U, 4])
        rstd = sb("rstd", [s.TT, U, 4])
        q_f = sb("q_f", [PARTS, 2, NT])
        k_f = sb("k_f", [PARTS, 2, NT])
        q_parts = sb("q_parts", [PARTS, 2, 3, 2, GB * s.TT], BF16)
        k_parts = sb("k_parts", [PARTS, 2, 3, GB * s.T], BF16)
        v_sb = sb("v_sb", [PARTS, 2, s.H, GB, 2, s.VW])
        h_p = [ps(f"h_p{i}") for i in range(2)]
        xn_p = [ps(f"xn_p{i}") for i in range(2)]
        q_p, k_p = ps("q_p"), ps("k_p")
        v_p = [ps(f"v_p{i}") for i in range(2)]
        w_loaded = sem("w_loaded2")
        pos_loaded = sem("pos_loaded")
        setup = sem("setup")
        pool_set = sem("pool_set")
        pos_transposed = sem("pos_transposed")
        pos_copied = sem("pos_copied")
        pos_projected = sem("pos_projected")
        pos_biased = sem("pos_biased")
        vu_ready = sem("vu_ready")
        c_ready = sem("c_ready")
        pos_cut = sem("pos_cut")
        bias_cut = sem("bias_cut")
        bias_stacked = sem("bias_stacked")
        tables_stored = sem("tables_stored")
        h_ready = sem("h_ready")
        h_turned = sem("h_turned")
        h_copied = sem("h_copied")
        h_stored = [sem(f"h_stored{u}") for u in range(U)]
        stats_done = sem("stats_done2")
        moments_ready = sem("moments_ready2")
        std_ready = sem("std_ready2")
        rstd_ready = sem("rstd_ready")
        xn_ready = sem("xn_ready")
        xn_turned = sem("xn_turned")
        xn_copied = sem("xn_copied")
        qk_projected = sem("qk_projected")
        v_projected = sem("v_projected")
        q_biased = sem("q_biased")
        k_biased = sem("k_biased")
        v_copied = sem("v_copied")
        q_step = sem("q_step")
        k_step = sem("k_step")
        qkv_stored = [sem(f"qkv_stored{i}") for i in range(2)]
        STORES = 2 * SLOTS + 1
        block = ctx.enter_context(nc.Block())

        @block.sync
        def _(sp):
            for i, w in enumerate((wq, wk, wv, wp)):
                sp.dma_start(w_qkvp[:, i, :], w).then_inc(w_loaded, 16)
            for i, v in enumerate((bq, bk, bp)):
                sp.dma_start(vec[:, i:i + 1], v.rearrange("(p a) -> p a", a=1)).then_inc(w_loaded, 16)
            for i, v in enumerate((bias_u, bias_v)):
                sp.dma_start(vec[:, 3 + i:4 + i], dram(v, 0, [[1, PARTS], [1, 1]])).then_inc(w_loaded, 16)
            sp.dma_start(bv_row[0:1, :].rearrange("p (a c) -> p a c", a=4), dram(bv, 0, [[s.D, 1], [0, 4], [1, s.D]]))\
              .then_inc(w_loaded, 16)
            for a in range(4):
                rows = min(PARTS, s.P - PARTS * a)
                sp.dma_start(pos_in[0:rows, a, :], pos_emb[0, PARTS * a:PARTS * a + rows, :]).then_inc(pos_loaded, 16)
            sp.wait_ge(bias_cut, 1)
            for part in range(3):
                sp.dma_start(bv_stack[part:part + 1, :], bv_parts[0:1, part, :]).then_inc(bias_stacked, 16)
            sp.wait_ge(pos_cut, 2)
            for slot in range(SLOTS):
                sp.dma_start(dram(scratch["p"], s.PW * slot, [[s.PW * SLOTS, PARTS], [1, s.PW]]),
                             pos_parts[:, KEY_PART[slot], :]).then_inc(tables_stored, 16)
            for part in range(3):
                sp.dma_start(dram(scratch["c"], s.H * s.PW * part, [[s.PW, s.H], [1, s.PW]]),
                             c_parts[:, part, :]).then_inc(tables_stored, 16)

            def store_h(u, k):
                n = U * k + u
                sp.wait_ge(h_copied, n + 1)
                sp.dma_start(dram(scratch["h"], 2 * s.D * n,
                                  [[s.B * s.D, s.TT], [s.TT * s.B * s.D, 2], [1, 2 * s.D]]),
                             h_sb[:, u, :, :].rearrange("p (a b) c -> p a (b c)", a=2)).then_inc(h_stored[u], 16)

            def store_group(i, k):
                n = U * k + 2 * i + 1
                b0 = GB * (2 * k + i)
                sp.wait_ge(q_step, 4 * (n + 1))
                for slot in range(SLOTS):
                    sp.dma_start(dram(scratch["q"], b0 * s.TT + s.ROW * slot,
                                      [[s.ROW * SLOTS, PARTS], [s.B * s.TT, 2], [1, GB * s.TT]]),
                                 q_parts[:, i, QUERY_PART[slot], :, :]).then_inc(qkv_stored[i], 16)
                sp.wait_ge(k_step, 3 * (n + 1))
                for slot in range(SLOTS):
                    sp.dma_start(dram(scratch["k"], b0 * s.T + s.ROW * slot,
                                      [[s.ROW * SLOTS, PARTS], [1, GB * s.T]]),
                                 k_parts[:, i, KEY_PART[slot], :]).then_inc(qkv_stored[i], 16)
                sp.wait_ge(v_copied, 2 * (n + 1))
                sp.dma_start(dram(scratch["v"], b0 * 2 * s.VW,
                                  [[s.B * 2 * s.VW, PARTS], [PARTS * s.B * 2 * s.VW, s.H], [1, GB * 2 * s.VW]]),
                             v_sb[:, i, :, :, :, :].rearrange("p h b j c -> p h (b j c)")).then_inc(qkv_stored[i], 16)

            def step(k):
                for u in range(U):
                    store_h(u, k)
                    if u % 2 and not (isinstance(k, int) and k == 0):
                        store_group(u // 2, k - 1)

            step(0)
            with sp.Fori(1, STEPS) as k:
                step(k)
            for i in range(2):
                store_group(i, STEPS - 1)
            sp.wait_ge(tables_stored, 16 * (SLOTS + 3))
            for u in range(U):
                sp.wait_ge(h_stored[u], 16 * STEPS)
            for i in range(2):
                sp.wait_ge(qkv_stored[i], 16 * STORES * STEPS)

        @block.gpsimd
        def _(pool):
            nc.gpsimd.memset(head_mask[:, :], 1.0).then_inc(pool_set, 1)
            pool.wait_ge(pool_set, 1)
            nc.gpsimd.affine_select(out=head_mask[:, :], in_=head_mask[:, :], compare_op=ALU.is_ge, fill=0.0, base=0,
                                    pattern=[[-s.DK, s.H]], channel_multiplier=1).then_inc(pool_set, 1)
            pool.wait_ge(pool_set, 2)
            nc.gpsimd.affine_select(out=head_mask[:, :], in_=head_mask[:, :], compare_op=ALU.is_ge, fill=0.0,
                                    base=s.DK - 1, pattern=[[s.DK, s.H]], channel_multiplier=-1)\
              .then_inc(pool_set, 1)
            nc.gpsimd.memset(v_sb[:, :, :, :, :, :], 0.0).then_inc(pool_set, 1)
            pool.wait_ge(pool_set, 4)
            nc.gpsimd.memset(v_sb[:, :, :, :, :, s.DK:s.VW], 1.0).then_inc(pool_set, 1)
            pool.wait_ge(pool_set, 5)

            def cut_keys(u, k):
                n = U * k + u
                pool.wait_ge(k_biased, n + 1)
                left, zero = k_f[:, u % 2, :], zeros[:, :].to_broadcast([PARTS, NT])
                part = [k_parts[:, u // 2, j, NT * (u % 2):NT * (u % 2 + 1)] for j in range(3)]
                nc.gpsimd.tensor_tensor(left, left, part[0], ALU.subtract).then_inc(k_step, 1)
                pool.wait_ge(k_step, 3 * n + 1)
                nc.gpsimd.tensor_tensor(part[1], left, zero, ALU.add).then_inc(k_step, 1)
                pool.wait_ge(k_step, 3 * n + 2)
                nc.gpsimd.tensor_tensor(part[2], left, part[1], ALU.subtract).then_inc(k_step, 1)

            for u in range(U):
                cut_keys(u, 0)
            with pool.Fori(1, STEPS) as k:
                for u in range(U):
                    cut_keys(u, k)

        @block.tensor
        def _(pe):
            pe.wait_ge(pos_loaded, 64)
            for a in range(4):
                rows = min(PARTS, s.P - PARTS * a)
                last = nc.tensor.matmul(h_p[0][:, PARTS * a:PARTS * a + rows], pos_in[0:rows, a, :],
                                        ident[0:rows, 0:rows], start=True, stop=True, is_transpose=True)
            last.then_inc(pos_transposed, 1)
            pe.wait_ge(w_loaded, 160)
            pe.wait_ge(pos_copied, 1)
            nc.tensor.matmul(q_p[:, 0:s.P], w_qkvp[:, 3, :], pos_t[:, 0:s.P], start=True, stop=True)\
              .then_inc(pos_projected, 1)
            pe.wait_ge(pos_biased, 1)
            pe.wait_ge(vu_ready, 1)
            nc.tensor.matmul(k_p[0:s.H, 0:s.P], vu_block[:, :], pos_f[:, 0:s.P], start=True, stop=True)\
              .then_inc(c_ready, 1)
            pe.wait_ge(pos_cut, 2)
            pe.wait_ge(bias_stacked, 48)

            def turn_h(u, n):
                pe.wait_ge(h_ready, n + 1)
                wait(pe, h_copied, n - 1)
                src = h_t[:, u % 2, :].rearrange("p (b a t) -> p a b t", b=2, a=2)
                for a in range(2):
                    for b in range(2):
                        c = PARTS * (2 * a + b)
                        last = nc.tensor.matmul(h_p[u % 2][0:s.TT, c:c + PARTS], src[:, a, b, :], ident[:, :],
                                                start=True, stop=True, is_transpose=True)
                last.then_inc(h_turned, 1)

            def turn_xn(u, n):
                pe.wait_ge(xn_ready, n + 1)
                wait(pe, xn_copied, n - 1)
                for a in range(2):
                    for b in range(2):
                        c = s.T * b + s.TT * a
                        last = nc.tensor.matmul(xn_p[u % 2][:, c:c + s.TT], xn[:, u % 2, 2 * a + b, :],
                                                ident[0:s.TT, 0:s.TT], start=True, stop=True, is_transpose=True)
                last.then_inc(xn_turned, 1)

            def project(u, n):
                pe.wait_ge(xn_copied, n + 1)
                wait(pe, q_biased, n)
                wait(pe, k_biased, n)
                nc.tensor.matmul(q_p[:, 0:NT], w_qkvp[:, 0, :], xn_t[:, u % 2, :], start=True, stop=True)
                nc.tensor.matmul(k_p[:, 0:NT], w_qkvp[:, 1, :], xn_t[:, u % 2, :], start=True, stop=True)\
                  .then_inc(qk_projected, 1)
                wait(pe, v_copied, 2 * (n - 1))
                bank = v_p[u % 2]
                nc.tensor.matmul(bank[:, :], ones_bf[:, :], bv_stack[:, :], start=True, stop=False, skip_group_check=True)
                for b in range(2):
                    for j, keys in enumerate((s.J0, s.J1)):
                        c = PARTS * (2 * b + j)
                        lhs = xn_t[:, u % 2, s.T * b + PARTS * j:s.T * b + PARTS * j + keys]
                        last = nc.tensor.matmul(bank[0:keys, c:c + PARTS], lhs, w_qkvp[:, 2, :], start=False,
                                                stop=True, skip_group_check=True)
                last.then_inc(v_projected, 1)

            def step(k):
                for u in range(U):
                    n = U * k + u
                    turn_h(u, n)
                    if not (isinstance(k, int) and n < 2):
                        turn_xn((u - 2) % U, n - 2)
                    if not (isinstance(k, int) and n < 3):
                        project((u - 3) % U, n - 3)

            step(0)
            with pe.Fori(1, STEPS) as k:
                step(k)
            turn_xn(U - 2, s.PAIRS - 2)
            project(U - 3, s.PAIRS - 3)
            turn_xn(U - 1, s.PAIRS - 1)
            project(U - 2, s.PAIRS - 2)
            project(U - 1, s.PAIRS - 1)

        @block.scalar
        def _(act):
            act.wait_ge(pos_transposed, 1)
            nc.scalar.activation(pos_t[:, 0:s.P], h_p[0][:, 0:s.P], ACT.Copy).then_inc(pos_copied, 1)
            act.wait_ge(pos_projected, 1)
            act.wait_ge(setup, 3)
            nc.scalar.activation(pos_f[:, 0:s.P], q_p[:, 0:s.P], ACT.Identity, bias=vec[:, 2:3])\
              .then_inc(pos_biased, 1)

            def make_h(u, n):
                wait(act, h_turned, n - 1)
                nc.scalar.activation(h_t[:, u % 2, :], y[:, bass.ds(NT * n, NT)], ACT.Relu, bias=norm[:, 1:2],
                                     scale=norm[:, 0:1]).then_inc(h_ready, 1)

            def copy_h(u, k):
                n = U * k + u
                act.wait_ge(h_turned, n + 1)
                wait(act, h_stored[u], 16 * k)
                wait(act, xn_ready, n - U + 1)
                nc.scalar.activation(h_sb[:, u, :, :].rearrange("p a c -> p (a c)"), h_p[u % 2][0:s.TT, :], ACT.Copy)\
                  .then_inc(h_copied, 1)

            def deviation(u, n):
                act.wait_ge(moments_ready, n + 1)
                nc.scalar.activation(std[:, u, :], mv[:, u, :, 1], ACT.Sqrt, bias=eps[0:s.TT, 0:1])\
                  .then_inc(std_ready, 1)

            def copy_xn(u, n):
                act.wait_ge(xn_turned, n + 1)
                wait(act, v_projected, n - 1)
                nc.scalar.activation(xn_t[:, u % 2, :], xn_p[u % 2][:, 0:NT], ACT.Copy).then_inc(xn_copied, 1)

            def copy_qkv(u, k):
                n = U * k + u
                act.wait_ge(qk_projected, n + 1)
                wait(act, q_step, 4 * (n - 1))
                nc.scalar.activation(q_f[:, u % 2, :], q_p[:, 0:NT], ACT.Identity, bias=vec[:, 5:6], scale=SCALE)\
                  .then_inc(q_biased, 1)
                wait(act, k_step, 3 * (n - 1))
                if u % 2 == 0:
                    wait(act, qkv_stored[u // 2], 16 * STORES * k)
                nc.scalar.activation(k_parts[:, u // 2, 0, NT * (u % 2):NT * (u % 2 + 1)], k_p[:, 0:NT], ACT.Identity,
                                     bias=vec[:, 1:2])
                nc.scalar.activation(k_f[:, u % 2, :], k_p[:, 0:NT], ACT.Identity, bias=vec[:, 1:2])\
                  .then_inc(k_biased, 1)
                act.wait_ge(v_projected, n + 1)
                if u % 2 == 0:
                    if isinstance(k, int) and k == 0:
                        act.wait_ge(pool_set, 5)
                src = v_p[u % 2][:, :].rearrange("p (b j h d) -> p j h b d", b=2, j=2, h=s.H)
                dst = v_sb[:, u // 2, :, 2 * (u % 2):2 * (u % 2) + 2, :, 0:s.DK]
                for j, keys in enumerate((s.J0, s.J1)):
                    nc.scalar.activation(dst[0:keys, :, :, j, :], src[0:keys, j, :, :, :], ACT.Copy)\
                      .then_inc(v_copied, 1)

            def step(k, last=False):
                for u in range(U):
                    n = U * k + u
                    if not (last and u == U - 1):
                        make_h((u + 1) % U, n + 1)
                    copy_h(u, k)
                    if not (isinstance(k, int) and n < 1):
                        deviation((u - 1) % U, n - 1)
                    if not (isinstance(k, int) and n < 2):
                        copy_xn((u - 2) % U, n - 2)
                    if not (isinstance(k, int) and n < 3):
                        copy_qkv((u - 3) % U, k if u >= 3 else k - 1)

            act.wait_ge(setup, 3)
            act.wait_ge(pos_cut, 2)
            make_h(0, 0)
            step(0)
            with act.Fori(1, STEPS - 1) as k:
                step(k)
            step(STEPS - 1, last=True)
            deviation(U - 1, s.PAIRS - 1)
            copy_xn(U - 2, s.PAIRS - 2)
            copy_qkv(U - 3, STEPS - 1)
            copy_xn(U - 1, s.PAIRS - 1)
            copy_qkv(U - 2, STEPS - 1)
            copy_qkv(U - 1, STEPS - 1)

        @block.vector
        def _(dve):
            dve.wait_ge(w_loaded, 160)
            nc.vector.tensor_scalar(vec[:, 5:6], vec[:, 0:1], vec[:, 3:4], SCALE, ALU.add, ALU.mult).then_inc(setup, 1)
            nc.vector.tensor_scalar(vec[:, 6:7], vec[:, 4:5], vec[:, 3:4], SCALE, ALU.subtract, ALU.mult)\
              .then_inc(setup, 1)
            nc.vector.memset(pos_f[:, s.P:s.PW], 0.0).then_inc(setup, 1)
            dve.wait_ge(setup, 3)
            dve.wait_ge(pool_set, 3)
            nc.vector.tensor_scalar(vu_block[:, :], head_mask[:, :], vec[:, 6:7], None, ALU.mult).then_inc(vu_ready, 1)
            nc.vector.memset(c_f[:, s.P:s.PW], 0.0).then_inc(setup, 1)
            dve.wait_ge(c_ready, 1)
            nc.vector.tensor_copy(c_f[:, 0:s.P], k_p[0:s.H, 0:s.P]).then_inc(setup, 1)
            dve.wait_ge(setup, 5)
            nc.vector.memset(ones_bf[:, :], 1.0).then_inc(setup, 1)
            dve.wait_ge(setup, 6)
            done = 6
            for full, left, part, cut in ((bv_row, bv_row, bv_parts, bias_cut), (c_f, c_f, c_parts, pos_cut),
                                          (pos_f, pos_r, pos_parts, pos_cut)):
                nc.vector.tensor_copy(part[:, 0, :], full[:, :]).then_inc(setup, 1)
                dve.wait_ge(setup, done + 1)
                nc.vector.tensor_tensor(left[:, :], full[:, :], part[:, 0, :], ALU.subtract).then_inc(setup, 1)
                dve.wait_ge(setup, done + 2)
                nc.vector.tensor_copy(part[:, 1, :], left[:, :]).then_inc(setup, 1)
                dve.wait_ge(setup, done + 3)
                nc.vector.tensor_tensor(part[:, 2, :], left[:, :], part[:, 1, :], ALU.subtract).then_inc(cut, 1)
                done += 3

            def stats_of(u, n):
                dve.wait_ge(h_copied, n + 1)
                for a in range(4):
                    last = nc.vector.bn_stats(stats[:, u, a, :], h_sb[:, u, a, :])
                last.then_inc(stats_done, 1)

            def invert(u, n):
                dve.wait_ge(std_ready, n + 1)
                nc.vector.reciprocal(rstd[:, u, :], std[:, u, :]).then_inc(rstd_ready, 1)

            def moments(u):
                for a in range(4):
                    last = nc.vector.bn_aggr(mv[:, u, a, :], stats[:, u, a, :])
                last.then_inc(moments_ready, 1)

            def normalise(u, n):
                dve.wait_ge(rstd_ready, n + 1)
                wait(dve, xn_turned, n - 1)
                for a in range(4):
                    last = nc.vector.tensor_scalar(xn[:, u % 2, a, :], h_sb[:, u, a, :], mv[:, u, a, 0:1],
                                                   rstd[:, u, a:a + 1], ALU.subtract, ALU.mult)
                last.then_inc(xn_ready, 1)

            def cut_queries(u, k):
                n = U * k + u
                dve.wait_ge(q_biased, n + 1)
                if u % 2 == 0:
                    wait(dve, qkv_stored[u // 2], 16 * STORES * k)
                left = q_f[:, u % 2, :].rearrange("p (b a t) -> p b a t", b=2, a=2)
                part = [q_parts[:, u // 2, j, :, :].rearrange("p a (b t) -> p b a t", b=GB)
                        [:, 2 * (u % 2):2 * (u % 2) + 2, :, :] for j in range(3)]
                nc.vector.tensor_copy(part[0], left).then_inc(q_step, 1)
                dve.wait_ge(q_step, 4 * n + 1)
                nc.vector.tensor_tensor(left, left, part[0], ALU.subtract).then_inc(q_step, 1)
                dve.wait_ge(q_step, 4 * n + 2)
                nc.vector.tensor_copy(part[1], left).then_inc(q_step, 1)
                dve.wait_ge(q_step, 4 * n + 3)
                nc.vector.tensor_tensor(part[2], left, part[1], ALU.subtract).then_inc(q_step, 1)

            def step(k):
                for u in range(U):
                    n = U * k + u
                    stats_of(u, n)
                    dve.wait_ge(stats_done, n + 1)
                    if isinstance(k, int) and n < 1:
                        moments(u)
                    else:
                        invert((u - 1) % U, n - 1)
                        moments(u)
                        normalise((u - 1) % U, n - 1)
                    if not (isinstance(k, int) and n < 4):
                        cut_queries(u, k - 1)

            step(0)
            with dve.Fori(1, STEPS) as k:
                step(k)
            invert(U - 1, s.PAIRS - 1)
            normalise(U - 1, s.PAIRS - 1)
            for u in range(U):
                cut_queries(u, STEPS - 1)


def attend_block(nc, s, ident, scratch):
    UNITS = 2 * s.H
    ITERS = 4
    G = UNITS * ITERS
    IB = s.B // ITERS
    NP = IB // 2
    HALF = IB // 2
    CT = 7
    CHUNKS = s.QT // CT
    CN = CT * s.B
    UROW = s.B * s.T
    STACK = SLOTS * s.DK
    CROWS = STACK + 3
    EW = 256
    BESIDE = ((0, 1), (2,), (3, 4), (5,), (6, 7), (8,), (), ())
    assert CHUNKS == 9 and NP == len(BESIDE)
    with ExitStack() as ctx:
        sb, ps, sem = opener(nc, ctx)
        pos = sb("pos", [CROWS, 2 * s.PW], BF16)
        q_all = sb("q_all", [CROWS, 2 * s.B * s.TT], BF16)
        bd_t = sb("bd_t", [PARTS, 2 * UROW])
        bd_in = sb("bd_in", [PARTS, 2, HALF, 2, s.TT])
        q_in = sb("q_in", [STACK, 2, HALF, s.TT], BF16)
        k_in = sb("k_in", [STACK, 2, HALF, s.T], BF16)
        v_in = sb("v_in", [PARTS, 2, HALF, 2, s.VW])
        neg_max = sb("neg_max", [s.TT, 4, 2])
        e_sb = sb("e_sb", [s.TT, 2, 2, EW])
        e_t = sb("e_t", [PARTS, 4, 2 * s.T])
        o_sb = sb("o_sb", [PARTS, IB // 4, s.TT])
        bd_p = [ps(f"bd_p{i}") for i in range(3)]
        s_p = [ps(f"s_p{i}") for i in range(2)]
        e_p = [ps(f"e_p{i}") for i in range(2)]
        o_p = ps("o_p")
        const_set = sem("const_set3")
        pos_loaded = sem("pos_loaded3")
        q_all_loaded = sem("q_all_loaded")
        bd_ready = sem("bd_ready")
        bd_copied = sem("bd_copied")
        in_loaded = [sem(f"in_loaded{i}") for i in range(2)]
        v_loaded = [sem(f"v_loaded{i}") for i in range(2)]
        s_ready = sem("s_ready")
        max_ready = sem("max_ready")
        exp_done = sem("exp_done")
        e_turned = sem("e_turned")
        e_copied = sem("e_copied")
        o_ready = sem("o_ready")
        o_cleared = sem("o_cleared")
        o_copied = sem("o_copied")
        o_stored = sem("o_stored")
        block = ctx.enter_context(nc.Block())

        @block.sync
        def _(sp):
            def load_half(g, half):
                unit, head = g // ITERS, g // (2 * ITERS)
                b0 = (g % ITERS) * IB + half * HALF
                wait(sp, s_ready, NP * (g - 1) + NP // 2 * (half + 1))
                sp.wait_ge(bd_copied, CHUNKS * ITERS * (unit + 1))
                sp.dma_start(bd_in[:, half, :, :, :].rearrange("p b j t -> p (b j t)"),
                             bd_t[:, bass.ds((unit % 2) * UROW + b0 * s.T, HALF * s.T)]).then_inc(in_loaded[half], 16)
                sp.dma_start(q_in[:, half, :, :].rearrange("p b t -> p (b t)"),
                             dram(scratch["q"], head * STACK * s.ROW + (unit % 2) * s.B * s.TT + b0 * s.TT,
                                  [[s.ROW, STACK], [1, HALF * s.TT]]))\
                  .then_inc(in_loaded[half], 16)
                sp.dma_start(k_in[:, half, :, :].rearrange("p b t -> p (b t)"),
                             dram(scratch["k"], head * STACK * s.ROW + b0 * s.T, [[s.ROW, STACK], [1, HALF * s.T]]))\
                  .then_inc(in_loaded[half], 16)

            def load_values(g, half):
                head = g // (2 * ITERS)
                b0 = (g % ITERS) * IB + half * HALF
                wait(sp, o_ready, NP // 2 * (g - 1) + NP // 4 * (half + 1))
                sp.dma_start(v_in[:, half, :, :, :].rearrange("p b j c -> p (b j c)"),
                             dram(scratch["v"], head * PARTS * s.B * 2 * s.VW + b0 * 2 * s.VW,
                                  [[s.B * 2 * s.VW, PARTS], [1, HALF * 2 * s.VW]])).then_inc(v_loaded[half], 16)

            def store_o(g):
                sp.wait_ge(o_copied, g + 1)
                row = IB // 4 * s.TT
                sp.dma_start(dram(scratch["o"], g * PARTS * row, [[row, PARTS], [1, row]]),
                             o_sb[:, :, :].rearrange("p m t -> p (m t)")).then_inc(o_stored, 16)

            load_half(0, 0)
            load_values(0, 0)
            load_half(0, 1)
            load_values(0, 1)

            def step(g, first=False):
                if not first:
                    store_o(g - 1)
                load_half(g + 1, 0)
                load_values(g + 1, 0)
                load_half(g + 1, 1)
                load_values(g + 1, 1)

            step(0, first=True)
            with sp.Fori(1, G - 1) as g:
                step(g)
            store_o(G - 2)
            store_o(G - 1)
            sp.wait_ge(o_stored, 16 * G)

        @block.gpsimd
        def _(pool):
            nc.gpsimd.memset(q_all[STACK:CROWS, :], 1.0).then_inc(const_set, 1)
            pool.wait_ge(const_set, 1)
            nc.gpsimd.memset(e_sb[:, :, :, s.T:EW], 0.0).then_inc(const_set, 1)
            PCOLS = s.PW // 8

            def load_positions(head, part, cols, before):
                wait(pool, pos_loaded, 16 * before)
                at = (head % 2) * s.PW + part * cols
                pool.dma_start(pos[0:STACK, bass.ds(at, cols)],
                             dram(scratch["p"], head * STACK * s.PW + part * cols, [[s.PW, STACK], [1, cols]]))\
                  .then_inc(pos_loaded, 16)
                pool.dma_start(pos[STACK:CROWS, bass.ds(at, cols)],
                             dram(scratch["c"], head * s.PW + part * cols, [[s.H * s.PW, 3], [1, cols]]))\
                  .then_inc(pos_loaded, 16)

            PART = s.B // ITERS * s.TT

            def load_queries(unit, part, before):
                wait(pool, q_all_loaded, 16 * before)
                pool.dma_start(q_all[0:STACK, bass.ds((unit % 2) * s.B * s.TT + part * PART, PART)],
                             dram(scratch["q"],
                                  (unit // 2) * STACK * s.ROW + (unit % 2) * s.B * s.TT + part * PART,
                                  [[s.ROW, STACK], [1, PART]])).then_inc(q_all_loaded, 16)

            def load_next_queries(i):
                wait(pool, bd_ready, CHUNKS * ITERS * (i // ITERS))
                load_queries(i // ITERS + 1, i % ITERS, i + ITERS)

            def load_next_positions(i):
                wait(pool, bd_ready, CHUNKS * 2 * ITERS * (i // 8))
                load_positions(i // 8 + 1, i % 8, PCOLS, 2 * (i + 1))

            load_positions(0, 0, s.PW, 0)
            for i in range(ITERS):
                load_queries(0, i, i)
            LAST_P, LAST_Q = G - 2 * ITERS, G - ITERS
            for i in range(ITERS):
                load_next_queries(i)
                load_next_positions(i)
            with pool.Fori(ITERS, LAST_P) as i:
                load_next_queries(i)
                load_next_positions(i)
            with pool.Fori(LAST_P, LAST_Q) as i:
                load_next_queries(i)


        @block.tensor
        def _(pe):
            pe.wait_ge(const_set, 2)
            pe.wait_ge(o_cleared, 1)

            def position_chunk(i, c):
                head, quarter, tile = i // 8, (i // 2) % 4, i % 2
                if c == 0:
                    pe.wait_ge(q_all_loaded, 16 * ITERS * (i // ITERS + 1))
                    pe.wait_ge(pos_loaded, 32 * (8 * (i // 8) + 1))
                wait(pe, bd_copied, CHUNKS * i + c - 2)
                window = pe.snap((head % 2) * s.PW + PARTS * tile + s.T - 1 - s.QT * quarter - CT * c - (CT - 1))
                column = pe.snap(((i // ITERS) % 2) * s.B * s.TT + ((i // 2) % 2) * s.QT + CT * c)
                for t in range(CT):
                    last = nc.tensor.matmul(
                        bd_p[c % 3][:, s.B * t:s.B * (t + 1)],
                        pos[:, bass.ds(window + (CT - 1 - t), PARTS)],
                        bass.AP(tensor=q_all[:, :].tensor, offset=column + t,
                                ap=[[2 * s.B * s.TT, CROWS], [s.TT, s.B]]),
                        start=True, stop=True)
                last.then_inc(bd_ready, 1)

            def scores(g, p):
                half = p // (NP // 2)
                if p % (NP // 2) == 0:
                    pe.wait_ge(in_loaded[half], 48 * (g + 1))
                wait(pe, exp_done, 2 * (NP * g + p - 1))
                for i in range(2):
                    b = (2 * p + i) % HALF
                    bank, c = s_p[p % 2], s.T * i
                    nc.tensor.matmul(bank[0:s.TT, c:c + s.J0], bd_in[:, half, b, 0, :], ident[:, :], start=(i == 0),
                                     stop=False, is_transpose=True, skip_group_check=True)
                    nc.tensor.matmul(bank[0:s.TT, c + s.J0:c + s.T], bd_in[0:s.J1, half, b, 1, :],
                                     ident[0:s.J1, 0:s.J1], start=False, stop=False, is_transpose=True,
                                     skip_group_check=True)
                    last = nc.tensor.matmul(bank[0:s.TT, c:c + s.T], q_in[:, half, b, :], k_in[:, half, b, :],
                                            start=False, stop=True, skip_group_check=True)
                last.then_inc(s_ready, 1)

            def turn_weights(n, p):
                pe.wait_ge(exp_done, 2 * (n + 1))
                wait(pe, e_copied, n - 1)
                for i in range(2):
                    for j in range(2):
                        c = s.T * i + s.TT * j
                        last = nc.tensor.matmul(e_p[p % 2][:, c:c + s.TT], e_sb[:, p % 2, i, PARTS * j:PARTS * (j + 1)],
                                                ident[0:s.TT, 0:s.TT], start=True, stop=True, is_transpose=True)
                last.then_inc(e_turned, 1)

            def values(n, g, p):
                half = p // (NP // 2)
                if p % (NP // 2) == 0:
                    pe.wait_ge(v_loaded[half], 16 * (g + 1))
                if p == 0:
                    wait(pe, o_copied, g)
                pe.wait_ge(e_copied, n + 2)
                for j in range(2):
                    for i in range(4):
                        c = s.T * (i % 2) + s.TT * j
                        last = nc.tensor.matmul(
                            o_p[32 * i:32 * i + s.VW, s.TT * (p // 2):s.TT * (p // 2 + 1)],
                            v_in[:, half, (2 * p + i) % HALF, j, :], e_t[:, (p + i // 2) % 4, c:c + s.TT],
                            start=(j == 0), stop=(j == 1))
                last.then_inc(o_ready, 1)

            def step(g, positions, first=False):
                for p in range(NP):
                    scores(g, p)
                    if positions:
                        for c in BESIDE[p]:
                            position_chunk(g + ITERS, c)
                    if not (first and p < 1):
                        turn_weights(NP * g + p - 1, (p - 1) % NP)
                    if p % 2 and not (first and p < 3):
                        values(NP * g + p - 3, g if p >= 3 else g - 1, (p - 3) % NP)

            for c in range(CHUNKS):
                position_chunk(0, c)
            with pe.Fori(1, ITERS) as i:
                for c in range(CHUNKS):
                    position_chunk(i, c)
            step(0, True, first=True)
            with pe.Fori(1, G - ITERS) as g:
                step(g, True)
            with pe.Fori(G - ITERS, G) as g:
                step(g, False)
            turn_weights(NP * G - 1, NP - 1)
            values(NP * G - 2, G - 1, NP - 2)

        @block.scalar
        def _(act):
            def copy_chunk(i, c, g=0):
                unit, part, tile = i // 4, (i // 2) % 2, i % 2
                if c == 0:
                    for half in range(2):
                        wait(act, in_loaded[half], 48 * ITERS * (g // ITERS))
                act.wait_ge(bd_ready, CHUNKS * i + c + 1)
                first = act.snap((unit % 2) * UROW + tile * s.TT + part * s.QT + CT * c)
                dst = bass.AP(tensor=bd_t[:, :].tensor, offset=first,
                              ap=[[2 * UROW, PARTS], [1, CT], [s.T, s.B]])
                nc.scalar.activation(dst, bd_p[c % 3][:, 0:CN].rearrange("p (t b) -> p t b", t=CT), ACT.Copy)\
                  .then_inc(bd_copied, 1)

            def exps(n, p):
                act.wait_ge(max_ready, n + 1)
                wait(act, e_turned, n - 1)
                for i in range(2):
                    nc.scalar.activation(e_sb[:, p % 2, i, 0:s.T], s_p[p % 2][0:s.TT, s.T * i:s.T * (i + 1)], ACT.Exp,
                                         bias=neg_max[:, p % 4, i:i + 1]).then_inc(exp_done, 1)

            def step(g, positions):
                for p in range(NP):
                    if positions:
                        for c in BESIDE[p]:
                            copy_chunk(g + ITERS, c, g)
                    exps(NP * g + p, p)

            for i in range(ITERS):
                for c in range(CHUNKS):
                    copy_chunk(i, c)
            step(0, True)
            with act.Fori(1, G - ITERS) as g:
                step(g, True)
            with act.Fori(G - ITERS, G) as g:
                step(g, False)

        @block.vector
        def _(dve):
            def maxima(n, p):
                dve.wait_ge(s_ready, n + 1)
                nc.vector.tensor_reduce(neg_max[:, p % 4, :],
                                        s_p[p % 2][0:s.TT, 0:2 * s.T].rearrange("p (b t) -> p b t", b=2), AX_X,
                                        ALU.max, negate=True).then_inc(max_ready, 1)

            def copy_weights(n, g, p):
                dve.wait_ge(e_turned, n + 1)
                if not (isinstance(n, int) and n < 4):
                    dve.wait_ge(o_ready, (NP // 2) * g + p // 2 - 1)
                nc.vector.tensor_copy(e_t[:, p % 4, :], e_p[p % 2][:, 0:2 * s.T]).then_inc(e_copied, 1)

            def copy_o(g):
                dve.wait_ge(o_ready, NP // 2 * (g + 1))
                wait(dve, o_stored, 16 * g)
                nc.vector.tensor_copy(o_sb[:, :, :].rearrange("p m t -> p (m t)"), o_p[:, 0:s.TT * IB // 4])\
                  .then_inc(o_copied, 1)

            def step(g, first=False):
                for p in range(NP):
                    maxima(NP * g + p, p)
                    if not (first and p < 1):
                        copy_weights(NP * g + p - 1, g if p else g - 1, (p - 1) % NP)
                    if p == 2 and not first:
                        copy_o(g - 1)

            nc.vector.memset(o_p[:, :], 0.0).then_inc(o_cleared, 1)
            step(0, first=True)
            with dve.Fori(1, G) as g:
                step(g)
            copy_weights(NP * G - 1, G - 1, NP - 1)
            copy_o(G - 1)


def finish_block(nc, s, wo, bo, ident, ones, eps, zeros, scratch, out):
    U = 4
    QUARTERS = 4
    STEPS = 2 * QUARTERS
    N = STEPS * U
    TILES = 4
    NT = TILES * s.TT
    with ExitStack() as ctx:
        sb, ps, sem = opener(nc, ctx)
        wo_sb = sb("wo_sb", [PARTS, s.D])
        bo_row = sb("bo_row", [1, TILES * s.D])
        bo_parts = sb("bo_parts", [1, 3, TILES * s.D], BF16)
        bo_stack = sb("bo_stack", [3, TILES * s.D], BF16)
        ones_bf = sb("ones_bf4", [3, PARTS], BF16)
        o_in = sb("o_in", [PARTS, U, NT])
        sums = sb("sums", [PARTS, 2 * NT])
        inverse = sb("inverse", [s.H, STEPS, U * NT])
        spread = sb("spread", [s.H, PARTS])
        h_in = sb("h_in", [s.TT, U, TILES * s.D])
        o_n = sb("o_n", [PARTS, U, NT])
        r_sb = sb("r_sb", [s.TT, U, TILES, s.D])
        z_sb = sb("z_sb", [s.TT, U, TILES, s.D])
        out_sb = sb("out_sb", [s.TT, U, TILES, s.D])
        stats = sb("stats4", [s.TT, U, TILES, 6])
        mv = sb("mv4", [s.TT, U, TILES, 2])
        std = sb("std4", [s.TT, U, TILES])
        shift = sb("shift4", [s.TT, U, TILES])
        scale = sb("scale4", [s.TT, U, TILES])
        a_p = [ps(f"a_p{i}") for i in range(U)]
        inverse_p = [ps(f"inverse_p{i}") for i in range(U)]
        w_loaded = sem("w_loaded4")
        sums_loaded = sem("sums_loaded")
        sums_inverted = sem("sums_inverted")
        inverse_placed = sem("inverse_placed")
        spread_ready = sem("spread_ready")
        setup = sem("setup4")
        bias_cut = sem("bias_cut4")
        bias_stacked = sem("bias_stacked4")
        o_loaded = [sem(f"o_loaded{u}") for u in range(U)]
        h_loaded = [sem(f"h_loaded{u}") for u in range(U)]
        inverse_ready = sem("inverse_ready")
        o_normed = sem("o_normed")
        attention_ready = sem("attention_ready")
        r_ready = sem("r_ready")
        stats_done = sem("stats_done4")
        moments_ready = sem("moments_ready4")
        std_ready = sem("std_ready4")
        scale_ready = sem("scale_ready")
        coefficients_ready = sem("coefficients_ready")
        z_ready = sem("z_ready")
        out_ready = sem("out_ready")
        out_stored = [sem(f"out_stored{u}") for u in range(U)]
        block = ctx.enter_context(nc.Block())

        @block.sync
        def _(sp):
            row = 4 * s.TT
            iteration = PARTS * row
            for half in range(2):
                sp.dma_start(sums[64 * half:64 * half + 64, :].rearrange("p (b t) -> p b t", b=2),
                             dram(scratch["o"], (64 * half + s.DK) * row, [[iteration, 64], [32 * row, 2], [1, row]]))\
                  .then_inc(sums_loaded, 16)
            sp.dma_start(bo_row[0:1, :].rearrange("p (a c) -> p a c", a=TILES),
                         dram(bo, 0, [[s.D, 1], [0, TILES], [1, s.D]])).then_inc(w_loaded, 16)
            sp.dma_start(wo_sb[:, :], wo).then_inc(w_loaded, 16)

            def load(k, u):
                n = U * k + u
                wait(sp, o_normed, n - U + 1)
                sp.dma_start(o_in[:, u, :],
                             dram(scratch["o"], k * iteration + 32 * u * row,
                                  [[STEPS * iteration, s.H], [row, s.DK], [1, row]])).then_inc(o_loaded[u], 16)
                wait(sp, r_ready, n - U + 1)
                sp.dma_start(h_in[:, u, :].rearrange("p (m c) -> p m c", m=TILES),
                             dram(scratch["h"], (k // QUARTERS * s.TT * s.B + k % QUARTERS * 16 + u) * s.D,
                                  [[s.B * s.D, s.TT], [4 * s.D, TILES], [1, s.D]])).then_inc(h_loaded[u], 16)

            def store(k, u):
                n = U * k + u
                sp.wait_ge(out_ready, n + 1)
                sp.dma_start(dram(out, ((k % QUARTERS * 16 + u) * s.T + k // QUARTERS * s.TT) * s.D,
                                  [[s.D, s.TT], [4 * s.T * s.D, TILES], [1, s.D]]),
                             out_sb[:, u, :, :]).then_inc(out_stored[u], 16)

            load(0, 0)
            load(0, 1)
            sp.wait_ge(bias_cut, 1)
            for part in range(3):
                sp.dma_start(bo_stack[part:part + 1, :], bo_parts[0:1, part, :]).then_inc(bias_stacked, 16)
            load(0, 2)
            load(0, 3)
            sp.wait_ge(sums_inverted, 1)
            for half in range(2):
                sp.dma_start(inverse[:, :, 2 * NT * half:2 * NT * half + 2 * NT],
                             sums[64 * half:64 * half + 64, :]).then_inc(inverse_placed, 16)
            with sp.Fori(1, STEPS) as k:
                for u in range(U):
                    load(k, u)
                    store(k - 1, u)
            for u in range(U):
                store(STEPS - 1, u)
            for u in range(U):
                sp.wait_ge(out_stored[u], 16 * STEPS)

        @block.gpsimd
        def _(pool):
            def add(k, u):
                n = U * k + u
                pool.wait_ge(z_ready, n + 1)
                wait(pool, out_stored[u], 16 * k)
                nc.gpsimd.tensor_tensor(out_sb[:, u, :, :], r_sb[:, u, :, :], z_sb[:, u, :, :], ALU.add)\
                  .then_inc(out_ready, 1)

            for u in range(U):
                add(0, u)
            with pool.Fori(1, STEPS) as k:
                for u in range(U):
                    add(k, u)

        @block.tensor
        def _(pe):
            pe.wait_ge(w_loaded, 32)
            pe.wait_ge(bias_stacked, 48)
            pe.wait_ge(setup, 1)
            pe.wait_ge(spread_ready, 1)
            pe.wait_ge(inverse_placed, 32)

            def spread_inverse(k, u):
                wait(pe, o_normed, U * k + u - U + 1)
                nc.tensor.matmul(inverse_p[u][:, 0:NT], spread[:, :], inverse[:, k, NT * u:NT * u + NT],
                                 start=True, stop=True).then_inc(inverse_ready, 1)

            def project(k, u):
                n = U * k + u
                pe.wait_ge(o_normed, n + 1)
                wait(pe, r_ready, n - U + 1)
                bank = a_p[u]
                nc.tensor.matmul(bank[0:s.TT, :], ones_bf[:, 0:s.TT], bo_stack[:, :], start=True, stop=False,
                                 skip_group_check=True)
                for m in range(TILES):
                    last = nc.tensor.matmul(bank[0:s.TT, s.D * m:s.D * m + s.D], o_n[:, u, s.TT * m:s.TT * m + s.TT],
                                            wo_sb[:, :], start=False, stop=True, skip_group_check=True)
                last.then_inc(attention_ready, 1)

            def step(k, last=False):
                for u in range(U):
                    if not (last and u >= U - 2):
                        spread_inverse(k if u < 2 else k + 1, (u + 2) % U)
                    project(k, u)

            spread_inverse(0, 0)
            spread_inverse(0, 1)
            step(0)
            with pe.Fori(1, STEPS - 1) as k:
                step(k)
            step(STEPS - 1, last=True)

        @block.scalar
        def _(act):
            def deviation(n, u):
                act.wait_ge(moments_ready, n + 1)
                nc.scalar.activation(std[:, u, :], mv[:, u, :, 1], ACT.Sqrt, bias=eps[0:s.TT, 0:1])\
                  .then_inc(std_ready, 1)

            def normed(n, u):
                act.wait_ge(coefficients_ready, n + 1)
                wait(act, out_ready, n - 1)
                for b in range(TILES):
                    last = nc.scalar.activation(z_sb[:, u, b, :], r_sb[:, u, b, :], ACT.Identity,
                                                bias=shift[:, u, b:b + 1], scale=scale[:, u, b:b + 1])
                last.then_inc(z_ready, 1)

            def step(k):
                for u in range(U):
                    n = U * k + u
                    deviation(n, u)
                    if not (isinstance(k, int) and u < 2):
                        normed(n - 2, (u - 2) % U)

            step(0)
            with act.Fori(1, STEPS) as k:
                step(k)
            normed(N - 2, U - 2)
            normed(N - 1, U - 1)

        @block.vector
        def _(dve):
            nc.vector.memset(ones_bf[:, :], 1.0).then_inc(setup, 1)
            nc.vector.tensor_copy(spread[:, :].rearrange("p (h v) -> p h v", h=s.H),
                                  ident[0:s.H, 0:s.H].unsqueeze(2).to_broadcast([s.H, s.H, s.DK]))\
              .then_inc(spread_ready, 1)
            dve.wait_ge(w_loaded, 32)
            nc.vector.tensor_copy(bo_parts[:, 0, :], bo_row[:, :]).then_inc(setup, 1)
            dve.wait_ge(setup, 2)
            nc.vector.tensor_tensor(bo_row[:, :], bo_row[:, :], bo_parts[:, 0, :], ALU.subtract).then_inc(setup, 1)
            dve.wait_ge(setup, 3)
            nc.vector.tensor_copy(bo_parts[:, 1, :], bo_row[:, :]).then_inc(setup, 1)
            dve.wait_ge(setup, 4)
            nc.vector.tensor_tensor(bo_parts[:, 2, :], bo_row[:, :], bo_parts[:, 1, :], ALU.subtract)\
              .then_inc(bias_cut, 1)
            dve.wait_ge(sums_loaded, 32)
            nc.vector.reciprocal(sums[:, :], sums[:, :]).then_inc(sums_inverted, 1)

            def divide(k, u):
                n = U * k + u
                dve.wait_ge(inverse_ready, n + 1)
                dve.wait_ge(o_loaded[u], 16 * (k + 1))
                wait(dve, attention_ready, n - U + 1)
                nc.vector.tensor_tensor(o_n[:, u, :], o_in[:, u, :], inverse_p[u][:, 0:NT], ALU.mult)\
                  .then_inc(o_normed, 1)

            def residual(k, u):
                n = U * k + u
                dve.wait_ge(attention_ready, n + 1)
                dve.wait_ge(h_loaded[u], 16 * (k + 1))
                wait(dve, out_ready, n - U + 1)
                nc.vector.tensor_tensor(r_sb[:, u, :, :].rearrange("p b c -> p (b c)"), a_p[u][0:s.TT, :],
                                        h_in[:, u, :], ALU.add).then_inc(r_ready, 1)
                dve.wait_ge(r_ready, n + 1)
                for b in range(TILES):
                    last = nc.vector.bn_stats(stats[:, u, b, :], r_sb[:, u, b, :])
                last.then_inc(stats_done, 1)

            def moments(u):
                for b in range(TILES):
                    last = nc.vector.bn_aggr(mv[:, u, b, :], stats[:, u, b, :])
                last.then_inc(moments_ready, 1)

            def invert(n, u):
                dve.wait_ge(std_ready, n + 1)
                nc.vector.reciprocal(scale[:, u, :], std[:, u, :]).then_inc(scale_ready, 1)

            def shift_of(n, u):
                dve.wait_ge(scale_ready, n + 1)
                nc.vector.scalar_tensor_tensor(shift[:, u, :], mv[:, u, :, 0], -1.0, scale[:, u, :], ALU.mult,
                                               ALU.mult).then_inc(coefficients_ready, 1)

            def step(k, last=False):
                for u in range(U):
                    n = U * k + u
                    if not (last and u == U - 1):
                        divide(k if u < U - 1 else k + 1, (u + 1) % U)
                    residual(k, u)
                    dve.wait_ge(stats_done, n + 1)
                    if isinstance(k, int) and n < 1:
                        moments(u)
                    else:
                        invert(n - 1, (u - 1) % U)
                        moments(u)
                        shift_of(n - 1, (u - 1) % U)

            divide(0, 0)
            step(0)
            with dve.Fori(1, STEPS - 1) as k:
                step(k)
            step(STEPS - 1, last=True)
            invert(N - 1, U - 1)
            shift_of(N - 1, U - 1)


_INS = ["x", "L0_tok_W", "L0_tok_b", "L0_tok_gamma", "L0_tok_beta", "L0_attn_pos_emb", "L0_attn_Wq", "L0_attn_bq",
        "L0_attn_Wk", "L0_attn_bk", "L0_attn_Wv", "L0_attn_bv", "L0_attn_Wp", "L0_attn_bp", "L0_attn_Wo",
        "L0_attn_bo", "L0_attn_pos_bias_u", "L0_attn_pos_bias_v"]


def kernel(**inputs):
    import numpy as _np
    import concourse.bacc as _bacc
    from concourse import mybir as _mybir
    from concourse.bass_utils import run_bass_kernel_spmd as _run

    nc = _bacc.Bacc("TRN2", target_bir_lowering=False, num_devices=1)
    arrays, args = {}, []
    for name in _INS:
        a = _np.ascontiguousarray(inputs[name])
        arrays[f"in_{name}"] = a
        args.append(nc.dram_tensor(f"in_{name}", a.shape, _mybir.dt.from_np(a.dtype), kind="ExternalInput").ap())
    batches, steps, channels = inputs["x"].shape
    frames = steps - inputs["L0_tok_W"].shape[1] // channels + 1
    out = nc.dram_tensor("out_0", (batches, frames, channels), _mybir.dt.float32, kind="ExternalOutput").ap()
    build(nc, *args, out)
    r = _run(nc, [arrays], core_ids=[0])
    return r.results[0]["out_0"]
```

```python
import concourse.bass as bass
from concourse import mybir
from concourse.alu_op_type import AluOpType as ALU
from contextlib import ExitStack

F32 = mybir.dt.float32
BF16 = mybir.dt.bfloat16
ACT = mybir.ActivationFunctionType
AX_X = mybir.AxisListType.X

PARTS = 128
QUERY_GROUPS, QUERY_SLOTS = (2, 0, 1, 0), (0, 1, 1, 2, 2, 3)
KEY_GROUPS, KEY_SLOTS = (0, 0, 1, 2), (0, 1, 2, 1, 2, 3)
GROUPS, SLOTS = len(QUERY_GROUPS), len(QUERY_SLOTS)
KEY_PART = tuple(KEY_GROUPS[g] for g in KEY_SLOTS)
EPS = 1e-5


def wait(engine, semaphore, value):
    if not (isinstance(value, int) and value <= 0):
        engine.wait_ge(semaphore, value)


def dram(ap, offset, pattern):
    return bass.AP(tensor=ap.tensor, offset=offset, ap=pattern)


class Shapes:
    def __init__(self, x, conv_w, pos_emb, pos_bias_u):
        self.B, self.S, self.D = x.shape
        self.CONTEXT = conv_w.shape[1] // self.D
        self.T = self.S - self.CONTEXT + 1
        self.P = pos_emb.shape[1]
        self.H, self.DK = pos_bias_u.shape
        self.TT = self.T // 2
        self.QT = self.T // 4
        self.J0 = PARTS
        self.J1 = self.T - PARTS
        self.PAIRS = self.B // 2
        self.ROW = self.B * self.T
        self.SCALE = float(self.DK) ** -0.5
        self.SC = 36
        self.SP = 16 * self.TT // self.SC
        self.VW = self.DK + 1
        self.PW = 512
        self.PROWS = SLOTS * self.DK + 3
        assert self.D == PARTS and self.H * self.DK == self.D and self.T == 252 and self.B == 64


def build(nc, x, tok_w, tok_b, tok_gamma, tok_beta, pos_emb, wq, bq, wk, bk, wv, bv, wp, bp, wo, bo, bias_u, bias_v,
          out):
    s = Shapes(x, tok_w, pos_emb, bias_u)
    scratch = {
        "q": nc.dram_tensor("scratch_q", [GROUPS * PARTS, s.ROW], BF16, kind="Internal").ap(),
        "k": nc.dram_tensor("scratch_k", [GROUPS * PARTS, s.ROW], BF16, kind="Internal").ap(),
        "p": nc.dram_tensor("scratch_p", [s.H * s.PROWS, s.PW], BF16, kind="Internal").ap(),
        "v": nc.dram_tensor("scratch_v", [s.H * PARTS, s.B * 2 * s.VW], F32, kind="Internal").ap(),
        "h": nc.dram_tensor("scratch_h", [2 * s.TT, s.B * s.D], F32, kind="Internal").ap(),
        "i": nc.dram_tensor("scratch_i", [3 * s.H, 2 * s.B * s.TT], BF16, kind="Internal").ap(),
        "o": nc.dram_tensor("scratch_o", [s.H * 2 * s.B // 16 * PARTS, 4 * s.TT], F32, kind="Internal").ap(),
    }
    with ExitStack() as ctx:
        ident = ctx.enter_context(nc.sbuf_tensor("ident", [PARTS, PARTS], F32))
        eps = ctx.enter_context(nc.sbuf_tensor("eps", [PARTS, 1], F32))
        zeros = ctx.enter_context(nc.sbuf_tensor("zeros", [PARTS, 1], F32))
        wo_sb = ctx.enter_context(nc.sbuf_tensor("wo_sb", [PARTS, s.D], F32))
        bias_stack = ctx.enter_context(nc.sbuf_tensor("bias_stack", [3, 2, 4 * s.D], BF16))
        ones_bf = ctx.enter_context(nc.sbuf_tensor("ones_bf", [3, PARTS], BF16))
        spread = ctx.enter_context(nc.sbuf_tensor("spread", [3 * s.H, PARTS], BF16))
        with ExitStack() as early:
            y = early.enter_context(nc.sbuf_tensor("y", [PARTS, s.ROW], F32))
            norm = early.enter_context(nc.sbuf_tensor("norm", [PARTS, 8], F32))
            w_qkv = early.enter_context(nc.sbuf_tensor("w_qkv", [PARTS, 3, s.D], F32))
            biases = early.enter_context(nc.sbuf_tensor("biases", [PARTS, 8], F32))
            conv_block(nc, s, x, tok_w, tok_b, tok_gamma, tok_beta, pos_emb, wq, bq, wk, bk, wv, bv, wp, bp, bias_u,
                       bias_v, wo, bo, w_qkv, biases, wo_sb, bias_stack, ones_bf, spread, ident, eps, zeros, y, norm,
                       scratch)
            project_block(nc, s, w_qkv, biases, bias_stack, ones_bf, ident, eps, zeros, y, norm, scratch)
        attend_block(nc, s, ident, zeros, scratch)
        finish_block(nc, s, wo_sb, bias_stack, ones_bf, spread, eps, scratch, out)


def opener(nc, ctx):
    def sb(name, shape, dt=F32):
        return ctx.enter_context(nc.sbuf_tensor(name, shape, dt))

    def ps(name, shape=(PARTS, 512), dt=F32):
        return ctx.enter_context(nc.psum_tensor(name, list(shape), dt))

    def sem(name):
        return ctx.enter_context(nc.semaphore(name))

    return sb, ps, sem


def conv_block(nc, s, x, tok_w, tok_b, tok_gamma, tok_beta, pos_emb, wq, bq, wk, bk, wv, bv, wp, bp, bias_u, bias_v,
               wo, bo, w_qkv, biases, wo_sb, bias_stack, ones_bf, spread, ident, eps, zeros, y, norm, scratch):
    U = 4
    STEPS = s.PAIRS // U
    NT = 2 * s.T
    with ExitStack() as ctx:
        sb, ps, sem = opener(nc, ctx)
        w_in = sb("w_in", [PARTS, s.CONTEXT * s.D])
        w_t = sb("w_t", [PARTS, s.CONTEXT, PARTS])
        vec = sb("vec", [PARTS, 4])
        x_in = sb("x_in", [PARTS, U, 4 * s.D])
        x_t = sb("x_t", [PARTS, 2, 2 * s.S])
        stats = sb("stats", [PARTS, s.PAIRS, 6])
        mv = sb("mv", [PARTS, 5])
        wp_sb = sb("wp_sb", [PARTS, s.D])
        bias_row = sb("bias_row", [1, 2 * 4 * s.D])
        bias_parts = sb("bias_parts", [1, 3, 2 * 4 * s.D], BF16)
        spread_part = sb("spread_part", [s.H, PARTS], BF16)
        pos_in = sb("pos_in", [PARTS, 4, s.D])
        pos_t = sb("pos_t", [PARTS, s.PW])
        pos_f = sb("pos_f", [PARTS, s.PW])
        pos_r = sb("pos_r", [PARTS, s.PW])
        pos_parts = sb("pos_parts", [PARTS, 3, s.PW], BF16)
        head_mask = sb("head_mask", [PARTS, s.H])
        vu_block = sb("vu_block", [PARTS, s.H])
        c_f = sb("c_f", [s.H, s.PW])
        c_parts = sb("c_parts", [s.H, 3, s.PW], BF16)
        x_tp = [ps(f"x_tp{i}") for i in range(2)]
        y_p = [ps(f"y_p{i}") for i in range(2)]
        w_p = [ps(f"w_p{i}") for i in range(2)]
        pos_tp = ps("pos_tp")
        pos_p = ps("pos_p")
        const_set = sem("const_set")
        weights_loaded = sem("weights_loaded")
        pos_loaded = sem("pos_loaded")
        setup = sem("setup")
        mask_set = sem("mask_set")
        pos_transposed = sem("pos_transposed")
        pos_copied = sem("pos_copied")
        pos_projected = sem("pos_projected")
        pos_biased = sem("pos_biased")
        vu_ready = sem("vu_ready")
        c_ready = sem("c_ready")
        pos_cut = sem("pos_cut")
        bias_cut = sem("bias_cut")
        bias_stacked = sem("bias_stacked")
        spread_ready = sem("spread_ready")
        spread_placed = sem("spread_placed")
        tables_stored = sem("tables_stored")
        ident_ready = sem("ident_ready")
        w_loaded = sem("w_loaded")
        vec_loaded = sem("vec_loaded")
        x_loaded = [sem(f"x_loaded{u}") for u in range(U)]
        w_transposed = sem("w_transposed")
        w_copied = sem("w_copied")
        x_transposed = sem("x_transposed")
        x_copied = sem("x_copied")
        y_ready = sem("y_ready")
        y_copied = sem("y_copied")
        stats_done = sem("stats_done")
        moments_ready = sem("moments_ready")
        std_ready = sem("std_ready")
        norm_step = sem("norm_step")
        block = ctx.enter_context(nc.Block())

        @block.sync
        def _(sp):
            sp.dma_start(w_in[:, :], tok_w).then_inc(w_loaded, 16)
            for i, v in enumerate((tok_b, tok_gamma, tok_beta)):
                sp.dma_start(vec[:, i:i + 1], v.rearrange("(p a) -> p a", a=1)).then_inc(vec_loaded, 16)

            def step(k):
                for u in range(U):
                    n = U * k + u
                    wait(sp, x_transposed, n - U + 1)
                    sp.dma_start(x_in[:, u, :].rearrange("p (a c) -> p a c", a=4),
                                 dram(x, 2 * s.S * s.D * n, [[s.D, PARTS], [PARTS * s.D, 4], [1, s.D]]))\
                      .then_inc(x_loaded[u], 16)

            step(0)
            for dst, w in ((w_qkv[:, 0, :], wq), (w_qkv[:, 1, :], wk), (w_qkv[:, 2, :], wv), (wp_sb[:, :], wp),
                           (wo_sb[:, :], wo)):
                sp.dma_start(dst, w).then_inc(weights_loaded, 16)
            for i, v in enumerate((bq, bk, bp)):
                sp.dma_start(biases[:, i:i + 1], v.rearrange("(p a) -> p a", a=1)).then_inc(weights_loaded, 16)
            for i, v in enumerate((bias_u, bias_v)):
                sp.dma_start(biases[:, 3 + i:4 + i], dram(v, 0, [[1, PARTS], [1, 1]])).then_inc(weights_loaded, 16)
            for i, v in enumerate((bv, bo)):
                sp.dma_start(bias_row[0:1, 4 * s.D * i:4 * s.D * (i + 1)].rearrange("p (a c) -> p a c", a=4),
                             dram(v, 0, [[s.D, 1], [0, 4], [1, s.D]])).then_inc(weights_loaded, 16)
            for a in range(4):
                rows = min(PARTS, s.P - PARTS * a)
                sp.dma_start(pos_in[0:rows, a, :], pos_emb[0, PARTS * a:PARTS * a + rows, :]).then_inc(pos_loaded, 16)
            step(1)
            with sp.Fori(2, STEPS) as k:
                step(k)
            sp.wait_ge(spread_ready, 1)
            sp.wait_ge(bias_cut, 1)
            for part in range(3):
                sp.dma_start(bias_stack[part:part + 1, :, :].rearrange("p a c -> p (a c)"), bias_parts[0:1, part, :])\
                  .then_inc(bias_stacked, 16)
                sp.dma_start(spread[s.H * part:s.H * (part + 1), :], spread_part[:, :]).then_inc(spread_placed, 16)
            sp.wait_ge(pos_cut, 2)
            for slot in range(SLOTS):
                sp.dma_start(dram(scratch["p"], s.PW * s.DK * slot,
                                  [[s.PW * s.PROWS, s.H], [s.PW, s.DK], [1, s.PW]]),
                             pos_parts[:, KEY_PART[slot], :]).then_inc(tables_stored, 16)
            for part in range(3):
                sp.dma_start(dram(scratch["p"], s.PW * (SLOTS * s.DK + part), [[s.PW * s.PROWS, s.H], [1, s.PW]]),
                             c_parts[:, part, :]).then_inc(tables_stored, 16)
            sp.wait_ge(bias_stacked, 48)
            sp.wait_ge(spread_placed, 48)
            sp.wait_ge(tables_stored, 16 * (SLOTS + 3))

        @block.gpsimd
        def _(pool):
            nc.gpsimd.memset(ident[:, :], 0.0).then_inc(const_set, 1)
            nc.gpsimd.memset(eps[:, :], EPS).then_inc(const_set, 1)
            nc.gpsimd.memset(zeros[:, :], 0.0).then_inc(const_set, 1)
            pool.wait_ge(const_set, 3)
            nc.gpsimd.affine_select(out=ident[:, :], in_=ident[:, :], compare_op=ALU.not_equal, fill=1.0, base=0,
                                    pattern=[[-1, PARTS]], channel_multiplier=1).then_inc(ident_ready, 1)
            pool.wait_ge(ident_ready, 1)
            nc.gpsimd.memset(head_mask[:, :], 1.0).then_inc(mask_set, 1)
            pool.wait_ge(mask_set, 1)
            nc.gpsimd.affine_select(out=head_mask[:, :], in_=head_mask[:, :], compare_op=ALU.is_ge, fill=0.0, base=0,
                                    pattern=[[-s.DK, s.H]], channel_multiplier=1).then_inc(mask_set, 1)
            pool.wait_ge(mask_set, 2)
            nc.gpsimd.affine_select(out=head_mask[:, :], in_=head_mask[:, :], compare_op=ALU.is_ge, fill=0.0,
                                    base=s.DK - 1, pattern=[[s.DK, s.H]], channel_multiplier=-1)\
              .then_inc(mask_set, 1)

        @block.tensor
        def _(pe):
            pe.wait_ge(ident_ready, 1)
            pe.wait_ge(w_loaded, 16)
            for tap in range(s.CONTEXT):
                last = nc.tensor.matmul(w_p[tap // 4][:, PARTS * (tap % 4):PARTS * (tap % 4 + 1)],
                                        w_in[:, PARTS * tap:PARTS * (tap + 1)], ident[:, :], start=True, stop=True,
                                        is_transpose=True)
                if tap == 3 or tap == s.CONTEXT - 1:
                    last.then_inc(w_transposed, 1)

            def transpose_x(u, k):
                n = U * k + u
                pe.wait_ge(x_loaded[u], 16 * (k + 1))
                wait(pe, x_copied, n - 1)
                for a in range(4):
                    last = nc.tensor.matmul(x_tp[u % 2][:, PARTS * a:PARTS * (a + 1)],
                                            x_in[:, u, PARTS * a:PARTS * (a + 1)], ident[:, :], start=True,
                                            stop=True, is_transpose=True)
                last.then_inc(x_transposed, 1)

            def convolve(u, n):
                wait(pe, x_copied, n + 1)
                wait(pe, y_copied, n - 1)
                src = x_t[:, u % 2, :].rearrange("p (b c) -> p b c", b=2)
                for tap in range(s.CONTEXT):
                    last = nc.tensor.matmul(y_p[u % 2][:, 0:NT], w_t[:, tap, :], src[:, :, tap:tap + s.T],
                                            start=(tap == 0), stop=(tap == s.CONTEXT - 1))
                last.then_inc(y_ready, 1)

            def step(k):
                for u in range(U):
                    transpose_x(u, k)
                    if not (isinstance(k, int) and k == 0 and u == 0):
                        convolve((u - 1) % U, U * k + u - 1)

            pe.wait_ge(w_copied, 2)
            step(0)
            pe.wait_ge(pos_loaded, 64)
            for a in range(4):
                rows = min(PARTS, s.P - PARTS * a)
                last = nc.tensor.matmul(pos_tp[:, PARTS * a:PARTS * a + rows], pos_in[0:rows, a, :],
                                        ident[0:rows, 0:rows], start=True, stop=True, is_transpose=True)
            last.then_inc(pos_transposed, 1)
            step(1)
            pe.wait_ge(weights_loaded, 192)
            pe.wait_ge(pos_copied, 1)
            nc.tensor.matmul(pos_p[:, 0:s.P], wp_sb[:, :], pos_t[:, 0:s.P], start=True, stop=True)\
              .then_inc(pos_projected, 1)
            step(2)
            pe.wait_ge(pos_biased, 1)
            pe.wait_ge(vu_ready, 1)
            nc.tensor.matmul(pos_tp[0:s.H, 0:s.P], vu_block[:, :], pos_f[:, 0:s.P], start=True, stop=True)\
              .then_inc(c_ready, 1)
            with pe.Fori(3, STEPS) as k:
                step(k)
            convolve(U - 1, s.PAIRS - 1)

        @block.scalar
        def _(act):
            act.wait_ge(w_transposed, 2)
            nc.scalar.activation(w_t[:, 0:4, :].rearrange("p a c -> p (a c)"), w_p[0][:, :], ACT.Copy)\
              .then_inc(w_copied, 1)
            nc.scalar.activation(w_t[:, 4, :], w_p[1][:, 0:PARTS], ACT.Copy).then_inc(w_copied, 1)
            act.wait_ge(vec_loaded, 48)

            def copy_x(u, n):
                act.wait_ge(x_transposed, n + 1)
                wait(act, y_ready, n - 1)
                nc.scalar.activation(x_t[:, u % 2, :], x_tp[u % 2][:, :], ACT.Copy).then_inc(x_copied, 1)

            def copy_y(u, n):
                act.wait_ge(y_ready, n + 1)
                nc.scalar.activation(y[:, bass.ds(NT * n, NT)], y_p[u % 2][:, 0:NT], ACT.Identity,
                                     bias=vec[:, 0:1]).then_inc(y_copied, 1)

            def step(k):
                for u in range(U):
                    copy_x(u, U * k + u)
                    if not (isinstance(k, int) and k == 0 and u == 0):
                        copy_y((u - 1) % U, U * k + u - 1)

            step(0)
            act.wait_ge(pos_transposed, 1)
            nc.scalar.activation(pos_t[:, 0:s.P], pos_tp[:, 0:s.P], ACT.Copy).then_inc(pos_copied, 1)
            step(1)
            act.wait_ge(pos_projected, 1)
            act.wait_ge(setup, 3)
            nc.scalar.activation(pos_f[:, 0:s.P], pos_p[:, 0:s.P], ACT.Identity, bias=biases[:, 2:3])\
              .then_inc(pos_biased, 1)
            with act.Fori(2, STEPS) as k:
                step(k)
            copy_y(U - 1, s.PAIRS - 1)
            act.wait_ge(moments_ready, 1)
            act.wait_ge(const_set, 3)
            nc.scalar.activation(mv[:, 2:3], mv[:, 1:2], ACT.Sqrt, bias=eps[:, 0:1]).then_inc(std_ready, 1)

        @block.vector
        def _(dve):
            dve.wait_ge(weights_loaded, 192)
            nc.vector.tensor_scalar(biases[:, 5:6], biases[:, 0:1], biases[:, 3:4], s.SCALE, ALU.add, ALU.mult)\
              .then_inc(setup, 1)
            nc.vector.tensor_scalar(biases[:, 6:7], biases[:, 4:5], biases[:, 3:4], s.SCALE, ALU.subtract, ALU.mult)\
              .then_inc(setup, 1)
            nc.vector.memset(pos_f[:, s.P:s.PW], 0.0).then_inc(setup, 1)
            dve.wait_ge(setup, 3)
            dve.wait_ge(mask_set, 3)
            nc.vector.tensor_scalar(vu_block[:, :], head_mask[:, :], biases[:, 6:7], None, ALU.mult)\
              .then_inc(vu_ready, 1)
            nc.vector.memset(c_f[:, s.P:s.PW], 0.0).then_inc(setup, 1)
            dve.wait_ge(c_ready, 1)
            nc.vector.tensor_copy(c_f[:, 0:s.P], pos_tp[0:s.H, 0:s.P]).then_inc(setup, 1)
            dve.wait_ge(setup, 5)
            nc.vector.memset(ones_bf[:, :], 1.0).then_inc(setup, 1)
            dve.wait_ge(ident_ready, 1)
            nc.vector.tensor_copy(spread_part[:, :].rearrange("p (h v) -> p h v", h=s.H),
                                  ident[0:s.H, 0:s.H].unsqueeze(2).to_broadcast([s.H, s.H, s.DK]))\
              .then_inc(spread_ready, 1)
            dve.wait_ge(setup, 6)
            done = 6
            for full, left, part, cut in ((bias_row, bias_row, bias_parts, bias_cut), (c_f, c_f, c_parts, pos_cut),
                                          (pos_f, pos_r, pos_parts, pos_cut)):
                nc.vector.tensor_copy(part[:, 0, :], full[:, :]).then_inc(setup, 1)
                dve.wait_ge(setup, done + 1)
                nc.vector.tensor_tensor(left[:, :], full[:, :], part[:, 0, :], ALU.subtract).then_inc(setup, 1)
                dve.wait_ge(setup, done + 2)
                nc.vector.tensor_copy(part[:, 1, :], left[:, :]).then_inc(setup, 1)
                dve.wait_ge(setup, done + 3)
                nc.vector.tensor_tensor(part[:, 2, :], left[:, :], part[:, 1, :], ALU.subtract).then_inc(cut, 1)
                done += 3

            with dve.Fori(0, s.PAIRS) as n:
                dve.wait_ge(y_copied, n + 1)
                nc.vector.bn_stats(stats[:, bass.ds(n, 1), :].rearrange("p a b -> p (a b)"),
                                   y[:, bass.ds(NT * n, NT)]).then_inc(stats_done, 1)
            dve.wait_ge(stats_done, s.PAIRS)
            nc.vector.bn_aggr(mv[:, 0:2], stats[:, :, :].rearrange("p a b -> p (a b)")).then_inc(moments_ready, 1)
            dve.wait_ge(std_ready, 1)
            nc.vector.reciprocal(mv[:, 4:5], mv[:, 2:3]).then_inc(norm_step, 1)
            dve.wait_ge(norm_step, 1)
            dve.wait_ge(vec_loaded, 48)
            nc.vector.tensor_tensor(norm[:, 0:1], mv[:, 4:5], vec[:, 1:2], ALU.mult).then_inc(norm_step, 1)
            dve.wait_ge(norm_step, 2)
            nc.vector.tensor_tensor(mv[:, 3:4], mv[:, 0:1], norm[:, 0:1], ALU.mult).then_inc(norm_step, 1)
            dve.wait_ge(norm_step, 3)
            nc.vector.tensor_tensor(norm[:, 1:2], vec[:, 2:3], mv[:, 3:4], ALU.subtract)


def project_block(nc, s, w_qkv, biases, bias_stack, ones_bf, ident, eps, zeros, y, norm, scratch):
    U = 4
    STEPS = s.PAIRS // U
    NT = 2 * s.T
    GB = 2 * U
    with ExitStack() as ctx:
        sb, ps, sem = opener(nc, ctx)
        h_t = sb("h_t", [PARTS, 2, NT])
        h_sb = sb("h_sb", [s.TT, U, 4, s.D])
        xn = sb("xn", [s.TT, 2, 4, s.D])
        xn_t = sb("xn_t", [PARTS, 2, NT])
        stats = sb("stats2", [s.TT, U, 4, 6])
        mv = sb("mv2", [s.TT, U, 4, 2])
        std = sb("std", [s.TT, U, 4])
        rstd = sb("rstd", [s.TT, U, 4])
        q_f = sb("q_f", [PARTS, 2, NT])
        k_f = sb("k_f", [PARTS, 2, NT])
        q_parts = sb("q_parts", [PARTS, 2, 3, 2, GB * s.TT], BF16)
        k_parts = sb("k_parts", [PARTS, 3, 2, GB * s.T], BF16)
        v_sb = sb("v_sb", [PARTS, 2, s.H, GB, 2, s.VW])
        h_p = [ps(f"h_p{i}") for i in range(2)]
        xn_p = [ps(f"xn_p{i}") for i in range(2)]
        q_p, k_p = ps("q_p"), ps("k_p")
        v_p = [ps(f"v_p{i}") for i in range(2)]
        pool_set = sem("pool_set")
        h_ready = sem("h_ready")
        h_turned = sem("h_turned")
        h_copied = sem("h_copied")
        h_stored = [sem(f"h_stored{u}") for u in range(U)]
        stats_done = sem("stats_done2")
        moments_ready = sem("moments_ready2")
        std_ready = sem("std_ready2")
        rstd_ready = sem("rstd_ready")
        xn_ready = sem("xn_ready")
        xn_turned = sem("xn_turned")
        xn_copied = sem("xn_copied")
        qk_projected = sem("qk_projected")
        v_projected = sem("v_projected")
        q_biased = sem("q_biased")
        k_biased = sem("k_biased")
        v_copied = sem("v_copied")
        q_step = sem("q_step")
        k_step = sem("k_step")
        q_stored = sem("q_stored")
        kv_stored = sem("kv_stored")
        KV_STORES = GROUPS + 1
        block = ctx.enter_context(nc.Block())

        @block.sync
        def _(sp):
            def store_h(u, k):
                n = U * k + u
                sp.wait_ge(h_copied, n + 1)
                sp.dma_start(dram(scratch["h"], 2 * s.D * n,
                                  [[s.B * s.D, s.TT], [s.TT * s.B * s.D, 2], [1, 2 * s.D]]),
                             h_sb[:, u, :, :].rearrange("p (a b) c -> p a (b c)", a=2)).then_inc(h_stored[u], 16)

            def store_group(count):
                b0, slot = GB * (count - 1), bass.ds((count - 1) % 2, 1)
                sp.wait_ge(q_step, 4 * U * count)
                wait(sp, q_stored, 16 * GROUPS * count - 16 * GROUPS)
                for group, part in enumerate(QUERY_GROUPS):
                    sp.dma_start(dram(scratch["q"], s.ROW * s.DK * group + b0 * s.T,
                                      [[s.ROW * s.DK * GROUPS, s.H], [s.ROW, s.DK], [1, GB * s.T]]),
                                 q_parts[:, slot, part, :, :].rearrange("p s a t -> p (s a t)")).then_inc(q_stored, 16)
                sp.wait_ge(k_step, 3 * U * count)
                wait(sp, kv_stored, 16 * KV_STORES * count - 16 * KV_STORES)
                for group, part in enumerate(KEY_GROUPS):
                    sp.dma_start(dram(scratch["k"], s.ROW * s.DK * group + b0 * s.T,
                                      [[s.ROW * s.DK * GROUPS, s.H], [s.ROW, s.DK], [1, GB * s.T]]),
                                 k_parts[:, part, slot, :].rearrange("p s t -> p (s t)")).then_inc(kv_stored, 16)
                sp.wait_ge(v_copied, 2 * U * count)
                sp.dma_start(dram(scratch["v"], b0 * 2 * s.VW,
                                  [[s.B * 2 * s.VW, PARTS], [PARTS * s.B * 2 * s.VW, s.H], [1, GB * 2 * s.VW]]),
                             v_sb[:, slot, :, :, :, :].rearrange("p s h b j c -> p (s h) (b j c)"))\
                  .then_inc(kv_stored, 16)

            def step(k):
                for u in range(U):
                    store_h(u, k)
                if not (isinstance(k, int) and k < 2):
                    store_group(k)

            step(0)
            step(1)
            store_group(1)
            with sp.Fori(2, STEPS) as k:
                step(k)
            store_group(STEPS)
            for u in range(U):
                sp.wait_ge(h_stored[u], 16 * STEPS)
            sp.wait_ge(q_stored, 16 * GROUPS * STEPS)
            sp.wait_ge(kv_stored, 16 * KV_STORES * STEPS)

        @block.gpsimd
        def _(pool):
            nc.gpsimd.memset(v_sb[:, :, :, :, :, :], 0.0).then_inc(pool_set, 1)
            pool.wait_ge(pool_set, 1)
            nc.gpsimd.memset(v_sb[:, :, :, :, :, s.DK:s.VW], 1.0).then_inc(pool_set, 1)
            pool.wait_ge(pool_set, 2)

            def cut_keys(u, k, slot):
                n = U * k + u
                pool.wait_ge(k_biased, n + 1)
                left, zero = k_f[:, u % 2, :], zeros[:, :].to_broadcast([PARTS, NT])
                part = [k_parts[:, j, slot, NT * u:NT * (u + 1)] for j in range(3)]
                nc.gpsimd.tensor_tensor(left, left, part[0], ALU.subtract).then_inc(k_step, 1)
                pool.wait_ge(k_step, 3 * n + 1)
                nc.gpsimd.tensor_tensor(part[1], left, zero, ALU.add).then_inc(k_step, 1)
                pool.wait_ge(k_step, 3 * n + 2)
                nc.gpsimd.tensor_tensor(part[2], left, part[1], ALU.subtract).then_inc(k_step, 1)

            for u in range(U):
                cut_keys(u, 0, 0)
            with pool.Fori(0, (STEPS - 2) // 2) as pair:
                for odd in range(2):
                    for u in range(U):
                        cut_keys(u, 2 * pair + 1 + odd, (1 + odd) % 2)
            for u in range(U):
                cut_keys(u, STEPS - 1, 1)

        @block.tensor
        def _(pe):
            def turn_h(u, n):
                pe.wait_ge(h_ready, n + 1)
                wait(pe, h_copied, n - 1)
                src = h_t[:, u % 2, :].rearrange("p (b a t) -> p a b t", b=2, a=2)
                for a in range(2):
                    for b in range(2):
                        c = PARTS * (2 * a + b)
                        last = nc.tensor.matmul(h_p[u % 2][0:s.TT, c:c + PARTS], src[:, a, b, :], ident[:, :],
                                                start=True, stop=True, is_transpose=True)
                last.then_inc(h_turned, 1)

            def turn_xn(u, n):
                pe.wait_ge(xn_ready, n + 1)
                wait(pe, xn_copied, n - 1)
                for a in range(2):
                    for b in range(2):
                        c = s.T * b + s.TT * a
                        last = nc.tensor.matmul(xn_p[u % 2][:, c:c + s.TT], xn[:, u % 2, 2 * a + b, :],
                                                ident[0:s.TT, 0:s.TT], start=True, stop=True, is_transpose=True)
                last.then_inc(xn_turned, 1)

            def project(u, n):
                pe.wait_ge(xn_copied, n + 1)
                wait(pe, q_biased, n)
                wait(pe, k_biased, n)
                nc.tensor.matmul(q_p[:, 0:NT], w_qkv[:, 0, :], xn_t[:, u % 2, :], start=True, stop=True)
                nc.tensor.matmul(k_p[:, 0:NT], w_qkv[:, 1, :], xn_t[:, u % 2, :], start=True, stop=True)\
                  .then_inc(qk_projected, 1)
                wait(pe, v_copied, 2 * (n - 1))
                bank = v_p[u % 2]
                nc.tensor.matmul(bank[:, :], ones_bf[:, :], bias_stack[:, 0, :], start=True, stop=False,
                                 skip_group_check=True)
                for b in range(2):
                    for j, keys in enumerate((s.J0, s.J1)):
                        c = PARTS * (2 * b + j)
                        lhs = xn_t[:, u % 2, s.T * b + PARTS * j:s.T * b + PARTS * j + keys]
                        last = nc.tensor.matmul(bank[0:keys, c:c + PARTS], lhs, w_qkv[:, 2, :], start=False,
                                                stop=True, skip_group_check=True)
                last.then_inc(v_projected, 1)

            def step(k):
                for u in range(U):
                    n = U * k + u
                    turn_h(u, n)
                    if not (isinstance(k, int) and n < 2):
                        turn_xn((u - 2) % U, n - 2)
                    if not (isinstance(k, int) and n < 3):
                        project((u - 3) % U, n - 3)

            step(0)
            with pe.Fori(1, STEPS) as k:
                step(k)
            turn_xn(U - 2, s.PAIRS - 2)
            project(U - 3, s.PAIRS - 3)
            turn_xn(U - 1, s.PAIRS - 1)
            project(U - 2, s.PAIRS - 2)
            project(U - 1, s.PAIRS - 1)

        @block.scalar
        def _(act):
            def make_h(u, n):
                wait(act, h_turned, n - 1)
                nc.scalar.activation(h_t[:, u % 2, :], y[:, bass.ds(NT * n, NT)], ACT.Relu, bias=norm[:, 1:2],
                                     scale=norm[:, 0:1]).then_inc(h_ready, 1)

            def copy_h(u, k):
                n = U * k + u
                act.wait_ge(h_turned, n + 1)
                wait(act, h_stored[u], 16 * k)
                wait(act, xn_ready, n - U + 1)
                nc.scalar.activation(h_sb[:, u, :, :].rearrange("p a c -> p (a c)"), h_p[u % 2][0:s.TT, :], ACT.Copy)\
                  .then_inc(h_copied, 1)

            def deviation(u, n):
                act.wait_ge(moments_ready, n + 1)
                nc.scalar.activation(std[:, u, :], mv[:, u, :, 1], ACT.Sqrt, bias=eps[0:s.TT, 0:1])\
                  .then_inc(std_ready, 1)

            def copy_xn(u, n):
                act.wait_ge(xn_turned, n + 1)
                wait(act, v_projected, n - 1)
                nc.scalar.activation(xn_t[:, u % 2, :], xn_p[u % 2][:, 0:NT], ACT.Copy).then_inc(xn_copied, 1)

            def copy_qkv(u, k, slot):
                n = U * k + u
                act.wait_ge(qk_projected, n + 1)
                wait(act, q_step, 4 * (n - 1))
                nc.scalar.activation(q_f[:, u % 2, :], q_p[:, 0:NT], ACT.Identity, bias=biases[:, 5:6], scale=s.SCALE)\
                  .then_inc(q_biased, 1)
                wait(act, k_step, 3 * (n - 1))
                if u == 0:
                    wait(act, kv_stored, 16 * KV_STORES * (k - 1))
                nc.scalar.activation(k_parts[:, 0, slot, NT * u:NT * (u + 1)], k_p[:, 0:NT], ACT.Identity,
                                     bias=biases[:, 1:2])
                nc.scalar.activation(k_f[:, u % 2, :], k_p[:, 0:NT], ACT.Identity, bias=biases[:, 1:2])\
                  .then_inc(k_biased, 1)
                act.wait_ge(v_projected, n + 1)
                if isinstance(k, int) and k == 0 and u == 0:
                    act.wait_ge(pool_set, 2)
                src = v_p[u % 2][:, :].rearrange("p (b j h d) -> p j h b d", b=2, j=2, h=s.H)
                for j, keys in enumerate((s.J0, s.J1)):
                    nc.scalar.activation(v_sb[0:keys, slot, :, 2 * u:2 * u + 2, j, 0:s.DK],
                                         src[0:keys, j, :, :, :], ACT.Copy)\
                      .then_inc(v_copied, 1)

            def step(k, slot, last=False):
                for u in range(U):
                    n = U * k + u
                    if not (last and u == U - 1):
                        make_h((u + 1) % U, n + 1)
                    copy_h(u, k)
                    if not (isinstance(k, int) and n < 1):
                        deviation((u - 1) % U, n - 1)
                    if not (isinstance(k, int) and n < 2):
                        copy_xn((u - 2) % U, n - 2)
                    if not (isinstance(k, int) and n < 3):
                        copy_qkv((u - 3) % U, k if u >= 3 else k - 1, slot if u >= 3 else 1 - slot)

            make_h(0, 0)
            for k in range(3):
                step(k, k % 2)
            with act.Fori(0, (STEPS - 4) // 2) as pair:
                for odd in range(2):
                    step(2 * pair + 3 + odd, (3 + odd) % 2)
            step(STEPS - 1, 1, last=True)
            deviation(U - 1, s.PAIRS - 1)
            copy_xn(U - 2, s.PAIRS - 2)
            copy_qkv(U - 3, STEPS - 1, 1)
            copy_xn(U - 1, s.PAIRS - 1)
            copy_qkv(U - 2, STEPS - 1, 1)
            copy_qkv(U - 1, STEPS - 1, 1)

        @block.vector
        def _(dve):
            def stats_of(u, n):
                dve.wait_ge(h_copied, n + 1)
                for a in range(4):
                    last = nc.vector.bn_stats(stats[:, u, a, :], h_sb[:, u, a, :])
                last.then_inc(stats_done, 1)

            def invert(u, n):
                dve.wait_ge(std_ready, n + 1)
                nc.vector.reciprocal(rstd[:, u, :], std[:, u, :]).then_inc(rstd_ready, 1)

            def moments(u):
                for a in range(4):
                    last = nc.vector.bn_aggr(mv[:, u, a, :], stats[:, u, a, :])
                last.then_inc(moments_ready, 1)

            def normalise(u, n):
                dve.wait_ge(rstd_ready, n + 1)
                wait(dve, xn_turned, n - 1)
                for a in range(4):
                    last = nc.vector.tensor_scalar(xn[:, u % 2, a, :], h_sb[:, u, a, :], mv[:, u, a, 0:1],
                                                   rstd[:, u, a:a + 1], ALU.subtract, ALU.mult)
                last.then_inc(xn_ready, 1)

            def cut_queries(u, k, slot):
                n = U * k + u
                dve.wait_ge(q_biased, n + 1)
                if u == 0:
                    wait(dve, q_stored, 16 * GROUPS * (k - 1))
                left = q_f[:, u % 2, :].rearrange("p (b a t) -> p b a t", b=2, a=2)
                part = [q_parts[:, slot, j, :, 2 * s.TT * u:2 * s.TT * (u + 1)].rearrange("p a (b t) -> p b a t", b=2)
                        for j in range(3)]
                nc.vector.tensor_copy(part[0], left).then_inc(q_step, 1)
                dve.wait_ge(q_step, 4 * n + 1)
                nc.vector.tensor_tensor(left, left, part[0], ALU.subtract).then_inc(q_step, 1)
                dve.wait_ge(q_step, 4 * n + 2)
                nc.vector.tensor_copy(part[1], left).then_inc(q_step, 1)
                dve.wait_ge(q_step, 4 * n + 3)
                nc.vector.tensor_tensor(part[2], left, part[1], ALU.subtract).then_inc(q_step, 1)

            def step(k, slot):
                for u in range(U):
                    n = U * k + u
                    stats_of(u, n)
                    dve.wait_ge(stats_done, n + 1)
                    if isinstance(k, int) and n < 1:
                        moments(u)
                    else:
                        invert((u - 1) % U, n - 1)
                        moments(u)
                        normalise((u - 1) % U, n - 1)
                    if not (isinstance(k, int) and n < 4):
                        cut_queries(u, k - 1, 1 - slot)

            for k in range(3):
                step(k, k % 2)
            with dve.Fori(0, (STEPS - 4) // 2) as pair:
                for odd in range(2):
                    step(2 * pair + 3 + odd, (3 + odd) % 2)
            step(STEPS - 1, 1)
            invert(U - 1, s.PAIRS - 1)
            normalise(U - 1, s.PAIRS - 1)
            for u in range(U):
                cut_queries(u, STEPS - 1, 1)


def attend_block(nc, s, ident, zeros, scratch):
    UNITS = 2 * s.H
    ITERS = 4
    G = UNITS * ITERS
    IB = s.B // ITERS
    NP = IB // 2
    HALF = IB // 2
    QUAD = IB // 4
    CT = 7
    CHUNKS = s.QT // CT
    CN = CT * s.B
    STACK = SLOTS * s.DK
    CROWS = s.PROWS
    CYCLE = 2 * ITERS
    INVERTED = G - ITERS
    SC, SP = s.SC, s.SP
    WINDOWS = 4
    WW = s.QT - 1 + PARTS
    EW = 256
    AHEAD = ITERS + 1
    HEADS = (G - 1 - AHEAD) // CYCLE
    BESIDE = (((ITERS, 6),), ((ITERS, 7), (ITERS, 8)),
              ((AHEAD, 0),), ((AHEAD, 1),), ((AHEAD, 2),), ((AHEAD, 3),), ((AHEAD, 4),), ((AHEAD, 5),))
    BEFORE = 6
    EARLY = ITERS * CHUNKS + BEFORE
    assert CHUNKS == 9 and NP == len(BESIDE)
    with ExitStack() as ctx:
        sb, ps, sem = opener(nc, ctx)
        pos = sb("pos", [CROWS, WINDOWS, WW], BF16)
        q_all = sb("q_all", [CROWS, 2, s.B, s.TT], BF16)
        bd_t = sb("bd_t", [PARTS, 2, s.B, 2, s.TT])
        bd_in = sb("bd_in", [PARTS, 4, QUAD, 2, s.TT])
        ones_row = sb("ones_row", [3, s.T], BF16)
        q_in = sb("q_in", [STACK, 2, HALF, s.TT], BF16)
        k_in = sb("k_in", [STACK, 2, HALF, s.T], BF16)
        v_in = sb("v_in", [PARTS, 2, HALF, 2, s.VW])
        neg_max = sb("neg_max", [s.TT, 4, 2])
        e_sb = sb("e_sb", [s.TT, 2, 2, EW])
        e_t = sb("e_t", [PARTS, 4, 2 * s.T])
        o_sb = sb("o_sb", [PARTS, IB // 4, s.TT])
        sums = sb("sums3", [SP, SC])
        inverse = sb("inverse3", [SP, SC])
        inverse_parts = sb("inverse_parts3", [SP, 3, SC], BF16)
        bd_p = [ps(f"bd_p{i}") for i in range(3)]
        s_p = [ps(f"s_p{i}") for i in range(2)]
        e_p = [ps(f"e_p{i}") for i in range(2)]
        o_p = ps("o_p")
        const_set = sem("const_set3")
        ones_set = sem("ones_set")
        ones_placed = sem("ones_placed")
        first_pos_loaded = sem("first_pos_loaded")
        pos_loaded = sem("pos_loaded3")
        first_queries_loaded = [sem(f"first_queries_loaded{i}") for i in range(2)]
        q_all_loaded = sem("q_all_loaded")
        bd_ready = sem("bd_ready")
        bd_copied = sem("bd_copied")
        bd_copied_dve = sem("bd_copied_dve")
        bd_loaded = [sem(f"bd_loaded{i}") for i in range(4)]
        qk_loaded = [sem(f"qk_loaded{i}") for i in range(2)]
        v_loaded = [sem(f"v_loaded{i}") for i in range(2)]
        s_ready = sem("s_ready")
        max_ready = sem("max_ready")
        exp_done = sem("exp_done")
        e_turned = sem("e_turned")
        e_copied = sem("e_copied")
        o_ready = sem("o_ready")
        o_cleared = sem("o_cleared")
        o_copied = sem("o_copied")
        o_stored = sem("o_stored")
        sums_loaded = sem("sums_loaded3")
        inverse_ready = sem("inverse_ready3")
        inverse_step = sem("inverse_step3")
        inverse_stored = sem("inverse_stored3")

        def wait_copied(engine, q):
            if isinstance(q, int) and q < EARLY:
                engine.wait_ge((bd_copied, bd_copied_dve)[q % 2], q // 2 + 1)
            else:
                engine.wait_ge(bd_copied, q + 1 - EARLY // 2)

        def chunk_place(j, c):
            first = (j // 2) % 2 * s.QT + CT * c
            return bd_t[:, j // ITERS, :, j % 2, first:first + CT].rearrange("p b t -> p t b")

        def chunk_made(c):
            return bd_p[c % 3][:, 0:CN].rearrange("p (t b) -> p t b", t=CT)

        def window_rows(i):
            head, quarter, tile = i // CYCLE, (i // 2) % 4, i % 2
            first = PARTS * tile + s.T - s.QT - s.QT * quarter
            return dram(scratch["p"], head * CROWS * s.PW + first, [[s.PW, CROWS], [1, WW]])

        def query_rows(head, tile, b0):
            group = s.DK * s.ROW
            return dram(scratch["q"], head * GROUPS * group + b0 * s.T + tile * HALF * s.TT,
                        [[group, 3], [s.ROW, 2 * s.DK], [1, HALF * s.TT]])

        def key_rows(head, first, columns):
            group = s.DK * s.ROW
            return dram(scratch["k"], head * GROUPS * group + first, [[group, 2], [s.ROW, 3 * s.DK], [1, columns]])

        block = ctx.enter_context(nc.Block())

        @block.sync
        def _(sp):
            def load_position_scores(g, quarter):
                unit, b0 = g // ITERS, (g % ITERS) * IB + quarter * QUAD
                wait(sp, s_ready, NP * (g - 1) + NP // 4 * (quarter + 1))
                if quarter == 0:
                    wait_copied(sp, CHUNKS * ITERS * (unit + 1) - 1)
                sp.dma_start(bd_in[:, quarter, :, :, :].rearrange("p b j t -> p (b j t)"),
                             bd_t[:, bass.ds(unit % 2, 1), bass.ds(b0, QUAD), :, :]
                             .rearrange("p a b j t -> p (a b j t)"))\
                  .then_inc(bd_loaded[quarter], 16)

            def load_queries_keys(g, half):
                unit, head = g // ITERS, g // (2 * ITERS)
                b0 = (g % ITERS) * IB + half * HALF
                wait(sp, s_ready, NP * (g - 1) + NP // 2 * (half + 1))
                sp.dma_start(q_in[:, half, :, :].rearrange("p b t -> p (b t)"),
                             query_rows(head, unit % 2, b0))\
                  .then_inc(qk_loaded[half], 16)
                sp.dma_start(k_in[:, half, :, :].rearrange("p b t -> p (b t)"),
                             key_rows(head, b0 * s.T, HALF * s.T))\
                  .then_inc(qk_loaded[half], 16)

            def load_values(g, half):
                head = g // (2 * ITERS)
                b0 = (g % ITERS) * IB + half * HALF
                wait(sp, o_ready, NP // 2 * (g - 1) + NP // 4 * (half + 1))
                sp.dma_start(v_in[:, half, :, :, :].rearrange("p b j c -> p (b j c)"),
                             dram(scratch["v"], head * PARTS * s.B * 2 * s.VW + b0 * 2 * s.VW,
                                  [[s.B * 2 * s.VW, PARTS], [1, HALF * 2 * s.VW]])).then_inc(v_loaded[half], 16)

            def store_o(g):
                sp.wait_ge(o_copied, g + 1)
                row = IB // 4 * s.TT
                sp.dma_start(dram(scratch["o"], g * PARTS * row, [[row, PARTS], [1, row]]),
                             o_sb[:, :, :].rearrange("p m t -> p (m t)")).then_inc(o_stored, 16)

            def load_first_queries(unit):
                for b0 in range(0, s.B, HALF):
                    sp.dma_start(q_all[0:STACK, unit, b0:b0 + HALF, :].rearrange("p b t -> p (b t)"),
                                 query_rows(0, unit, b0)).then_inc(first_queries_loaded[unit], 16)

            load_first_queries(0)
            for i in range(WINDOWS):
                sp.dma_start(pos[:, i, :], window_rows(i)).then_inc(first_pos_loaded, 16)
            sp.wait_ge(ones_placed, 32)
            load_first_queries(1)
            for half in range(2):
                load_queries_keys(0, half)
                load_values(0, half)
            wait_copied(sp, CHUNKS * ITERS - 2)
            for quarter in range(4):
                load_position_scores(0, quarter)
            wait_copied(sp, EARLY - 1)
            wait_copied(sp, EARLY - 2)

            def step(g, first=False, last=False):
                if not last:
                    load_position_scores(g + 1, 0)
                if not first:
                    load_values(g, 1)
                    store_o(g - 1)
                if not last:
                    load_position_scores(g + 1, 1)
                    load_queries_keys(g + 1, 0)
                    load_position_scores(g + 1, 2)
                    load_values(g + 1, 0)
                    load_position_scores(g + 1, 3)
                    load_queries_keys(g + 1, 1)

            step(0, first=True)
            with sp.Fori(1, G - 1) as g:
                step(g)
            step(G - 1, last=True)
            store_o(G - 1)
            sp.wait_ge(o_stored, 16 * G)

        @block.gpsimd
        def _(pool):
            def load_positions(i):
                wait(pool, pos_loaded, 16 * (i - WINDOWS))
                wait(pool, bd_ready, CHUNKS * (i - WINDOWS + 1))
                pool.dma_start(pos[:, bass.ds(i % WINDOWS, 1), :].rearrange("p a c -> p (a c)"), window_rows(i))\
                  .then_inc(pos_loaded, 16)

            def load_queries(i):
                wait(pool, q_all_loaded, 32 * (i - ITERS))
                wait(pool, bd_ready, CHUNKS * ITERS * (i // ITERS))
                unit = i // ITERS + 1
                for half in range(2):
                    b0 = (i % ITERS) * IB + half * HALF
                    pool.dma_start(q_all[0:STACK, bass.ds(unit % 2, 1), bass.ds(b0, HALF), :]
                                   .rearrange("p a b t -> p (a b t)"), query_rows(unit // 2, unit % 2, b0))\
                      .then_inc(q_all_loaded, 16)

            for i in range(ITERS):
                load_positions(i + WINDOWS)
            def load_sums(g):
                pool.wait_ge(o_stored, 16 * (g + 1))
                wait(pool, inverse_ready, g)
                row = IB // 4 * s.TT
                pool.dma_start(sums[:, :], dram(scratch["o"], (g * PARTS + s.DK) * row,
                                                [[32 * row, 4], [SC, SP // 4], [1, SC]])).then_inc(sums_loaded, 16)

            def cut_inverse(g):
                pool.wait_ge(inverse_ready, g + 1)
                wait(pool, inverse_stored, 16 * g)
                zero = zeros[0:SP, :].to_broadcast([SP, SC])
                nc.gpsimd.tensor_tensor(inverse_parts[:, 0, :], inverse[:, :], zero, ALU.add).then_inc(inverse_step, 1)
                pool.wait_ge(inverse_step, 4 * g + 1)
                nc.gpsimd.tensor_tensor(inverse[:, :], inverse[:, :], inverse_parts[:, 0, :], ALU.subtract)\
                  .then_inc(inverse_step, 1)
                pool.wait_ge(inverse_step, 4 * g + 2)
                nc.gpsimd.tensor_tensor(inverse_parts[:, 1, :], inverse[:, :], zero, ALU.add).then_inc(inverse_step, 1)
                pool.wait_ge(inverse_step, 4 * g + 3)
                nc.gpsimd.tensor_tensor(inverse_parts[:, 2, :], inverse[:, :], inverse_parts[:, 1, :], ALU.subtract)\
                  .then_inc(inverse_step, 1)
                pool.wait_ge(inverse_step, 4 * g + 4)
                pool.dma_start(dram(scratch["i"], g * SP * SC, [[SC, SP], [G * SP * SC, 3], [1, SC]]),
                               inverse_parts[:, :, :]).then_inc(inverse_stored, 16)

            def step(i):
                load_queries(i)
                load_positions(i + WINDOWS)
                if not (isinstance(i, int) and i < BEHIND + 1):
                    cut_inverse(i - BEHIND - 1)
                if not (isinstance(i, int) and i < BEHIND):
                    load_sums(i - BEHIND)

            BEHIND = ITERS + 3
            for i in range(ITERS, BEHIND + 2):
                step(i)
            with pool.Fori(BEHIND + 2, G - ITERS) as i:
                step(i)
            with pool.Fori(G - ITERS - BEHIND, INVERTED) as g:
                cut_inverse(g - 1)
                load_sums(g)
            cut_inverse(INVERTED - 1)
            pool.wait_ge(inverse_stored, 16 * INVERTED)

        @block.tensor
        def _(pe):
            pe.wait_ge(ones_placed, 32)
            pe.wait_ge(o_cleared, 1)

            def position_chunk(i, j, c):
                if c == 0:
                    wait(pe, q_all_loaded, 32 * (i - j % ITERS - ITERS))
                    wait(pe, pos_loaded, 16 * (i + 1 - WINDOWS))
                q = CHUNKS * i + c - 3
                if not (isinstance(q, int) and q < 0):
                    wait_copied(pe, q)
                unit, part = j // ITERS, (j // 2) % 2
                for t in range(CT):
                    query = CT * c + t
                    window = s.QT - 1 - query
                    last = nc.tensor.matmul(bd_p[c % 3][:, s.B * t:s.B * (t + 1)],
                                            pos[:, j % WINDOWS, window:window + PARTS],
                                            q_all[:, unit, :, part * s.QT + query], start=True, stop=True)
                last.then_inc(bd_ready, 1)

            def scores(g, p):
                half, quarter = p // (NP // 2), p // (NP // 4)
                if p % (NP // 2) == 0:
                    pe.wait_ge(qk_loaded[half], 32 * (g + 1))
                if p % (NP // 4) == 0:
                    pe.wait_ge(bd_loaded[quarter], 16 * (g + 1))
                wait(pe, exp_done, 2 * (NP * g + p - 1))
                for i in range(2):
                    b, b4 = (2 * p + i) % HALF, (2 * p + i) % QUAD
                    bank, c = s_p[p % 2], s.T * i
                    nc.tensor.matmul(bank[0:s.TT, c:c + s.J0], bd_in[:, quarter, b4, 0, :], ident[:, :], start=(i == 0),
                                     stop=False, is_transpose=True, skip_group_check=True)
                    nc.tensor.matmul(bank[0:s.TT, c + s.J0:c + s.T], bd_in[0:s.J1, quarter, b4, 1, :],
                                     ident[0:s.J1, 0:s.J1], start=False, stop=False, is_transpose=True,
                                     skip_group_check=True)
                    last = nc.tensor.matmul(bank[0:s.TT, c:c + s.T], q_in[:, half, b, :], k_in[:, half, b, :],
                                            start=False, stop=True, skip_group_check=True)
                last.then_inc(s_ready, 1)

            def turn_weights(n, p):
                pe.wait_ge(exp_done, 2 * (n + 1))
                wait(pe, e_copied, n - 1)
                for i in range(2):
                    for j in range(2):
                        c = s.T * i + s.TT * j
                        last = nc.tensor.matmul(e_p[p % 2][:, c:c + s.TT], e_sb[:, p % 2, i, PARTS * j:PARTS * (j + 1)],
                                                ident[0:s.TT, 0:s.TT], start=True, stop=True, is_transpose=True)
                last.then_inc(e_turned, 1)

            def values(n, g, p, j):
                half = p // (NP // 2)
                if j == 0:
                    if p % (NP // 2) == 0:
                        pe.wait_ge(v_loaded[half], 16 * (g + 1))
                    if p == 0:
                        wait(pe, o_copied, g)
                    pe.wait_ge(e_copied, n + 2)
                for i in range(4):
                    c = s.T * (i % 2) + s.TT * j
                    last = nc.tensor.matmul(
                        o_p[32 * i:32 * i + s.VW, s.TT * (p // 2):s.TT * (p // 2 + 1)],
                        v_in[:, half, (2 * p + i) % HALF, j, :], e_t[:, (p + i // 2) % 4, c:c + s.TT],
                        start=(j == 0), stop=(j == 1))
                if j == 1:
                    last.then_inc(o_ready, 1)

            def step(g, j, more, first=False):
                for p in range(NP):
                    scores(g, p)
                    for ahead, c in BESIDE[p]:
                        if ahead <= more:
                            position_chunk(g + ahead, (j + ahead) % CYCLE, c)
                    if p % 2 == 0 and not (first and p < 4):
                        values(NP * g + p - 4, g if p >= 4 else g - 1, (p - 4) % NP, 1)
                    if not (first and p < 1):
                        turn_weights(NP * g + p - 1, (p - 1) % NP)
                    if p % 2 and not (first and p < 3):
                        values(NP * g + p - 3, g if p >= 3 else g - 1, (p - 3) % NP, 0)

            pe.wait_ge(first_queries_loaded[0], 16 * s.B // HALF)
            pe.wait_ge(first_pos_loaded, 16 * WINDOWS)
            for i in range(ITERS):
                for c in range(CHUNKS):
                    position_chunk(i, i, c)
            pe.wait_ge(const_set, 1)
            pe.wait_ge(first_queries_loaded[1], 16 * s.B // HALF)
            for c in range(BEFORE):
                position_chunk(ITERS, ITERS, c)
            step(0, 0, AHEAD, first=True)
            with pe.Fori(0, HEADS) as head:
                for j in range(CYCLE):
                    step(head * CYCLE + 1 + j, (1 + j) % CYCLE, AHEAD)
            for g in range(HEADS * CYCLE + 1, G - ITERS):
                step(g, g % CYCLE, min(AHEAD, G - 1 - g))
            with pe.Fori(G - ITERS, G) as g:
                step(g, 0, 0)
            turn_weights(NP * G - 1, NP - 1)
            values(NP * G - 4, G - 1, NP - 4, 1)
            values(NP * G - 2, G - 1, NP - 2, 0)
            values(NP * G - 2, G - 1, NP - 2, 1)

        @block.scalar
        def _(act):
            def copy_chunk(i, j, c, g):
                if c == 0:
                    for quarter in range(4):
                        act.wait_ge(bd_loaded[quarter], 16 * (g + 1))
                act.wait_ge(bd_ready, CHUNKS * i + c + 1)
                nc.scalar.activation(chunk_place(j, c), chunk_made(c), ACT.Copy).then_inc(bd_copied, 1)

            def exps(n, p):
                act.wait_ge(max_ready, n + 1)
                wait(act, e_turned, n - 1)
                for i in range(2):
                    nc.scalar.activation(e_sb[:, p % 2, i, 0:s.T], s_p[p % 2][0:s.TT, s.T * i:s.T * (i + 1)], ACT.Exp,
                                         bias=neg_max[:, p % 4, i:i + 1]).then_inc(exp_done, 1)

            def step(g, j, more):
                for p in range(NP):
                    for ahead, c in BESIDE[p]:
                        if ahead <= more:
                            copy_chunk(g + ahead, (j + ahead) % CYCLE, c, g)
                    exps(NP * g + p, p)

            act.wait_ge(ones_set, 1)
            for unit in range(2):
                act.dma_start(q_all[STACK:CROWS, unit, :, :].rearrange("p (c b) t -> p c (b t)", b=2),
                              ones_row[:, :].unsqueeze(1).to_broadcast([3, s.B // 2, s.T])).then_inc(ones_placed, 16)
            for q in range(0, EARLY, 2):
                act.wait_ge(bd_ready, q + 1)
                nc.scalar.activation(chunk_place(q // CHUNKS, q % CHUNKS), chunk_made(q % CHUNKS), ACT.Copy)\
                  .then_inc(bd_copied, 1)
            step(0, 0, AHEAD)
            with act.Fori(0, HEADS) as head:
                for j in range(CYCLE):
                    step(head * CYCLE + 1 + j, (1 + j) % CYCLE, AHEAD)
            for g in range(HEADS * CYCLE + 1, G - ITERS):
                step(g, g % CYCLE, min(AHEAD, G - 1 - g))
            with act.Fori(G - ITERS, G) as g:
                step(g, 0, 0)

        @block.vector
        def _(dve):
            def maxima(n, p):
                dve.wait_ge(s_ready, n + 1)
                nc.vector.tensor_reduce(neg_max[:, p % 4, :],
                                        s_p[p % 2][0:s.TT, 0:2 * s.T].rearrange("p (b t) -> p b t", b=2), AX_X,
                                        ALU.max, negate=True).then_inc(max_ready, 1)

            def copy_weights(n, g, p):
                dve.wait_ge(e_turned, n + 1)
                if not (isinstance(n, int) and n < 4):
                    dve.wait_ge(o_ready, (NP // 2) * g + p // 2 - 1)
                nc.vector.tensor_copy(e_t[:, p % 4, :], e_p[p % 2][:, 0:2 * s.T]).then_inc(e_copied, 1)

            def copy_o(g):
                dve.wait_ge(o_ready, NP // 2 * (g + 1))
                wait(dve, o_stored, 16 * g)
                nc.vector.tensor_copy(o_sb[:, :, :].rearrange("p m t -> p (m t)"), o_p[:, 0:s.TT * IB // 4])\
                  .then_inc(o_copied, 1)

            def invert_sums(g):
                dve.wait_ge(sums_loaded, 16 * (g + 1))
                wait(dve, inverse_step, 4 * g)
                nc.vector.reciprocal(inverse[:, :], sums[:, :]).then_inc(inverse_ready, 1)

            def step(g, first=False, sums=True):
                for p in range(NP):
                    if p == NP - 2 and sums and not (isinstance(g, int) and g < 3):
                        invert_sums(g - 3)
                    maxima(NP * g + p, p)
                    if p == 2 and not first:
                        copy_o(g - 1)
                    if not (first and p < 1):
                        copy_weights(NP * g + p - 1, g if p else g - 1, (p - 1) % NP)

            nc.vector.memset(ones_row[:, :], 1.0).then_inc(ones_set, 1)
            nc.vector.memset(e_sb[:, :, :, s.T:EW], 0.0).then_inc(const_set, 1)
            nc.vector.memset(o_p[:, :], 0.0).then_inc(o_cleared, 1)
            for q in range(1, EARLY, 2):
                dve.wait_ge(bd_ready, q + 1)
                nc.vector.tensor_copy(chunk_place(q // CHUNKS, q % CHUNKS), chunk_made(q % CHUNKS))\
                  .then_inc(bd_copied_dve, 1)
            step(0, first=True)
            for g in range(1, 4):
                step(g)
            with dve.Fori(4, INVERTED + 3) as g:
                step(g)
            for g in range(INVERTED + 3, G):
                step(g, sums=False)
            copy_weights(NP * G - 1, G - 1, NP - 1)
            copy_o(G - 1)


def finish_block(nc, s, wo_sb, bias_stack, ones_bf, spread, eps, scratch, out):
    U = 4
    QUARTERS = 4
    STEPS = 2 * QUARTERS
    N = STEPS * U
    TILES = 4
    NT = TILES * s.TT
    with ExitStack() as ctx:
        sb, ps, sem = opener(nc, ctx)
        o_in = sb("o_in", [PARTS, U, NT])
        inverse = sb("inverse", [3 * s.H, STEPS, U * NT], BF16)
        sums = sb("sums", [s.SP, QUARTERS, s.SC])
        inverse_parts = sb("inverse_parts", [s.SP, 3, QUARTERS, s.SC], BF16)
        h_in = sb("h_in", [s.TT, U, TILES * s.D])
        o_n = sb("o_n", [PARTS, U, NT])
        r_sb = sb("r_sb", [s.TT, U, TILES, s.D])
        z_sb = sb("z_sb", [s.TT, U, TILES, s.D])
        out_sb = sb("out_sb", [s.TT, U, TILES, s.D])
        stats = sb("stats4", [s.TT, U, TILES, 6])
        mv = sb("mv4", [s.TT, U, TILES, 2])
        std = sb("std4", [s.TT, U, TILES])
        shift = sb("shift4", [s.TT, U, TILES])
        scale = sb("scale4", [s.TT, U, TILES])
        a_p = [ps(f"a_p{i}") for i in range(U)]
        inverse_p = [ps(f"inverse_p{i}") for i in range(U)]
        inverse_loaded = [sem(f"inverse_loaded{i}") for i in range(2)]
        sums_loaded = sem("sums_loaded")
        sums_step = sem("sums_step")
        inverse_stored = sem("inverse_stored")
        o_loaded = [sem(f"o_loaded{u}") for u in range(U)]
        h_loaded = [sem(f"h_loaded{u}") for u in range(U)]
        inverse_ready = sem("inverse_ready")
        o_normed = sem("o_normed")
        attention_ready = sem("attention_ready")
        r_ready = sem("r_ready")
        stats_done = sem("stats_done4")
        moments_ready = sem("moments_ready4")
        std_ready = sem("std_ready4")
        scale_ready = sem("scale_ready")
        coefficients_ready = sem("coefficients_ready")
        z_ready = sem("z_ready")
        out_ready = sem("out_ready")
        out_stored = [sem(f"out_stored{u}") for u in range(U)]

        def inverse_rows(k):
            return dram(scratch["i"], k * U * NT, [[STEPS * U * NT, 3 * s.H], [1, QUARTERS * U * NT]])

        block = ctx.enter_context(nc.Block())

        @block.sync
        def _(sp):
            row = 4 * s.TT
            iteration = PARTS * row
            sp.dma_start(inverse[:, 0:QUARTERS, :], inverse_rows(0)).then_inc(inverse_loaded[0], 16)

            def load(k, u):
                n = U * k + u
                wait(sp, o_normed, n - U + 1)
                sp.dma_start(o_in[:, u, :],
                             dram(scratch["o"], k * iteration + 32 * u * row,
                                  [[STEPS * iteration, s.H], [row, s.DK], [1, row]])).then_inc(o_loaded[u], 16)
                wait(sp, r_ready, n - U + 1)
                sp.dma_start(h_in[:, u, :].rearrange("p (m c) -> p m c", m=TILES),
                             dram(scratch["h"], (k // QUARTERS * s.TT * s.B + k % QUARTERS * 16 + u) * s.D,
                                  [[s.B * s.D, s.TT], [4 * s.D, TILES], [1, s.D]])).then_inc(h_loaded[u], 16)

            load(0, 0)
            load(0, 1)
            for q in range(QUARTERS):
                g = s.H * STEPS - QUARTERS + q
                sp.dma_start(sums[:, q, :], dram(scratch["o"], g * iteration + s.DK * row,
                                                 [[32 * row, 4], [s.SC, s.SP // 4], [1, s.SC]]))\
                  .then_inc(sums_loaded, 16)
            load(0, 2)
            load(0, 3)
            with sp.Fori(1, STEPS) as k:
                for u in range(U):
                    load(k, u)

        @block.gpsimd
        def _(pool):
            def add(k, u):
                n = U * k + u
                pool.wait_ge(z_ready, n + 1)
                wait(pool, out_stored[u], 16 * k)
                nc.gpsimd.tensor_tensor(out_sb[:, u, :, :], r_sb[:, u, :, :], z_sb[:, u, :, :], ALU.add)\
                  .then_inc(out_ready, 1)

            pool.wait_ge(sums_step, 5)
            for part in range(3):
                pool.dma_start(dram(scratch["i"], (part * s.H * STEPS + s.H * STEPS - QUARTERS) * U * NT,
                                    [[s.SC, s.SP], [U * NT, QUARTERS], [1, s.SC]]),
                               inverse_parts[:, part, :, :]).then_inc(inverse_stored, 16)
            pool.wait_ge(inverse_stored, 48)
            pool.dma_start(inverse[:, QUARTERS:STEPS, :], inverse_rows(QUARTERS)).then_inc(inverse_loaded[1], 16)
            for u in range(U):
                add(0, u)
            with pool.Fori(1, STEPS) as k:
                for u in range(U):
                    add(k, u)

        @block.tensor
        def _(pe):
            pe.wait_ge(inverse_loaded[0], 16)

            def spread_inverse(k, u):
                wait(pe, o_normed, U * k + u - U + 1)
                nc.tensor.matmul(inverse_p[u][:, 0:NT], spread[:, :], inverse[:, k, NT * u:NT * u + NT],
                                 start=True, stop=True).then_inc(inverse_ready, 1)

            def project(k, u):
                n = U * k + u
                pe.wait_ge(o_normed, n + 1)
                wait(pe, r_ready, n - U + 1)
                bank = a_p[u]
                nc.tensor.matmul(bank[0:s.TT, :], ones_bf[:, 0:s.TT], bias_stack[:, 1, :], start=True, stop=False,
                                 skip_group_check=True)
                for m in range(TILES):
                    last = nc.tensor.matmul(bank[0:s.TT, s.D * m:s.D * m + s.D], o_n[:, u, s.TT * m:s.TT * m + s.TT],
                                            wo_sb[:, :], start=False, stop=True, skip_group_check=True)
                last.then_inc(attention_ready, 1)

            def step(k, last=False):
                for u in range(U):
                    if not (last and u >= U - 2):
                        spread_inverse(k if u < 2 else k + 1, (u + 2) % U)
                    project(k, u)

            spread_inverse(0, 0)
            spread_inverse(0, 1)
            step(0)
            with pe.Fori(1, QUARTERS - 1) as k:
                step(k)
            pe.wait_ge(inverse_loaded[1], 16)
            with pe.Fori(QUARTERS - 1, STEPS - 1) as k:
                step(k)
            step(STEPS - 1, last=True)

        @block.scalar
        def _(act):
            def deviation(n, u):
                act.wait_ge(moments_ready, n + 1)
                nc.scalar.activation(std[:, u, :], mv[:, u, :, 1], ACT.Sqrt, bias=eps[0:s.TT, 0:1])\
                  .then_inc(std_ready, 1)

            def normed(n, u):
                act.wait_ge(coefficients_ready, n + 1)
                wait(act, out_ready, n - 1)
                for b in range(TILES):
                    last = nc.scalar.activation(z_sb[:, u, b, :], r_sb[:, u, b, :], ACT.Identity,
                                                bias=shift[:, u, b:b + 1], scale=scale[:, u, b:b + 1])
                last.then_inc(z_ready, 1)

            def store(k, u):
                n = U * k + u
                act.wait_ge(out_ready, n + 1)
                act.dma_start(dram(out, ((k % QUARTERS * 16 + u) * s.T + k // QUARTERS * s.TT) * s.D,
                                  [[s.D, s.TT], [4 * s.T * s.D, TILES], [1, s.D]]),
                             out_sb[:, u, :, :]).then_inc(out_stored[u], 16)

            def step(k):
                for u in range(U):
                    n = U * k + u
                    deviation(n, u)
                    if not (isinstance(k, int) and u < 2):
                        normed(n - 2, (u - 2) % U)
                    if not (isinstance(k, int) and u < 3):
                        store(k if u >= 3 else k - 1, (u - 3) % U)

            step(0)
            with act.Fori(1, STEPS) as k:
                step(k)
            store(STEPS - 1, U - 3)
            normed(N - 2, U - 2)
            store(STEPS - 1, U - 2)
            normed(N - 1, U - 1)
            store(STEPS - 1, U - 1)
            for u in range(U):
                act.wait_ge(out_stored[u], 16 * STEPS)

        @block.vector
        def _(dve):
            def divide(k, u):
                n = U * k + u
                dve.wait_ge(inverse_ready, n + 1)
                dve.wait_ge(o_loaded[u], 16 * (k + 1))
                wait(dve, attention_ready, n - U + 1)
                nc.vector.tensor_tensor(o_n[:, u, :], o_in[:, u, :], inverse_p[u][:, 0:NT], ALU.mult)\
                  .then_inc(o_normed, 1)

            def residual(k, u):
                n = U * k + u
                dve.wait_ge(attention_ready, n + 1)
                dve.wait_ge(h_loaded[u], 16 * (k + 1))
                wait(dve, out_ready, n - U + 1)
                nc.vector.tensor_tensor(r_sb[:, u, :, :].rearrange("p b c -> p (b c)"), a_p[u][0:s.TT, :],
                                        h_in[:, u, :], ALU.add).then_inc(r_ready, 1)
                dve.wait_ge(r_ready, n + 1)
                for b in range(TILES):
                    last = nc.vector.bn_stats(stats[:, u, b, :], r_sb[:, u, b, :])
                last.then_inc(stats_done, 1)

            def moments(u):
                for b in range(TILES):
                    last = nc.vector.bn_aggr(mv[:, u, b, :], stats[:, u, b, :])
                last.then_inc(moments_ready, 1)

            def invert(n, u):
                dve.wait_ge(std_ready, n + 1)
                nc.vector.reciprocal(scale[:, u, :], std[:, u, :]).then_inc(scale_ready, 1)

            def shift_of(n, u):
                dve.wait_ge(scale_ready, n + 1)
                nc.vector.scalar_tensor_tensor(shift[:, u, :], mv[:, u, :, 0], -1.0, scale[:, u, :], ALU.mult,
                                               ALU.mult).then_inc(coefficients_ready, 1)

            def step(k, last=False):
                for u in range(U):
                    n = U * k + u
                    if not (last and u == U - 1):
                        divide(k if u < U - 1 else k + 1, (u + 1) % U)
                    residual(k, u)
                    dve.wait_ge(stats_done, n + 1)
                    if isinstance(k, int) and n < 1:
                        moments(u)
                    else:
                        invert(n - 1, (u - 1) % U)
                        moments(u)
                        shift_of(n - 1, (u - 1) % U)

            divide(0, 0)
            dve.wait_ge(sums_loaded, 16 * QUARTERS)
            nc.vector.reciprocal(sums[:, :, :], sums[:, :, :]).then_inc(sums_step, 1)
            dve.wait_ge(sums_step, 1)
            nc.vector.tensor_copy(inverse_parts[:, 0, :, :], sums[:, :, :]).then_inc(sums_step, 1)
            dve.wait_ge(sums_step, 2)
            nc.vector.tensor_tensor(sums[:, :, :], sums[:, :, :], inverse_parts[:, 0, :, :], ALU.subtract)\
              .then_inc(sums_step, 1)
            dve.wait_ge(sums_step, 3)
            nc.vector.tensor_copy(inverse_parts[:, 1, :, :], sums[:, :, :]).then_inc(sums_step, 1)
            dve.wait_ge(sums_step, 4)
            nc.vector.tensor_tensor(inverse_parts[:, 2, :, :], sums[:, :, :], inverse_parts[:, 1, :, :], ALU.subtract)\
              .then_inc(sums_step, 1)
            step(0)
            with dve.Fori(1, STEPS - 1) as k:
                step(k)
            step(STEPS - 1, last=True)
            invert(N - 1, U - 1)
            shift_of(N - 1, U - 1)


_INS = ["x", "L0_tok_W", "L0_tok_b", "L0_tok_gamma", "L0_tok_beta", "L0_attn_pos_emb", "L0_attn_Wq", "L0_attn_bq",
        "L0_attn_Wk", "L0_attn_bk", "L0_attn_Wv", "L0_attn_bv", "L0_attn_Wp", "L0_attn_bp", "L0_attn_Wo",
        "L0_attn_bo", "L0_attn_pos_bias_u", "L0_attn_pos_bias_v"]


def kernel(**inputs):
    import numpy as _np
    import concourse.bacc as _bacc
    from concourse import mybir as _mybir
    from concourse.bass_utils import run_bass_kernel_spmd as _run

    nc = _bacc.Bacc("TRN2", target_bir_lowering=False, num_devices=1)
    arrays, args = {}, []
    for name in _INS:
        a = _np.ascontiguousarray(inputs[name])
        arrays[f"in_{name}"] = a
        args.append(nc.dram_tensor(f"in_{name}", a.shape, _mybir.dt.from_np(a.dtype), kind="ExternalInput").ap())
    batches, steps, channels = inputs["x"].shape
    frames = steps - inputs["L0_tok_W"].shape[1] // channels + 1
    out = nc.dram_tensor("out_0", (batches, frames, channels), _mybir.dt.float32, kind="ExternalOutput").ap()
    build(nc, *args, out)
    r = _run(nc, [arrays], core_ids=[0])
    return r.results[0]["out_0"]
```
